# Optimizing a Trainium2 kernel written in Bass

```python
import numpy as np
import jax
import jax.numpy as jnp

def _softmax(x, axis=-1):
    return jax.nn.softmax(x, axis=axis)

def _gelu(x):
    return jax.nn.gelu(x, approximate=True)

def _silu(x):
    return jax.nn.silu(x)

def _sigmoid(x):
    return jax.nn.sigmoid(x)

def _layernorm(x, axis=-1, eps=1e-05):
    m = jnp.mean(x, axis=axis, keepdims=True)
    v = jnp.var(x, axis=axis, keepdims=True)
    return (x - m) / jnp.sqrt(v + eps)

def _scatter_add(tgt, idx, src, axis=0):
    return tgt.at[idx].add(src)

def _segment_sum(src, seg, n):
    return jax.ops.segment_sum(src, seg, n)
kernel_name = 'mk_seq_postln_d4_jaxref_r8_9b6edc'

def setup_inputs(seed: int=0):
    np.random.seed(seed)
    _w = jnp.asarray

    def _L0_attn_setup():
        import jax, jax.numpy as jnp
        import numpy as np
        HIDDEN = 512
        N_HEADS = 32
        N_KV = 8
        HEAD_DIM = HIDDEN // N_HEADS
        Q_PER_KV = N_HEADS // N_KV
        SEQ = 256
        ROPE_BASE = 1000000.0
        POS_SCALE = 1.0
        SM_SCALE = 1.0 / HEAD_DIM
        BLOCK = 64
        LOCAL_BLOCKS = 16
        VERT_STRIDE = 8

        def _blocksparse_mask(seq_len):
            nb = seq_len // BLOCK
            qb = np.arange(nb)[:, None]
            kb = np.arange(nb)[None, :]
            bmask = (kb <= qb) & ((qb - kb < LOCAL_BLOCKS) | ((kb + 1) % VERT_STRIDE == 0))
            emask = np.kron(bmask, np.ones((BLOCK, BLOCK), dtype=bool))
            i = np.arange(seq_len)
            emask &= i[:, None] >= i[None, :]
            return jnp.asarray(emask)

        def _rope(x, cos, sin):
            x1, x2 = jnp.split(x, 2, axis=-1)
            rot = jnp.concatenate([-x2, x1], axis=-1)
            return x * cos[None, :, None, :] + rot * sin[None, :, None, :]
        key = jax.random.key(seed)
        k1, k2, k3, k4, k5 = jax.random.split(key, 5)
        qkv_out = (N_HEADS + 2 * N_KV) * HEAD_DIM
        return {'hidden_states': jax.random.normal(k1, (1, SEQ, HIDDEN), dtype=jnp.float32), 'w_qkv': jax.random.normal(k2, (qkv_out, HIDDEN), dtype=jnp.float32) * 0.02, 'b_qkv': jnp.zeros((qkv_out,), dtype=jnp.float32), 'w_dense': jax.random.normal(k3, (HIDDEN, HIDDEN), dtype=jnp.float32) * 0.02, 'b_dense': jnp.zeros((HIDDEN,), dtype=jnp.float32)}
    _L0_attn_in = _L0_attn_setup()

    def _L0_ffn_setup():
        import jax, jax.numpy as jnp
        import numpy as np
        HID, BOT, RDIM, NSLOT, K, VB = (512, 64, 48, 128, 8, 32)
        TAU_LOW, TAU_HIGH, EARLY_EXIT = (0.5, 2.0, 0.05)

        def _uncertainty(h, Wu1, bu1, Wu2, bu2):
            var = jnp.var(h, axis=-1)
            log_var = jnp.log1p(var)
            norm_var = log_var / (jnp.mean(log_var) + 1e-06)
            learned = (jax.nn.gelu(h @ Wu1.T + bu1) @ Wu2.T + bu2)[..., 0]
            return jnp.clip(norm_var * 0.5 + jax.nn.sigmoid(learned) * 2.5, 0.0, 5.0)
        key = jax.random.key(seed)
        ks = jax.random.split(key, 12)
        B, S = (2, 256)
        return {'hidden_states': jax.random.normal(ks[0], (B, S, HID), dtype=jnp.float32), 'Wq': jax.random.normal(ks[1], (BOT, HID), dtype=jnp.float32) / np.sqrt(HID), 'Wr': jax.random.normal(ks[2], (RDIM, BOT), dtype=jnp.float32) / np.sqrt(BOT), 'aux_keys': jax.random.normal(ks[3], (NSLOT, BOT), dtype=jnp.float32) * 0.01, 'aux_values': jax.random.normal(ks[4], (NSLOT, HID), dtype=jnp.float32) * 0.02, 'Wvd': jax.random.normal(ks[5], (VB, HID), dtype=jnp.float32) * 0.1 / np.sqrt(HID), 'Wvu': jax.random.normal(ks[6], (HID, VB), dtype=jnp.float32) * 0.1 / np.sqrt(VB), 'Wu1': jax.random.normal(ks[7], (HID // 4, HID), dtype=jnp.float32) / np.sqrt(HID), 'bu1': jnp.zeros((HID // 4,), dtype=jnp.float32), 'Wu2': jax.random.normal(ks[8], (1, HID // 4), dtype=jnp.float32) * 0.01, 'bu2': jnp.zeros((1,), dtype=jnp.float32), 'gate_w1': jnp.float32(0.5), 'gate_bias': jnp.float32(-1.0), 'log_rel': jnp.zeros((NSLOT,), dtype=jnp.float32)}
    _L0_ffn_in = _L0_ffn_setup()

    def _L1_attn_setup():
        import math
        import jax, jax.numpy as jnp
        import numpy as np
        NUM_HEADS = 32
        NUM_KV_HEADS = 8
        HEAD_DIM = 128
        HIDDEN = 512
        ROPE_THETA = 500000.0
        ROPE_FACTOR = 8.0
        HIGH_FF = 4.0
        LOW_FF = 1.0
        ORIG_MAX_POS = 1024

        def _llama3_inv_freq():
            inv = 1.0 / ROPE_THETA ** (np.arange(0, HEAD_DIM, 2, dtype=np.float32) / HEAD_DIM)
            wavelen = 2.0 * np.pi / inv
            low_wl = ORIG_MAX_POS / LOW_FF
            high_wl = ORIG_MAX_POS / HIGH_FF
            inv_scaled = np.where(wavelen > low_wl, inv / ROPE_FACTOR, inv)
            smooth = (ORIG_MAX_POS / wavelen - LOW_FF) / (HIGH_FF - LOW_FF)
            smoothed = (1.0 - smooth) / ROPE_FACTOR * inv + smooth * inv
            is_medium = (wavelen <= low_wl) & (wavelen >= high_wl)
            return jnp.asarray(np.where(is_medium, smoothed, inv_scaled), dtype=jnp.float32)

        def _rotate_half(x):
            h = x.shape[-1] // 2
            return jnp.concatenate([-x[..., h:], x[..., :h]], axis=-1)
        key = jax.random.key(seed)
        ks = jax.random.split(key, 5)
        s = 0.02
        return {'x': jax.random.normal(ks[0], (1, 256, HIDDEN), dtype=jnp.float32), 'Wq': jax.random.normal(ks[1], (NUM_HEADS * HEAD_DIM, HIDDEN), dtype=jnp.float32) * s, 'Wk': jax.random.normal(ks[2], (NUM_KV_HEADS * HEAD_DIM, HIDDEN), dtype=jnp.float32) * s, 'Wv': jax.random.normal(ks[3], (NUM_KV_HEADS * HEAD_DIM, HIDDEN), dtype=jnp.float32) * s, 'Wo': jax.random.normal(ks[4], (HIDDEN, NUM_HEADS * HEAD_DIM), dtype=jnp.float32) * s}
    _L1_attn_in = _L1_attn_setup()

    def _L1_ffn_setup():
        import jax, jax.numpy as jnp
        import numpy as np
        HIDDEN = 512
        INTER = 1376
        SPARSITY = 0.5

        def _ternary_weight(key, out_dim, in_dim, sparsity):
            k_mask, k_sign = jax.random.split(key)
            nonzero = jax.random.bernoulli(k_mask, 1.0 - sparsity, (out_dim, in_dim))
            sign = jnp.where(jax.random.bernoulli(k_sign, 0.5, (out_dim, in_dim)), 1.0, -1.0)
            return (nonzero * sign).astype(jnp.float32)
        key = jax.random.key(seed)
        kx, kg, ku, kd, ksg, ksu, ksd = jax.random.split(key, 7)
        x = jax.random.normal(kx, (4, 256, HIDDEN), dtype=jnp.float32)
        Wg = _ternary_weight(kg, INTER, HIDDEN, SPARSITY)
        Wu = _ternary_weight(ku, INTER, HIDDEN, SPARSITY)
        Wd = _ternary_weight(kd, HIDDEN, INTER, SPARSITY)
        ag = jax.random.uniform(ksg, (INTER,), dtype=jnp.float32, minval=0.5, maxval=1.5) / np.sqrt(HIDDEN)
        au = jax.random.uniform(ksu, (INTER,), dtype=jnp.float32, minval=0.5, maxval=1.5) / np.sqrt(HIDDEN)
        ad = jax.random.uniform(ksd, (HIDDEN,), dtype=jnp.float32, minval=0.5, maxval=1.5) / np.sqrt(INTER)
        return {'x': x, 'Wg': Wg, 'Wu': Wu, 'Wd': Wd, 'ag': ag, 'au': au, 'ad': ad}
    _L1_ffn_in = _L1_ffn_setup()

    def _L2_attn_setup():
        import jax, jax.numpy as jnp
        import numpy as np
        import math
        B, L, D, H = (32, 64, 512, 32)
        HD = D // H
        key = jax.random.key(seed)
        ks = jax.random.split(key, 9)
        s = 1.0 / math.sqrt(D)
        return {'x': jax.random.normal(ks[0], (B, L, D), jnp.float32), 'Wq': jax.random.normal(ks[1], (D, D), jnp.float32) * s, 'bq': jax.random.normal(ks[2], (D,), jnp.float32) * s, 'Wk': jax.random.normal(ks[3], (D, D), jnp.float32) * s, 'bk': jax.random.normal(ks[4], (D,), jnp.float32) * s, 'Wv': jax.random.normal(ks[5], (D, D), jnp.float32) * s, 'bv': jax.random.normal(ks[6], (D,), jnp.float32) * s, 'Wo': jax.random.normal(ks[7], (D, D), jnp.float32) * s, 'bo': jax.random.normal(ks[8], (D,), jnp.float32) * s}
    _L2_attn_in = _L2_attn_setup()

    def _L2_ffn_setup():
        import jax, jax.numpy as jnp
        import numpy as np
        B, S, D_IN, D_OUT = (2, 256, 512, 512)
        E, K, R = (8, 2, 16)
        SCALING = 32.0 / 16.0
        key = jax.random.key(seed)
        ks = jax.random.split(key, 6)
        x = jax.random.normal(ks[0], (B, S, D_IN), dtype=jnp.float32)
        gate_w = jax.random.normal(ks[1], (E, D_IN), dtype=jnp.float32) * 0.02
        base_w = jax.random.normal(ks[2], (D_OUT, D_IN), dtype=jnp.float32) * 0.02
        base_b = jax.random.normal(ks[3], (D_OUT,), dtype=jnp.float32) * 0.02
        lora_A = jax.random.normal(ks[4], (E, R, D_IN), dtype=jnp.float32) * 0.02
        lora_B = jax.random.normal(ks[5], (E, D_OUT, R), dtype=jnp.float32) * 0.02
        return {'x': x, 'gate_w': gate_w, 'base_w': base_w, 'base_b': base_b, 'lora_A': lora_A, 'lora_B': lora_B}
    _L2_ffn_in = _L2_ffn_setup()

    def _L3_attn_setup():
        import jax, jax.numpy as jnp
        import numpy as np
        B, S, D = (2, 256, 512)
        NH, NKV = (32, 8)
        HD = D // NH
        NREP = NH // NKV
        SCALE = HD ** (-0.5)
        key = jax.random.key(seed)
        kx, kq, kk, kv, ko = jax.random.split(key, 5)
        s = 0.02
        return {'x': jax.random.normal(kx, (B, S, D), dtype=jnp.float32), 'wq': jax.random.normal(kq, (D, NH * HD), dtype=jnp.float32) * s, 'wk': jax.random.normal(kk, (D, NKV * HD), dtype=jnp.float32) * s, 'wv': jax.random.normal(kv, (D, NKV * HD), dtype=jnp.float32) * s, 'wo': jax.random.normal(ko, (NH * HD, D), dtype=jnp.float32) * s}
    _L3_attn_in = _L3_attn_setup()

    def _L3_ffn_setup():
        import jax, jax.numpy as jnp
        import numpy as np
        LORA_SCALING = 1.0 / 2.0

        def _qlora_linear(x, wq, A, B):
            w = jnp.tile(wq, (1, 4))
            base = x @ w.T
            lora = x @ A.T @ B.T
            return base + lora * LORA_SCALING
        key = jax.random.key(seed)
        ks = jax.random.split(key, 10)
        d, h, r = (512, 1376, 2)
        return {'x': jax.random.normal(ks[0], (16, 1, d), dtype=jnp.float32), 'w1q': jax.random.normal(ks[1], (h, d // 4), dtype=jnp.float32) * 0.02, 'a1': jax.random.normal(ks[2], (r, d), dtype=jnp.float32) * 0.02, 'b1': jax.random.normal(ks[3], (h, r), dtype=jnp.float32) * 0.02, 'w3q': jax.random.normal(ks[4], (h, d // 4), dtype=jnp.float32) * 0.02, 'a3': jax.random.normal(ks[5], (r, d), dtype=jnp.float32) * 0.02, 'b3': jax.random.normal(ks[6], (h, r), dtype=jnp.float32) * 0.02, 'w2q': jax.random.normal(ks[7], (d, h // 4), dtype=jnp.float32) * 0.02, 'a2': jax.random.normal(ks[8], (r, h), dtype=jnp.float32) * 0.02, 'b2': jax.random.normal(ks[9], (d, r), dtype=jnp.float32) * 0.02}
    _L3_ffn_in = _L3_ffn_setup()
    _d = {'L0_attn_hidden_states': _L0_attn_in['hidden_states'], 'L0_attn_w_qkv': _L0_attn_in['w_qkv'], 'L0_attn_b_qkv': _L0_attn_in['b_qkv'], 'L0_attn_w_dense': _L0_attn_in['w_dense'], 'L0_attn_b_dense': _L0_attn_in['b_dense'], 'L0_ffn_Wq': _L0_ffn_in['Wq'], 'L0_ffn_Wr': _L0_ffn_in['Wr'], 'L0_ffn_aux_keys': _L0_ffn_in['aux_keys'], 'L0_ffn_aux_values': _L0_ffn_in['aux_values'], 'L0_ffn_Wvd': _L0_ffn_in['Wvd'], 'L0_ffn_Wvu': _L0_ffn_in['Wvu'], 'L0_ffn_Wu1': _L0_ffn_in['Wu1'], 'L0_ffn_bu1': _L0_ffn_in['bu1'], 'L0_ffn_Wu2': _L0_ffn_in['Wu2'], 'L0_ffn_bu2': _L0_ffn_in['bu2'], 'L0_ffn_gate_w1': _L0_ffn_in['gate_w1'], 'L0_ffn_gate_bias': _L0_ffn_in['gate_bias'], 'L0_ffn_log_rel': _L0_ffn_in['log_rel'], 'L1_attn_Wq': _L1_attn_in['Wq'], 'L1_attn_Wk': _L1_attn_in['Wk'], 'L1_attn_Wv': _L1_attn_in['Wv'], 'L1_attn_Wo': _L1_attn_in['Wo'], 'L1_ffn_Wg': _L1_ffn_in['Wg'], 'L1_ffn_Wu': _L1_ffn_in['Wu'], 'L1_ffn_Wd': _L1_ffn_in['Wd'], 'L1_ffn_ag': _L1_ffn_in['ag'], 'L1_ffn_au': _L1_ffn_in['au'], 'L1_ffn_ad': _L1_ffn_in['ad'], 'L2_attn_Wq': _L2_attn_in['Wq'], 'L2_attn_bq': _L2_attn_in['bq'], 'L2_attn_Wk': _L2_attn_in['Wk'], 'L2_attn_bk': _L2_attn_in['bk'], 'L2_attn_Wv': _L2_attn_in['Wv'], 'L2_attn_bv': _L2_attn_in['bv'], 'L2_attn_Wo': _L2_attn_in['Wo'], 'L2_attn_bo': _L2_attn_in['bo'], 'L2_ffn_gate_w': _L2_ffn_in['gate_w'], 'L2_ffn_base_w': _L2_ffn_in['base_w'], 'L2_ffn_base_b': _L2_ffn_in['base_b'], 'L2_ffn_lora_A': _L2_ffn_in['lora_A'], 'L2_ffn_lora_B': _L2_ffn_in['lora_B'], 'L3_attn_wq': _L3_attn_in['wq'], 'L3_attn_wk': _L3_attn_in['wk'], 'L3_attn_wv': _L3_attn_in['wv'], 'L3_attn_wo': _L3_attn_in['wo'], 'L3_ffn_w1q': _L3_ffn_in['w1q'], 'L3_ffn_a1': _L3_ffn_in['a1'], 'L3_ffn_b1': _L3_ffn_in['b1'], 'L3_ffn_w3q': _L3_ffn_in['w3q'], 'L3_ffn_a3': _L3_ffn_in['a3'], 'L3_ffn_b3': _L3_ffn_in['b3'], 'L3_ffn_w2q': _L3_ffn_in['w2q'], 'L3_ffn_a2': _L3_ffn_in['a2'], 'L3_ffn_b2': _L3_ffn_in['b2']}
    _x0 = _d['L0_attn_hidden_states']
    _d['L0_attn_hidden_states'] = jax.random.normal(jax.random.fold_in(jax.random.key(seed), 1), (2, 512, 512), dtype=_x0.dtype)
    del _x0
    return _d

def reference(L0_attn_hidden_states, L0_attn_w_qkv, L0_attn_b_qkv, L0_attn_w_dense, L0_attn_b_dense, L0_ffn_Wq, L0_ffn_Wr, L0_ffn_aux_keys, L0_ffn_aux_values, L0_ffn_Wvd, L0_ffn_Wvu, L0_ffn_Wu1, L0_ffn_bu1, L0_ffn_Wu2, L0_ffn_bu2, L0_ffn_gate_w1, L0_ffn_gate_bias, L0_ffn_log_rel, L1_attn_Wq, L1_attn_Wk, L1_attn_Wv, L1_attn_Wo, L1_ffn_Wg, L1_ffn_Wu, L1_ffn_Wd, L1_ffn_ag, L1_ffn_au, L1_ffn_ad, L2_attn_Wq, L2_attn_bq, L2_attn_Wk, L2_attn_bk, L2_attn_Wv, L2_attn_bv, L2_attn_Wo, L2_attn_bo, L2_ffn_gate_w, L2_ffn_base_w, L2_ffn_base_b, L2_ffn_lora_A, L2_ffn_lora_B, L3_attn_wq, L3_attn_wk, L3_attn_wv, L3_attn_wo, L3_ffn_w1q, L3_ffn_a1, L3_ffn_b1, L3_ffn_w3q, L3_ffn_a3, L3_ffn_b3, L3_ffn_w2q, L3_ffn_a2, L3_ffn_b2):

    def _L0_attn_ref(hidden_states, w_qkv, b_qkv, w_dense, b_dense):
        import jax, jax.numpy as jnp
        import numpy as np
        HIDDEN = 512
        N_HEADS = 32
        N_KV = 8
        HEAD_DIM = HIDDEN // N_HEADS
        Q_PER_KV = N_HEADS // N_KV
        SEQ = 256
        ROPE_BASE = 1000000.0
        POS_SCALE = 1.0
        SM_SCALE = 1.0 / HEAD_DIM
        BLOCK = 64
        LOCAL_BLOCKS = 16
        VERT_STRIDE = 8

        def _blocksparse_mask(seq_len):
            nb = seq_len // BLOCK
            qb = np.arange(nb)[:, None]
            kb = np.arange(nb)[None, :]
            bmask = (kb <= qb) & ((qb - kb < LOCAL_BLOCKS) | ((kb + 1) % VERT_STRIDE == 0))
            emask = np.kron(bmask, np.ones((BLOCK, BLOCK), dtype=bool))
            i = np.arange(seq_len)
            emask &= i[:, None] >= i[None, :]
            return jnp.asarray(emask)

        def _rope(x, cos, sin):
            x1, x2 = jnp.split(x, 2, axis=-1)
            rot = jnp.concatenate([-x2, x1], axis=-1)
            return x * cos[None, :, None, :] + rot * sin[None, :, None, :]
        B, S, _ = hidden_states.shape
        qkv = jnp.einsum('bsh,oh->bso', hidden_states, w_qkv) + b_qkv
        qkv = qkv.reshape(B, S, N_KV, Q_PER_KV + 2, HEAD_DIM)
        q = qkv[:, :, :, :Q_PER_KV].reshape(B, S, N_HEADS, HEAD_DIM)
        k = qkv[:, :, :, Q_PER_KV]
        v = qkv[:, :, :, Q_PER_KV + 1]
        inv_freq = 1.0 / ROPE_BASE ** (jnp.arange(0, HEAD_DIM, 2, dtype=jnp.float32) / HEAD_DIM)
        t = jnp.arange(S, dtype=jnp.float32) * POS_SCALE
        freqs = jnp.outer(t, inv_freq)
        emb = jnp.concatenate([freqs, freqs], axis=-1)
        cos, sin = (jnp.cos(emb), jnp.sin(emb))
        q = _rope(q, cos, sin)
        k = _rope(k, cos, sin)
        k = jnp.repeat(k, Q_PER_KV, axis=2)
        v = jnp.repeat(v, Q_PER_KV, axis=2)
        mask = _blocksparse_mask(S)
        scores = jnp.einsum('bqhd,bkhd->bhqk', q, k) * SM_SCALE
        scores = jnp.where(mask[None, None], scores, jnp.finfo(scores.dtype).min)
        probs = jax.nn.softmax(scores, axis=-1)
        ctx = jnp.einsum('bhqk,bkhd->bqhd', probs, v).reshape(B, S, HIDDEN)
        out = jnp.einsum('bsh,oh->bso', ctx, w_dense) + b_dense
        return out

    def _L0_ffn_ref(hidden_states, Wq, Wr, aux_keys, aux_values, Wvd, Wvu, Wu1, bu1, Wu2, bu2, gate_w1, gate_bias, log_rel):
        import jax, jax.numpy as jnp
        import numpy as np
        HID, BOT, RDIM, NSLOT, K, VB = (512, 64, 48, 128, 8, 32)
        TAU_LOW, TAU_HIGH, EARLY_EXIT = (0.5, 2.0, 0.05)

        def _uncertainty(h, Wu1, bu1, Wu2, bu2):
            var = jnp.var(h, axis=-1)
            log_var = jnp.log1p(var)
            norm_var = log_var / (jnp.mean(log_var) + 1e-06)
            learned = (jax.nn.gelu(h @ Wu1.T + bu1) @ Wu2.T + bu2)[..., 0]
            return jnp.clip(norm_var * 0.5 + jax.nn.sigmoid(learned) * 2.5, 0.0, 5.0)
        query = hidden_states @ Wq.T
        rq = query @ Wr.T
        rk = aux_keys @ Wr.T
        router_scores = jnp.einsum('bsr,nr->bsn', rq, rk) / np.sqrt(RDIM) + log_rel
        top_scores, top_idx = jax.lax.top_k(router_scores, K)
        sel_keys = aux_keys[top_idx]
        attn = jnp.einsum('bsd,bskd->bsk', query, sel_keys) / np.sqrt(BOT) + log_rel[top_idx]
        w = jax.nn.softmax(attn, axis=-1)
        sel_vals = aux_values[top_idx]
        aux_out = jnp.einsum('bsk,bskh->bsh', w, sel_vals)
        aux_out = aux_out @ Wvd.T @ Wvu.T
        u = _uncertainty(hidden_states, Wu1, bu1, Wu2, bu2)
        u_norm = jnp.clip((u - TAU_LOW) / (TAU_HIGH - TAU_LOW), 0.0, 1.0)
        gate = jax.nn.sigmoid(gate_w1 * u_norm + gate_bias)
        gate = jnp.where(gate < EARLY_EXIT, 0.0, gate)
        return hidden_states + gate[..., None] * aux_out

    def _L1_attn_ref(x, Wq, Wk, Wv, Wo):
        import math
        import jax, jax.numpy as jnp
        import numpy as np
        NUM_HEADS = 32
        NUM_KV_HEADS = 8
        HEAD_DIM = 128
        HIDDEN = 512
        ROPE_THETA = 500000.0
        ROPE_FACTOR = 8.0
        HIGH_FF = 4.0
        LOW_FF = 1.0
        ORIG_MAX_POS = 1024

        def _llama3_inv_freq():
            inv = 1.0 / ROPE_THETA ** (np.arange(0, HEAD_DIM, 2, dtype=np.float32) / HEAD_DIM)
            wavelen = 2.0 * np.pi / inv
            low_wl = ORIG_MAX_POS / LOW_FF
            high_wl = ORIG_MAX_POS / HIGH_FF
            inv_scaled = np.where(wavelen > low_wl, inv / ROPE_FACTOR, inv)
            smooth = (ORIG_MAX_POS / wavelen - LOW_FF) / (HIGH_FF - LOW_FF)
            smoothed = (1.0 - smooth) / ROPE_FACTOR * inv + smooth * inv
            is_medium = (wavelen <= low_wl) & (wavelen >= high_wl)
            return jnp.asarray(np.where(is_medium, smoothed, inv_scaled), dtype=jnp.float32)

        def _rotate_half(x):
            h = x.shape[-1] // 2
            return jnp.concatenate([-x[..., h:], x[..., :h]], axis=-1)
        B, T, _ = x.shape
        G = NUM_HEADS // NUM_KV_HEADS
        q = jnp.einsum('bth,oh->bto', x, Wq).reshape(B, T, NUM_HEADS, HEAD_DIM).transpose(0, 2, 1, 3)
        k = jnp.einsum('bth,oh->bto', x, Wk).reshape(B, T, NUM_KV_HEADS, HEAD_DIM).transpose(0, 2, 1, 3)
        v = jnp.einsum('bth,oh->bto', x, Wv).reshape(B, T, NUM_KV_HEADS, HEAD_DIM).transpose(0, 2, 1, 3)
        inv_freq = _llama3_inv_freq()
        pos = jnp.arange(T, dtype=jnp.float32)
        freqs = pos[:, None] * inv_freq[None, :]
        emb = jnp.concatenate([freqs, freqs], axis=-1)
        cos, sin = (jnp.cos(emb), jnp.sin(emb))
        q = q * cos + _rotate_half(q) * sin
        k = k * cos + _rotate_half(k) * sin
        qg = q.reshape(B, NUM_KV_HEADS, G, T, HEAD_DIM)
        scale = 1.0 / math.sqrt(HEAD_DIM)
        scores = jnp.einsum('bkgtd,bksd->bkgts', qg, k) * scale
        causal = jnp.tril(jnp.ones((T, T), dtype=bool))
        scores = jnp.where(causal, scores, -jnp.inf)
        attn = jax.nn.softmax(scores, axis=-1)
        out = jnp.einsum('bkgts,bksd->bkgtd', attn, v)
        out = out.reshape(B, NUM_HEADS, T, HEAD_DIM).transpose(0, 2, 1, 3).reshape(B, T, NUM_HEADS * HEAD_DIM)
        return jnp.einsum('bto,ho->bth', out, Wo)

    def _L1_ffn_ref(x, Wg, Wu, Wd, ag, au, ad):
        import jax, jax.numpy as jnp
        import numpy as np
        HIDDEN = 512
        INTER = 1376
        SPARSITY = 0.5

        def _ternary_weight(key, out_dim, in_dim, sparsity):
            k_mask, k_sign = jax.random.split(key)
            nonzero = jax.random.bernoulli(k_mask, 1.0 - sparsity, (out_dim, in_dim))
            sign = jnp.where(jax.random.bernoulli(k_sign, 0.5, (out_dim, in_dim)), 1.0, -1.0)
            return (nonzero * sign).astype(jnp.float32)
        gate = jnp.einsum('bsh,ih->bsi', x, Wg) * ag
        up = jnp.einsum('bsh,ih->bsi', x, Wu) * au
        h = jax.nn.silu(gate) * up
        out = jnp.einsum('bsi,hi->bsh', h, Wd) * ad
        return out

    def _L2_attn_ref(x, Wq, bq, Wk, bk, Wv, bv, Wo, bo):
        import jax, jax.numpy as jnp
        import numpy as np
        import math
        B, L, D, H = (32, 64, 512, 32)
        HD = D // H
        b, l, d = x.shape
        h, hd = (H, HD)
        q = (x @ Wq.T + bq).reshape(b, l, h, hd).transpose(0, 2, 1, 3)
        k = (x @ Wk.T + bk).reshape(b, l, h, hd).transpose(0, 2, 1, 3)
        v = (x @ Wv.T + bv).reshape(b, l, h, hd).transpose(0, 2, 1, 3)
        scores = jnp.einsum('bhqd,bhkd->bhqk', q, k) / math.sqrt(hd)
        causal = jnp.tril(jnp.ones((l, l), bool))
        scores = jnp.where(causal, scores, -jnp.inf)
        att = jax.nn.softmax(scores, axis=-1)
        out = jnp.einsum('bhqk,bhkd->bhqd', att, v)
        out = out.transpose(0, 2, 1, 3).reshape(b, l, d)
        return out @ Wo.T + bo

    def _L2_ffn_ref(x, gate_w, base_w, base_b, lora_A, lora_B):
        import jax, jax.numpy as jnp
        import numpy as np
        B, S, D_IN, D_OUT = (2, 256, 512, 512)
        E, K, R = (8, 2, 16)
        SCALING = 32.0 / 16.0
        gate_logits = jnp.einsum('bsd,ed->bse', x, gate_w)
        weights, selected = jax.lax.top_k(gate_logits, K)
        weights = jax.nn.softmax(weights.astype(jnp.float32), axis=2).astype(x.dtype)
        result = jnp.einsum('bsd,od->bso', x, base_w) + base_b
        w_full = jnp.sum(jax.nn.one_hot(selected, E, dtype=x.dtype) * weights[..., None], axis=2)
        low = jnp.einsum('bsd,erd->ebsr', x, lora_A)
        lora_out = jnp.einsum('ebsr,eor,bse->bso', low, lora_B, w_full)
        result = result + SCALING * lora_out
        return result

    def _L3_attn_ref(x, wq, wk, wv, wo):
        import jax, jax.numpy as jnp
        import numpy as np
        B, S, D = (2, 256, 512)
        NH, NKV = (32, 8)
        HD = D // NH
        NREP = NH // NKV
        SCALE = HD ** (-0.5)
        b, s, _ = x.shape
        q = (x @ wq).reshape(b, s, NH, HD)
        k = (x @ wk).reshape(b, s, NKV, HD)
        v = (x @ wv).reshape(b, s, NKV, HD)
        k = jnp.repeat(k, NREP, axis=2)
        v = jnp.repeat(v, NREP, axis=2)
        scores = jnp.einsum('bihd,bjhd->bhij', q, k) * SCALE
        causal = jnp.tril(jnp.ones((s, s), dtype=bool))
        scores = jnp.where(causal, scores, jnp.finfo(scores.dtype).min)
        attn = jax.nn.softmax(scores, axis=-1)
        out = jnp.einsum('bhij,bjhd->bihd', attn, v)
        out = out.reshape(b, s, NH * HD)
        return out @ wo

    def _L3_ffn_ref(x, w1q, a1, b1, w3q, a3, b3, w2q, a2, b2):
        import jax, jax.numpy as jnp
        import numpy as np
        LORA_SCALING = 1.0 / 2.0

        def _qlora_linear(x, wq, A, B):
            w = jnp.tile(wq, (1, 4))
            base = x @ w.T
            lora = x @ A.T @ B.T
            return base + lora * LORA_SCALING
        gate = jax.nn.silu(_qlora_linear(x, w1q, a1, b1))
        up = _qlora_linear(x, w3q, a3, b3)
        return _qlora_linear(gate * up, w2q, a2, b2)
    x = L0_attn_hidden_states
    x = _layernorm(x + _L0_attn_ref(x, L0_attn_w_qkv, L0_attn_b_qkv, L0_attn_w_dense, L0_attn_b_dense), axis=-1)
    x = _layernorm(x + _L0_ffn_ref(x, L0_ffn_Wq, L0_ffn_Wr, L0_ffn_aux_keys, L0_ffn_aux_values, L0_ffn_Wvd, L0_ffn_Wvu, L0_ffn_Wu1, L0_ffn_bu1, L0_ffn_Wu2, L0_ffn_bu2, L0_ffn_gate_w1, L0_ffn_gate_bias, L0_ffn_log_rel), axis=-1)
    x = _layernorm(x + _L1_attn_ref(x, L1_attn_Wq, L1_attn_Wk, L1_attn_Wv, L1_attn_Wo), axis=-1)
    x = _layernorm(x + _L1_ffn_ref(x, L1_ffn_Wg, L1_ffn_Wu, L1_ffn_Wd, L1_ffn_ag, L1_ffn_au, L1_ffn_ad), axis=-1)
    x = _layernorm(x + _L2_attn_ref(x, L2_attn_Wq, L2_attn_bq, L2_attn_Wk, L2_attn_bk, L2_attn_Wv, L2_attn_bv, L2_attn_Wo, L2_attn_bo), axis=-1)
    x = _layernorm(x + _L2_ffn_ref(x, L2_ffn_gate_w, L2_ffn_base_w, L2_ffn_base_b, L2_ffn_lora_A, L2_ffn_lora_B), axis=-1)
    x = _layernorm(x + _L3_attn_ref(x, L3_attn_wq, L3_attn_wk, L3_attn_wv, L3_attn_wo), axis=-1)
    x = _layernorm(x + _L3_ffn_ref(x, L3_ffn_w1q, L3_ffn_a1, L3_ffn_b1, L3_ffn_w3q, L3_ffn_a3, L3_ffn_b3, L3_ffn_w2q, L3_ffn_a2, L3_ffn_b2), axis=-1)
    return x

_drawn_inputs = setup_inputs


def setup_inputs(seed=0):
    import zlib

    import numpy as np

    out = dict(_drawn_inputs(seed))
    spreads = {'L0_attn_b_qkv': (0.0, 0.1),
     'L0_attn_b_dense': (0.0, 0.1),
     'L0_ffn_bu1': (0.0, 2.0),
     'L0_ffn_log_rel': (0.0, 2.0)}
    factors = {'L0_ffn_Wq': 30.959,
     'L0_ffn_Wr': 35.63,
     'L0_ffn_aux_keys': 29.742,
     'L0_ffn_aux_values': 29.233,
     'L0_ffn_Wvd': 29.35,
     'L0_ffn_Wvu': 29.23,
     'L0_ffn_Wu1': 64.0,
     'L0_ffn_Wu2': 64.0,
     'L1_attn_Wq': 3.629,
     'L1_attn_Wk': 3.614,
     'L2_attn_bq': 8.0,
     'L2_attn_bk': 64.0,
     'L2_ffn_base_b': 3.216,
     'L3_attn_wq': 8.0,
     'L3_attn_wk': 8.0,
     'L3_ffn_a1': 8.0,
     'L3_ffn_b1': 8.0,
     'L3_ffn_a3': 8.0,
     'L3_ffn_b3': 8.0,
     'L3_ffn_a2': 8.0,
     'L3_ffn_b2': 8.0}
    for name, (base, spread) in spreads.items():
        noise = np.random.default_rng([zlib.crc32(name.encode()), seed]).standard_normal(out[name].shape)
        drawn = base * np.exp(spread * noise) if base else spread * noise
        out[name] = jnp.asarray(drawn.astype(out[name].dtype))
    for name, factor in factors.items():
        out[name] = (out[name] * factor).astype(out[name].dtype)
    return out
```

```python
from contextlib import ExitStack

import numpy as np
import concourse.bass as bass
from concourse import mybir

F32 = mybir.dt.float32
BF16 = mybir.dt.bfloat16
U32 = mybir.dt.uint32
ALU = mybir.AluOpType
ACT = mybir.ActivationFunctionType
AX = mybir.AxisListType

P = 128
NB = 2
T = 512
NT = T // P
D = 512
NC = D // P
EPS = 1e-5
MASKED = -1e30
TAKEN = -3e38

NH, HD = 32, 16
UNITS, UH = 2, 16
SLOTS = 6
SR = SLOTS * HD
MR = 3
REGION = {0: 0, 1: 512, 3: 896, 2: 1024}
SCOLS = 1280
PBS = 5

L1H, L1KV, L1D, GQ = 32, 8, 128, 4
M1 = 11
M3 = 12


class Signal:

    loop, batch = 0, 0

    def __init__(self, sem, name, first=0, second=0, credit=0):
        self.sem, self.name, self.per, self.credit = sem, name, [first, second], credit

    def at(self, n):
        before = NB * self.per[0] if Signal.loop else 0
        return Signal.batch * self.per[Signal.loop] + (before + self.credit + n)

    def claim(self, loop, n):
        share = Share(self, self.per[loop])
        self.per[loop] += n
        return share


class GroupSignal(Signal):

    def __init__(self, sem, name, groups, each, credit):
        super().__init__(sem, name, 0, groups * each, credit)
        self.each = each

    def at(self, n, g):
        return super().at(n) + g * self.each


class Share:
    def __init__(self, whole, before):
        self.whole, self.sem, self.before = whole, whole.sem, before

    def at(self, n):
        return self.whole.at(self.before + n)


class Steps:

    def __init__(self, eng, sig):
        self.eng, self.sig, self.n = eng, sig, 0

    def done(self, ins):
        self.n += 1
        self.sig.n = self.n
        ins.then_inc(self.sig.sem, 1)
        return self.n

    def wait(self, n=None):
        self.eng.wait_ge(self.sig.sem, self.sig.at(self.n if n is None else n))

    def link(self, ins):
        self.done(ins)
        self.wait()


STEPS = {'vector': (131, 293), 'gpsimd': (48, 96)}


def build(nc, d, out):
    ctx = ExitStack()
    sigs = {}

    def sig(name, first=0, second=0, credit=0):
        sigs[name] = Signal(ctx.enter_context(nc.semaphore(name)), name, first, second, credit)
        return sigs[name]

    def sb(name, shape, dt=F32, where=None):
        return (where or ctx).enter_context(nc.sbuf_tensor(name, shape, dt))

    with ctx:
        PS = ctx.enter_context(nc.psum_tensor("PS", [P, 8, 512], F32))
        XB = sb("XB", [P, NT, D])
        XT = sb("XT", [P, NC, T])
        ident_masks = sb("ident_masks", [P, 3, P])
        ident_masks_b = sb("ident_masks_b", [P, 3, P], BF16)
        ident = ident_masks[:, 0]
        identb = ident_masks_b[:, 0]
        mask_qk = ident_masks_b[:, 1]
        mask_kq = ident_masks_b[:, 2]
        ones = sb("ones", [P, P])
        halfneg = sb("halfneg", [P, 1])
        S = sb("S", [P, 2, D])
        stat = sb("stat", [P, 2, 6])
        mv = sb("mv", [P, 2, 2])
        ve = sb("ve", [P, 2, 1])
        rstd = sb("rstd", [P, 2, 1])
        LV = sb("LV", [P, NB * NT])
        VV = sb("VV", [P, NT], F32)
        iota8 = sb("iota8", [P, 8])
        cos0 = sb("cos0", [P, NT, HD])
        sin0 = sb("sin0", [P, NT, HD])
        xmid = nc.dram_tensor("xmid", (NB, P, NT, D), F32, kind="Internal").ap()

        WA = sb("WA", [P, 8192])
        WB = sb("WB", [P, 5120])
        WC = sb("WC", [P, 5696])

        S_const = sig("const_loaded")
        S_wa, S_wb, S_wc = sig("wa_loaded", 0, 32), sig("wb_loaded", 0, 32), sig("wc_loaded", 0, 32)
        S_x = sig("x_loaded", 16, 16)
        S_bar = sig("stage_done")
        S_store = sig("x_stored", 16, 16)
        S_step = sig("vector_step", STEPS["vector"][0], STEPS["vector"][1])
        S_pstep = sig("pool_step", STEPS["gpsimd"][0], STEPS["gpsimd"][1])

        consts = []

        def const(name, shape, dt=F32, src=None):
            buf = sb(name, shape, dt)
            consts.append((buf[:], d[name] if src is None else src))
            return buf

        consts += [(ident_masks[:], d["c_ident_masks"])]

        start = sig("constants_ready")
        START = 4

        waited = sig("waited")

        def alone(eng):
            eng.sem_inc(waited.sem, 1)

        class Stage:

            def tensor(self, pe):
                pass

            def scalar(self, act):
                pass

            def vector(self, dve, st):
                pass

            def gpsimd(self, pool, st):
                pass

        TAIL = "y_ready var_ready rstd_ready x_ready xt_psum_ready xt_ready".split()
        s_tail = {k: sig("tail_" + k) for k in TAIL}

        class Tail(Stage):

            def __init__(self, loop, y_tile=None, y_done=None, mul=None, add=None, times=1.0,
                         last=False):
                self.times = times
                self.y, self.y_done, self.mul, self.add_t, self.last = y_tile, y_done, mul, add, last
                n = dict.fromkeys(TAIL, NT)
                if not y_tile:
                    n["y_ready"] = 0
                if last:
                    n["xt_psum_ready"] = n["xt_ready"] = 0
                self.s_y, self.s_v, self.s_r, self.s_x, self.s_tp, self.s_t = [
                    s_tail[k].claim(loop, n[k]) for k in TAIL]

            def tensor(self, pe):
                for t in range(NT + 1):
                    if t < NT and self.y:
                        if t >= 2:
                            pe.wait_ge(self.s_v.sem, self.s_v.at(t - 1))
                        self.y(pe, t, PS[:, t % 2, :]).then_inc(self.s_y.sem, 1)
                    if t >= 1 and not self.last:
                        u = t - 1
                        pe.wait_ge(self.s_x.sem, self.s_x.at(u + 1))
                        if u >= 2:
                            pe.wait_ge(self.s_t.sem, self.s_t.at(u - 1))
                        for c in range(NC):
                            x = pe.transpose(PS[:, 2 + u % 2, c * P:(c + 1) * P],
                                             XB[:, u, c * P:(c + 1) * P], ident[:, :])
                        x.then_inc(self.s_tp.sem, 1)

            def vector(self, dve, st):
                for t in range(NT + 1):
                    if t < NT:
                        src = S[:, t % 2, :]
                        if t >= 2:
                            dve.wait_ge(self.s_x.sem, self.s_x.at(t - 1))
                        if self.y or self.y_done:
                            if self.y:
                                dve.wait_ge(self.s_y.sem, self.s_y.at(t + 1))
                                y = PS[:, t % 2, :]
                            else:
                                dve.wait_ge(self.y_done[0].sem, self.y_done[0].at(self.y_done[1]))
                                y = PS[:, 4 + t, :]
                            if self.mul is not None:
                                st.link(dve.tensor_tensor(src, y, self.mul, ALU.mult))
                                y = src
                            st.link(dve.scalar_tensor_tensor(src, XB[:, t, :], self.times, y,
                                                             ALU.mult, ALU.add))
                            if self.add_t is not None:
                                st.link(dve.tensor_tensor(src, src, self.add_t, ALU.add))
                        else:
                            src = XB[:, t, :]
                        st.link(dve.bn_stats(stat[:, t % 2, :], src))
                        alone(dve)
                        st.link(dve.bn_aggr(mv[:, t % 2, :], stat[:, t % 2, :]))
                        dve.tensor_scalar(ve[:, t % 2, :], mv[:, t % 2, 1:2], EPS, None, ALU.add)\
                           .then_inc(self.s_v.sem, 1)
                    if t >= 1:
                        u = t - 1
                        dve.wait_ge(self.s_r.sem, self.s_r.at(u + 1))
                        src = S[:, u % 2, :] if self.y or self.y_done else XB[:, u, :]
                        dve.tensor_scalar(XB[:, u, :], src, mv[:, u % 2, 0:1], rstd[:, u % 2, :],
                                          ALU.subtract, ALU.mult).then_inc(self.s_x.sem, 1)
                dve.wait_ge(self.s_x.sem, self.s_x.at(NT))

            def gpsimd(self, pool, st):
                for t in range(NT):
                    pool.wait_ge(self.s_v.sem, self.s_v.at(t + 1))
                    if t >= 2:
                        pool.wait_ge(self.s_x.sem, self.s_x.at(t - 1))
                    pool.tensor_tensor(rstd[:, t % 2, :], ve[:, t % 2, :], halfneg[:, :], ALU.pow)\
                        .then_inc(self.s_r.sem, 1)

            def scalar(self, act):
                if self.last:
                    return
                for t in range(NT):
                    act.wait_ge(self.s_tp.sem, self.s_tp.at(t + 1))
                    act.copy(XT[:, :, t * P:(t + 1) * P],
                             PS[:, 2 + t % 2, :].rearrange("p (c q) -> p c q", c=NC))\
                       .then_inc(self.s_t.sem, 1)

        A16 = ExitStack()
        QT = sb("QT", [P, UH, T], BF16, A16)
        KT = sb("KT", [P, UH, T], BF16, A16)
        VA = sb("VA", [P, NT, UH, 32], F32, A16)
        PB = sb("PB", [P, PBS, SCOLS], F32, A16)
        CTX = sb("CTX", [P, NT, D], F32, A16)
        CT = sb("CT", [P, 2, D], F32, A16)
        QK = sb("QK", [P, 2, 512], F32, A16)
        SPL = sb("SPL", [P, 2, 2 * UH, SR], BF16, A16)
        R1 = sb("R1", [P, 512], F32, A16)
        RT = sb("RT", [P, 320], F32, A16)
        NM = sb("NM", [P, 2, UH], F32, A16)
        NMR = sb("NMR", [P, UH], F32, A16)
        NM3 = sb("NM3", [P, 2, MR * UH], BF16, A16)
        NMT = sb("NMT", [MR * UH, T], BF16, A16)
        OT = sb("OT", [P, 512], F32, A16)
        RC = sb("RC", [P, NT, 4], F32, A16)
        A16.close()
        s16 = {k: sig("a16_" + k) for k in (
            "pads_ready proj_ready parts_ready copies_ready v_ready qkT_psum_ready qkT_ready scores_ready max_ready "
            "max_parts_ready maxT_psum_ready maxT_ready max_rows_loaded scoresT_ready "
            "probs_ready pv_ready outT_ready out_psum_ready ctx_ready ctxT_psum_ready ctxT_ready").split()}

        class Attention16(Stage):
            def __init__(self, loop, W, Wo, nkv, scale, loaded, bias=None, rope=None, bo=None, last=False):
                self.W, self.Wo, self.scale, self.bias, self.rope = W, Wo, scale, bias, rope
                self.nk = nkv // UNITS
                self.rep = UH // self.nk
                self.nqk = UH * HD + self.nk * HD
                self.nv = self.nk * HD
                self.loaded = loaded
                self.tail = Tail(loop, self.y_tile, add=bo, last=last)
                hs = UH + self.nk
                self.lots = [(a, min(8, hs - a)) for a in range(0, hs, 8)]
                L, N = len(self.lots), UNITS * NT
                events = dict(pads_ready=3, proj_ready=N, v_ready=N, parts_ready=N, copies_ready=N,
                              qkT_psum_ready=N * L, qkT_ready=N * L, scores_ready=4 * N,
                              max_ready=4 * N, max_parts_ready=N, maxT_psum_ready=N, maxT_ready=N,
                              max_rows_loaded=16 * MR * UNITS, scoresT_ready=UNITS * UH,
                              probs_ready=UNITS * UH, pv_ready=4 * UNITS, outT_ready=4 * UNITS,
                              out_psum_ready=4 * UNITS, ctx_ready=4 * UNITS,
                              ctxT_psum_ready=NT, ctxT_ready=NT)
                self.on = {k: s16[k].claim(loop, n) for k, n in events.items()}

            def y_tile(self, pe, t, ps):
                if t + 1 < NT:
                    self.ctx_T(pe, t + 1)
                pe.wait_ge(self.on["ctxT_ready"].sem, self.on["ctxT_ready"].at(t + 1))
                for c in range(NC):
                    x = pe.matmul(ps, CT[:, t % 2, c * P:(c + 1) * P], self.Wo[:, c, :],
                                  start=(c == 0), stop=(c == NC - 1))
                return x

            def tensor(self, pe):
                L = len(self.lots)
                self.loaded(pe)
                for u in range(UNITS):
                    def project(t):
                        n = u * NT + t
                        if n >= 2 and t >= 2:
                            pe.wait_ge(self.on["parts_ready"].sem, self.on["parts_ready"].at(n - 1))
                            pe.wait_ge(self.on["v_ready"].sem, self.on["v_ready"].at(n - 1))
                        for c in range(NC):
                            pe.matmul(PS[:, t % 2, 0:self.nqk], XT[:, c, t * P:(t + 1) * P],
                                      self.W[:, c, u, 0:self.nqk], start=(c == 0), stop=(c == NC - 1))
                        for c in range(NC):
                            x = pe.matmul(PS[:, 2 + t % 2, 0:self.nv], XT[:, c, t * P:(t + 1) * P],
                                          self.W[:, c, u, self.nqk:self.nqk + self.nv],
                                          start=(c == 0), stop=(c == NC - 1))
                        x.then_inc(s16["proj_ready"].sem, 1)

                    def transposes(t):
                        n = u * NT + t
                        pe.wait_ge(self.on["copies_ready"].sem, self.on["copies_ready"].at(n + 1))
                        for i, (a, k) in enumerate(self.lots):
                            m = n * L + i
                            if m - u * NT * L >= 2:
                                pe.wait_ge(self.on["qkT_ready"].sem, self.on["qkT_ready"].at(m - 1))
                            tp = PS[:, 4 + m % 2, :].bitcast(BF16)
                            for h in range(k):
                                x = pe.transpose(tp[0:SR, h * P:(h + 1) * P],
                                                 SPL[:, t % 2, a + h, :], identb[:, :])
                            x.then_inc(s16["qkT_psum_ready"].sem, 1)
                    if u:
                        pe.wait_ge(self.on["ctx_ready"].sem, self.on["ctx_ready"].at(u * 4))
                    for t in range(NT + 1):
                        if t < NT:
                            project(t)
                        if t >= 1:
                            transposes(t - 1)
                    pe.wait_ge(self.on["qkT_ready"].sem, self.on["qkT_ready"].at((u + 1) * NT * L))
                    for i in range(NT):
                        n = (i + 1) * P
                        for g in range(4):
                            m = (u * NT + i) * 4 + g
                            if m - u * 16 >= 2:
                                pe.wait_ge(self.on["max_ready"].sem, self.on["max_ready"].at(m - 1))
                            for h in range(4):
                                head = 4 * g + h
                                ps = PS[:, 4 * (m % 2) + h, 0:n]
                                pe.matmul(ps, QT[0:SR, head, i * P:(i + 1) * P],
                                          KT[0:SR, head // self.rep, 0:n], start=True, stop=False)
                                x = pe.matmul(ps[:, n - P:n], identb[:, :], mask_qk[:, :],
                                              start=False, stop=True)
                            x.then_inc(s16["scores_ready"].sem, 1)
                        pe.wait_ge(self.on["max_parts_ready"].sem, self.on["max_parts_ready"].at(u * NT + i + 1))
                        if i >= 1:
                            pe.wait_ge(self.on["maxT_ready"].sem, self.on["maxT_ready"].at(u * NT + i))
                        alone(pe)
                        pe.transpose(PS[0:MR * UH, 0, 0:P // 2].bitcast(BF16),
                                     NM3[:, i % 2, :], identb[:, :])\
                          .then_inc(s16["maxT_psum_ready"].sem, 1)
                        pe.wait_ge(self.on["maxT_ready"].sem, self.on["maxT_ready"].at(u * NT + i + 1))
                    pe.wait_ge(self.on["pads_ready"].sem, self.on["pads_ready"].at(3))
                    pe.wait_ge(self.on["max_rows_loaded"].sem, self.on["max_rows_loaded"].at(16 * MR * (u + 1)))
                    for g in range(5):
                        for h in range(4):
                            if g < 4:
                                n = u * UH + 4 * g + h
                                if 4 * g + h >= 2:
                                    pe.wait_ge(self.on["probs_ready"].sem, self.on["probs_ready"].at(n - 1))
                                head = 4 * g + h
                                s = 3 * (n % 2)
                                flat = PS[:, s:s + 3, :].rearrange("p a b -> p (a b)")
                                for j in range(NT):
                                    w = T - j * P
                                    pe.matmul(flat[:, REGION[j]:REGION[j] + w],
                                              KT[0:SR + MR, head // self.rep, j * P:(j + 1) * P],
                                              QT[0:SR + MR, head, j * P:T], start=True, stop=False)
                                    x = pe.matmul(flat[:, REGION[j]:REGION[j] + P], identb[:, :],
                                                  mask_kq[:, :], start=False, stop=True)
                                x.then_inc(s16["scoresT_ready"].sem, 1)
                            if g >= 1 and h == 1:
                                self.pv(pe, u, g - 1)
                            if g >= 1 and h == 3:
                                self.back(pe, u, g - 1)
                pe.wait_ge(self.on["ctx_ready"].sem, self.on["ctx_ready"].at(UNITS * 4))
                self.ctx_T(pe, 0)
                self.tail.tensor(pe)

            def ctx_T(self, pe, t):
                if t >= 2:
                    pe.wait_ge(self.on["ctxT_ready"].sem, self.on["ctxT_ready"].at(t - 1))
                for c in range(NC):
                    x = pe.transpose(PS[:, 4 + t % 2, c * P:(c + 1) * P],
                                     CTX[:, t, c * P:(c + 1) * P], ident[:, :])
                x.then_inc(s16["ctxT_psum_ready"].sem, 1)

            def pv(self, pe, u, g):
                n = u * 4 + g
                pe.wait_ge(self.on["probs_ready"].sem, self.on["probs_ready"].at(u * UH + 4 * g + 4))
                if g >= 1:
                    pe.wait_ge(self.on["outT_ready"].sem, self.on["outT_ready"].at(n))
                for j in range(NT):
                    w = T - j * P
                    for h in range(4):
                        head = 4 * g + h
                        x = pe.matmul(PS[32 * h:32 * h + 32, 6, j * P:T],
                                      VA[:, j, head // self.rep, :],
                                      PB[:, (u * UH + head) % PBS, REGION[j]:REGION[j] + w],
                                      start=(j == 0), stop=(j == NT - 1), tile_position=(0, 32 * h))
                x.then_inc(s16["pv_ready"].sem, 1)

            def back(self, pe, u, g):
                n = u * 4 + g
                pe.wait_ge(self.on["outT_ready"].sem, self.on["outT_ready"].at(n + 1))
                if g >= 1:
                    pe.wait_ge(self.on["ctx_ready"].sem, self.on["ctx_ready"].at(n))
                for t in range(NT):
                    x = pe.transpose(PS[:, 7, t * P:(t + 1) * P], OT[:, t * P:(t + 1) * P], ident[:, :])
                x.then_inc(s16["out_psum_ready"].sem, 1)

            def vector(self, dve, st):
                NQK = self.nqk
                H = NQK // HD
                dve.memset(KT[SR:SR + MR, :, :], 1.0).then_inc(s16["pads_ready"].sem, 1)
                for u in range(UNITS):
                    for t in range(NT):
                        n = u * NT + t
                        dve.wait_ge(self.on["proj_ready"].sem, self.on["proj_ready"].at(n + 1))
                        if t >= 2:
                            dve.wait_ge(self.on["qkT_psum_ready"].sem, self.on["qkT_psum_ready"].at((n - 1) * len(self.lots)))
                        elif u:
                            dve.wait_ge(self.on["qkT_psum_ready"].sem, self.on["qkT_psum_ready"].at(u * NT * len(self.lots)))
                        src = PS[:, t % 2, 0:NQK]
                        vsrc = PS[:, 2 + t % 2, 0:self.nv]
                        va = VA[:, t, 0:self.nk, 0:HD]
                        if u and t == 0:
                            dve.wait_ge(self.on["pv_ready"].sem, self.on["pv_ready"].at(4 * u))
                        if self.bias is not None:
                            dve.tensor_tensor(va, vsrc.rearrange("p (h e) -> p h e", e=HD),
                                              self.bias[:, u, NQK:NQK + self.nv]
                                              .rearrange("p (h e) -> p h e", e=HD), ALU.add)\
                               .then_inc(s16["v_ready"].sem, 1)
                            st.link(dve.tensor_tensor(QK[:, t % 2, 0:NQK], src,
                                                      self.bias[:, u, 0:NQK], ALU.add))
                        else:
                            dve.tensor_copy(va, vsrc.rearrange("p (h e) -> p h e", e=HD))\
                               .then_inc(s16["v_ready"].sem, 1)
                            st.link(dve.tensor_copy(QK[:, t % 2, 0:NQK], src))
                        qk = QK[:, t % 2, 0:NQK].rearrange("p (h e) -> p h e", e=HD)
                        if self.rope is not None:
                            cos, sin = self.rope
                            r1 = R1[:, 0:NQK].rearrange("p (h e) -> p h e", e=HD)
                            rt = RT[:, 0:NQK].rearrange("p (h e) -> p h e", e=HD)
                            hh = HD // 2
                            bc = lambda a, w: a.unsqueeze(1).to_broadcast([P, H, w])
                            st.done(dve.tensor_tensor(r1, qk, bc(cos[:, t, :], HD), ALU.mult))
                            st.done(dve.tensor_tensor(rt[:, :, 0:hh], qk[:, :, hh:HD],
                                                      bc(sin[:, t, 0:hh], hh), ALU.mult))
                            st.link(dve.tensor_tensor(rt[:, :, hh:HD], qk[:, :, 0:hh],
                                                      bc(sin[:, t, hh:HD], hh), ALU.mult))
                            st.link(dve.tensor_tensor(qk, r1, rt, ALU.add))
                        sp = SPL[:, t % 2, 0:H, :].rearrange("p h (s e) -> p h s e", e=HD)
                        r1 = R1[:, 0:NQK].rearrange("p (h e) -> p h e", e=HD)
                        st.link(dve.tensor_copy(sp[:, :, 0, :], qk))
                        st.link(dve.tensor_tensor(r1, qk, sp[:, :, 0, :], ALU.subtract))
                        st.link(dve.tensor_copy(sp[:, :, 1, :], r1))
                        st.done(dve.tensor_tensor(sp[:, 0:UH, 2, :], r1[:, 0:UH, :],
                                                  sp[:, 0:UH, 1, :], ALU.subtract))
                        dve.tensor_tensor(sp[:, UH:H, 3, :], r1[:, UH:H, :],
                                          sp[:, UH:H, 1, :], ALU.subtract)\
                           .then_inc(s16["parts_ready"].sem, 1)
                        dve.wait_ge(self.on["parts_ready"].sem, self.on["parts_ready"].at(n + 1))
                        st.wait()
                    for i in range(NT):
                        n = (i + 1) * P
                        for g in range(4):
                            m = (u * NT + i) * 4 + g
                            dve.wait_ge(self.on["scores_ready"].sem, self.on["scores_ready"].at(m + 1))
                            dve.tensor_reduce(NM[:, i % 2, 4 * g:4 * g + 4],
                                              PS[:, 4 * (m % 2):4 * (m % 2) + 4, 0:n], AX.X, ALU.max,
                                              negate=True).then_inc(s16["max_ready"].sem, 1)
                        dve.wait_ge(self.on["max_ready"].sem, self.on["max_ready"].at((u * NT + i + 1) * 4))
                        if i >= 2:
                            dve.wait_ge(self.on["maxT_psum_ready"].sem, self.on["maxT_psum_ready"].at(u * NT + i - 1))
                        elif u:
                            dve.wait_ge(self.on["maxT_psum_ready"].sem, self.on["maxT_psum_ready"].at(u * NT))
                        nm, n3 = NM[:, i % 2, :], NM3[:, i % 2, :].rearrange("p (s h) -> p s h", s=MR)
                        st.link(dve.tensor_copy(n3[:, 0, :], nm))
                        st.link(dve.tensor_tensor(NMR[:, :], nm, n3[:, 0, :], ALU.subtract))
                        st.link(dve.tensor_copy(n3[:, 1, :], NMR[:, :]))
                        dve.tensor_tensor(n3[:, 2, :], NMR[:, :], n3[:, 1, :], ALU.subtract)\
                           .then_inc(s16["max_parts_ready"].sem, 1)
                        dve.wait_ge(self.on["max_parts_ready"].sem, self.on["max_parts_ready"].at(u * NT + i + 1))
                    for g in range(4):
                        n = u * 4 + g
                        dve.wait_ge(self.on["pv_ready"].sem, self.on["pv_ready"].at(n + 1))
                        if n >= 1:
                            dve.wait_ge(self.on["out_psum_ready"].sem, self.on["out_psum_ready"].at(n))
                        dve.tensor_copy(OT[:, :], PS[:, 6, :]).then_inc(s16["outT_ready"].sem, 1)
                        dve.wait_ge(self.on["out_psum_ready"].sem, self.on["out_psum_ready"].at(n + 1))
                        o = PS[:, 7, :].rearrange("p (t h e) -> p t h e", t=NT, h=4)
                        st.link(dve.reciprocal(RC[:, :, :], o[:, :, :, HD]))
                        c = CTX[:, :, u * 256 + g * 64:u * 256 + g * 64 + 64]
                        dve.tensor_tensor(c.rearrange("p t (h e) -> p t h e", e=HD), o[:, :, :, 0:HD],
                                          RC[:, :, :].unsqueeze(3).to_broadcast([P, NT, 4, HD]), ALU.mult)\
                           .then_inc(s16["ctx_ready"].sem, 1)
                self.tail.vector(dve, st)

            def gpsimd(self, pool, st):
                H = self.nqk // HD
                alone(pool)
                pool.memset(VA[:, :, :, HD + 1:32], 0.0).then_inc(s16["pads_ready"].sem, 1)
                pool.memset(VA[:, :, :, HD:HD + 1], 1.0).then_inc(s16["pads_ready"].sem, 1)
                for u in range(UNITS):
                    for t in range(NT):
                        n = u * NT + t
                        pool.wait_ge(self.on["parts_ready"].sem, self.on["parts_ready"].at(n + 1))
                        sp = SPL[:, t % 2, 0:H, :].rearrange("p h (s e) -> p h s e", e=HD)
                        q, k = sp[:, 0:UH], sp[:, UH:H]
                        alone(pool)
                        st.done(pool.tensor_copy(q[:, :, 3, :], q[:, :, 0, :]))
                        st.done(pool.tensor_copy(q[:, :, 4, :], q[:, :, 0, :]))
                        st.done(pool.tensor_copy(q[:, :, 5, :], q[:, :, 1, :]))
                        st.done(pool.tensor_copy(k[:, :, 2, :], k[:, :, 0, :]))
                        st.done(pool.tensor_copy(k[:, :, 5, :], k[:, :, 0, :]))
                        st.link(pool.tensor_copy(k[:, :, 4, :], k[:, :, 1, :]))
                        pool.sem_inc(s16["copies_ready"].sem, 1)
                self.tail.gpsimd(pool, st)

            def scalar(self, act):
                L = len(self.lots)
                for u in range(UNITS):
                    if u:
                        act.wait_ge(self.on["scoresT_ready"].sem, self.on["scoresT_ready"].at(u * UH))
                    for t in range(NT):
                        for i, (a, k) in enumerate(self.lots):
                            m = (u * NT + t) * L + i
                            act.wait_ge(self.on["qkT_psum_ready"].sem, self.on["qkT_psum_ready"].at(m + 1))
                            tp = PS[:, 4 + m % 2, :].bitcast(BF16)[0:SR, 0:k * P]
                            dst = QT[0:SR, a:a + k, t * P:(t + 1) * P] if a < UH else \
                                KT[0:SR, a - UH:a - UH + k, t * P:(t + 1) * P]
                            act.copy(dst, tp.rearrange("p (h q) -> p h q", q=P))\
                               .then_inc(s16["qkT_ready"].sem, 1)
                    for i in range(NT):
                        act.wait_ge(self.on["maxT_psum_ready"].sem, self.on["maxT_psum_ready"].at(u * NT + i + 1))
                        act.copy(NMT[:, i * P:(i + 1) * P], PS[0:MR * UH, 0, 0:P // 2].bitcast(BF16))\
                           .then_inc(s16["maxT_ready"].sem, 1)
                    act.wait_ge(self.on["maxT_ready"].sem, self.on["maxT_ready"].at((u + 1) * NT))
                    for r in range(MR):
                        act.dma_start(QT[SR + r:SR + r + 1, :, :], NMT[r * UH:(r + 1) * UH, :])\
                           .then_inc(s16["max_rows_loaded"].sem, 16)
                    for n in range(UH):
                        m = u * UH + n
                        act.wait_ge(self.on["scoresT_ready"].sem, self.on["scoresT_ready"].at(m + 1))
                        if n >= PBS:
                            act.wait_ge(self.on["pv_ready"].sem, self.on["pv_ready"].at(u * 4 + (n - PBS) // 4 + 1))
                        s = 3 * (m % 2)
                        act.activation(PB[:, m % PBS, :],
                                       PS[:, s:s + 3, :].rearrange("p a b -> p (a b)")[:, 0:SCOLS],
                                       ACT.Exp, scale=self.scale).then_inc(s16["probs_ready"].sem, 1)
                for t in range(NT):
                    act.wait_ge(self.on["ctxT_psum_ready"].sem, self.on["ctxT_psum_ready"].at(t + 1))
                    if t >= 2:
                        act.wait_ge(self.tail.s_y.sem, self.tail.s_y.at(t - 1))
                    act.copy(CT[:, t % 2, :], PS[:, 4 + t % 2, :]).then_inc(s16["ctxT_ready"].sem, 1)
                self.tail.scalar(act)

        F0 = ExitStack()
        QF = sb("QF", [64, T], F32, F0)
        GEL = sb("GEL", [P, T], F32, F0)
        RKT = sb("RKT", [48, P], F32, F0)
        G = sb("G", [64, 2 * P], F32, F0)
        AVT = sb("AVT", [32, P], F32, F0)
        PT0 = sb("PT0", [P, D], F32, F0)
        RS = sb("RS", [P, NT, 2 * P], F32, F0)
        MRP = sb("MRP", [P, NT, P], F32, F0)
        M8 = sb("M8", [P, NT, 8], F32, F0)
        EX = sb("EX", [P, NT, P], F32, F0)
        W0T = sb("W0T", [P, T], F32, F0)
        GA = sb("GA", [P, 12, NT], F32, F0)
        F0.close()
        f0 = {k: sig("f0_" + k, 0, n) for k, n in dict(
            q_psum=1, q_ready=1, u_psum=1, gelu_ready=1, rk_psum=1, rk_ready=1, g_psum=1, g_ready=1,
            av_psum=1, av_ready=1, p_psum=1, p_ready=1, r_psum=1, learned_psum=1, logvar_psum=1,
            masked_ready=1, exp_ready=1, learned=1, gate_arg=1, gate=1, weights_ready=1,
            wT_psum=1, wT_ready=1).items()}
        c0 = WC[:, :]
        f0_Wq = c0[:, 0:256].rearrange("p (c n) -> p c n", c=NC)
        f0_Wu1 = c0[:, 256:768].rearrange("p (c n) -> p c n", c=NC)
        f0_Wvd = c0[:, 768:896].rearrange("p (c n) -> p c n", c=NC)
        f0_avT = c0[:, 896:1408].rearrange("p (c n) -> p c n", c=NC)
        f0_Wr = c0[0:48, 1408:1472]
        f0_WrT = c0[0:64, 1472:1520]
        f0_keysT = c0[0:64, 1520:1648]
        f0_WvuT = c0[0:32, 1648:2160]
        f0_lr = c0[:, 2160:2288]
        f0_bu1, f0_Wu2, f0_bu2, f0_gw, f0_gb = [c0[:, 2288 + i:2289 + i] for i in range(5)]

        class Ffn0(Stage):
            def __init__(self, loop):
                self.tail = Tail(loop, self.y_tile, times=2.0)

            def y_tile(self, pe, t, ps):
                return pe.matmul(ps, W0T[:, t * P:(t + 1) * P], PT0[:, :], start=True, stop=True)

            def tensor(self, pe):
                pe.wait_ge(S_wc.sem, S_wc.at(W_C[0]))
                def mms(ps, pairs, s):
                    for i, (a, b) in enumerate(pairs):
                        x = pe.matmul(ps, a, b, start=(i == 0), stop=(i == len(pairs) - 1))
                    x.then_inc(f0[s].sem, 1)
                mms(PS[0:64, 0, :], [(f0_Wq[:, c, :], XT[:, c, :]) for c in range(NC)], "q_psum")
                mms(PS[:, 1, :], [(f0_Wu1[:, c, :], XT[:, c, :]) for c in range(NC)], "u_psum")
                mms(PS[0:48, 2, 0:P], [(f0_WrT, f0_keysT)], "rk_psum")
                mms(PS[0:32, 3, 0:P], [(f0_Wvd[:, c, :], f0_avT[:, c, :]) for c in range(NC)], "av_psum")
                pe.wait_ge(f0["rk_ready"].sem, f0["rk_ready"].at(1))
                alone(pe)
                mms(PS[0:64, 2, 0:P], [(f0_Wr, RKT[:, :])], "g_psum")
                pe.wait_ge(f0["av_ready"].sem, f0["av_ready"].at(1))
                mms(PS[:, 3, :], [(AVT[:, :], f0_WvuT)], "p_psum")
                mms(PS[:, 7, 0:NB * NT], [(ones[:, :], LV[:, :])], "logvar_psum")
                pe.wait_ge(f0["g_ready"].sem, f0["g_ready"].at(1))
                pe.wait_ge(f0["q_ready"].sem, f0["q_ready"].at(1))
                for t in range(NT):
                    x = pe.matmul(PS[:, 4 + t // 2, 256 * (t % 2):256 * (t % 2) + 256],
                                  QF[:, t * P:(t + 1) * P], G[:, :], start=True, stop=True)
                x.then_inc(f0["r_psum"].sem, 1)
                pe.wait_ge(f0["gelu_ready"].sem, f0["gelu_ready"].at(1))
                for t in range(NT):
                    x = pe.matmul(PS[:, 6, t:t + 1], GEL[:, t * P:(t + 1) * P], f0_Wu2,
                                  start=True, stop=True)
                x.then_inc(f0["learned_psum"].sem, 1)
                pe.wait_ge(f0["weights_ready"].sem, f0["weights_ready"].at(1))
                for t in range(NT):
                    x = pe.transpose(PS[:, 4, t * P:(t + 1) * P], EX[:, t, :], ident[:, :])
                x.then_inc(f0["wT_psum"].sem, 1)
                pe.wait_ge(f0["wT_ready"].sem, f0["wT_ready"].at(1))
                pe.wait_ge(f0["p_ready"].sem, f0["p_ready"].at(1))
                self.tail.tensor(pe)

            def scalar(self, act):
                act.wait_ge(f0["u_psum"].sem, f0["u_psum"].at(1))
                act.activation(GEL[:, :], PS[:, 1, :], ACT.Gelu_apprx_tanh, bias=f0_bu1)\
                   .then_inc(f0["gelu_ready"].sem, 1)
                act.wait_ge(f0["masked_ready"].sem, f0["masked_ready"].at(1))
                act.activation(EX[:, :, :], MRP[:, :, :], ACT.Exp).then_inc(f0["exp_ready"].sem, 1)
                act.wait_ge(f0["learned_psum"].sem, f0["learned_psum"].at(1))
                act.activation(GA[:, 3, :], PS[:, 6, 0:NT], ACT.Sigmoid, bias=f0_bu2)\
                   .then_inc(f0["learned"].sem, 1)
                act.wait_ge(f0["gate_arg"].sem, f0["gate_arg"].at(1))
                act.activation(GA[:, 7, :], GA[:, 5, :], ACT.Sigmoid).then_inc(f0["gate"].sem, 1)
                act.wait_ge(f0["wT_psum"].sem, f0["wT_psum"].at(1))
                act.copy(W0T[:, :], PS[:, 4, :]).then_inc(f0["wT_ready"].sem, 1)
                self.tail.scalar(act)

            def gpsimd(self, pool, st):
                self.tail.gpsimd(pool, st)

            def vector(self, dve, st):
                dve.wait_ge(S_wc.sem, S_wc.at(W_C[0]))
                dve.wait_ge(f0["rk_psum"].sem, f0["rk_psum"].at(1))
                dve.tensor_copy(RKT[:, :], PS[0:48, 2, 0:P]).then_inc(f0["rk_ready"].sem, 1)
                dve.wait_ge(f0["av_psum"].sem, f0["av_psum"].at(1))
                dve.tensor_copy(AVT[:, :], PS[0:32, 3, 0:P]).then_inc(f0["av_ready"].sem, 1)
                dve.wait_ge(f0["q_psum"].sem, f0["q_psum"].at(1))
                dve.tensor_copy(QF[:, :], PS[0:64, 0, :]).then_inc(f0["q_ready"].sem, 1)
                dve.wait_ge(f0["g_psum"].sem, f0["g_psum"].at(1))
                st.done(dve.tensor_scalar(G[:, 0:P], PS[0:64, 2, 0:P], 1.0 / np.sqrt(48.0), None, ALU.mult))
                dve.tensor_scalar(G[:, P:2 * P], f0_keysT, 0.125, None, ALU.mult)\
                   .then_inc(f0["g_ready"].sem, 1)
                dve.wait_ge(f0["p_psum"].sem, f0["p_psum"].at(1))
                dve.tensor_copy(PT0[:, :], PS[:, 3, :]).then_inc(f0["p_ready"].sem, 1)
                dve.wait_ge(f0["logvar_psum"].sem, f0["logvar_psum"].at(1))
                st.link(dve.tensor_reduce(GA[:, 8, 0:1], PS[:, 7, 0:NB * NT], AX.X, ALU.add))
                st.link(dve.tensor_scalar(GA[:, 8, 1:2], GA[:, 8, 0:1], 1.0 / (NB * T), 1e-6,
                                          ALU.mult, ALU.add))
                st.link(dve.reciprocal(GA[:, 8, 2:3], GA[:, 8, 1:2]))
                st.link(dve.tensor_scalar(GA[:, 9, :], LV[:, :].rearrange("p (b t) -> p b t", b=NB)
                                          [:, Signal.batch, :], GA[:, 8, 2:3], 0.5, ALU.mult, ALU.mult))
                dve.wait_ge(f0["r_psum"].sem, f0["r_psum"].at(1))
                rps = PS[:, 4:6, :].rearrange("p a (s h n) -> p (a s) h n", s=2, h=2)
                rs = RS[:, :, :].rearrange("p t (h n) -> p t h n", h=2)
                for h in range(2):
                    st.done(dve.tensor_tensor(rs[:, :, h, :], rps[:, :, h, :],
                                              f0_lr.unsqueeze(1).to_broadcast([P, NT, P]), ALU.add))
                st.wait()
                alone(dve)
                for t in range(NT):
                    st.done(dve.max(M8[:, t, :], RS[:, t, 0:P]))
                st.wait()
                alone(dve)
                for t in range(NT):
                    st.done(dve.match_replace(MRP[:, t, :], M8[:, t, :], RS[:, t, 0:P], TAKEN))
                st.wait()
                st.link(dve.tensor_scalar(MRP[:, :, :], MRP[:, :, :], TAKEN, 1.0, ALU.is_equal, ALU.subtract))
                st.link(dve.scalar_tensor_tensor(MRP[:, :, :], MRP[:, :, :], -MASKED, RS[:, :, P:2 * P],
                                                 ALU.mult, ALU.add))
                st.link(dve.tensor_reduce(GA[:, 10, :], MRP[:, :, :], AX.X, ALU.max))
                dve.tensor_tensor(MRP[:, :, :], MRP[:, :, :],
                                  GA[:, 10, :].unsqueeze(2).to_broadcast([P, NT, P]), ALU.subtract)\
                   .then_inc(f0["masked_ready"].sem, 1)
                dve.wait_ge(f0["learned"].sem, f0["learned"].at(1))
                st.link(dve.scalar_tensor_tensor(GA[:, 4, :], GA[:, 3, :], 2.5, GA[:, 9, :], ALU.mult, ALU.add))
                st.link(dve.tensor_scalar(GA[:, 4, :], GA[:, 4, :], 0.0, 5.0, ALU.max, ALU.min))
                st.link(dve.tensor_scalar(GA[:, 4, :], GA[:, 4, :], 0.5, 1.0 / 1.5, ALU.subtract, ALU.mult))
                st.link(dve.tensor_scalar(GA[:, 4, :], GA[:, 4, :], 0.0, 1.0, ALU.max, ALU.min))
                dve.tensor_scalar(GA[:, 5, :], GA[:, 4, :], f0_gw, f0_gb, ALU.mult, ALU.add)\
                   .then_inc(f0["gate_arg"].sem, 1)
                dve.wait_ge(f0["gate"].sem, f0["gate"].at(1))
                st.link(dve.tensor_scalar(GA[:, 11, :], GA[:, 7, :], 0.05, None, ALU.is_ge))
                st.link(dve.tensor_tensor(GA[:, 7, :], GA[:, 7, :], GA[:, 11, :], ALU.mult))
                dve.wait_ge(f0["exp_ready"].sem, f0["exp_ready"].at(1))
                st.link(dve.tensor_reduce(GA[:, 2, :], EX[:, :, :], AX.X, ALU.add))
                st.link(dve.reciprocal(GA[:, 2, :], GA[:, 2, :]))
                st.link(dve.tensor_tensor(GA[:, 2, :], GA[:, 2, :], GA[:, 7, :], ALU.mult))
                dve.tensor_tensor(EX[:, :, :], EX[:, :, :],
                                  GA[:, 2, :].unsqueeze(2).to_broadcast([P, NT, P]), ALU.mult)\
                   .then_inc(f0["weights_ready"].sem, 1)
                self.tail.vector(dve, st)

        L1 = ExitStack()
        kT = sb("kT", [P, T], F32, L1)
        V1 = sb("V1", [P, NT, P], F32, L1)
        qT = sb("qT", [P, 2, T], F32, L1)
        RA = sb("RA", [P, 2, T], F32, L1)
        RB = sb("RB", [P, 2, T], F32, L1)
        PR = sb("PR", [P, 2, SCOLS], F32, L1)
        PRT = sb("PRT", [P, 2, NT, T], F32, L1)
        OT1 = sb("OT1", [P, GQ, T], F32, L1)
        NX = sb("NX", [P, 2, NT], F32, L1)
        SM = sb("SM", [P, 2, NT], F32, L1)
        RCP = sb("RCP", [P, 2, NT], F32, L1)
        TAB = sb("TAB", [P, 4, T], F32, L1)
        L1.close()
        NG = 8
        ev1 = dict(proj=(6, 2), proj_read=(6, 2), rope=(5, 2), scores=(16, 1), negmax=(16, 0), exp=(16, 2),
                   recip=(16, 0), norm=(16, 0), pT_psum=(16, 0), pT=(16, 2), pv=(4, 2), oT=(4, 1),
                   y=(4, 2), added=(4, 2), qkv_loaded=(16, 0), wo_loaded=(16, 0))
        s1 = {k: sigs.setdefault(k, GroupSignal(ctx.enter_context(nc.semaphore("l1_" + k)), k, NG, n, c))
              for k, (n, c) in ev1.items()}
        s1["tab"] = sig("l1_tab_loaded", 0, 16)
        Wqkv1 = WB[:, 0:3072].rearrange("p (c n) -> p c n", c=NC)
        Wo1 = WB[:, 3072:5120].rearrange("p (h n) -> p h n", h=GQ)
        OFF = [0, 128, 384, 768]

        class Attention1(Stage):
            def __init__(self, loop):
                self.tail = Tail(loop)

            def tensor(self, pe):
                with pe.Fori(0, NG) as g:
                    pe.wait_ge(s1["qkv_loaded"].sem, s1["qkv_loaded"].at(16, g))

                    def project(n, col):
                        pe.wait_ge(s1["proj_read"].sem, s1["proj_read"].at(n - 1, g))
                        for c in range(NC):
                            x = pe.matmul(PS[:, n % 2, :], Wqkv1[:, c, col:col + P], XT[:, c, :],
                                          start=(c == 0), stop=(c == NC - 1))
                            yield x
                        x.then_inc(s1["proj"].sem, 1)

                    def whole(gen):
                        for _ in gen:
                            pass
                    whole(project(0, 512))
                    pe.wait_ge(s1["proj_read"].sem, s1["proj_read"].at(0, g))
                    for t in range(NT):
                        for c in range(NC):
                            x = pe.matmul(PS[:, 1, t * P:(t + 1) * P], XT[:, c, t * P:(t + 1) * P],
                                          Wqkv1[:, c, 640:768], start=(c == 0), stop=(c == NC - 1))
                    x.then_inc(s1["proj"].sem, 1)
                    whole(project(2, 0))
                    for h in range(GQ + 1):
                        q = project(h + 3, (h + 1) * P) if h < GQ - 1 else iter(())
                        for i in range(NT):
                            if h < GQ:
                                if i == 0:
                                    pe.wait_ge(s1["rope"].sem, s1["rope"].at(h + 2, g))
                                pe.wait_ge(s1["exp"].sem, s1["exp"].at(4 * h + i - 1, g))
                                n = (i + 1) * P
                                ps = PS[:, 2 + i % 2, 0:n]
                                pe.matmul(ps, qT[:, h % 2, i * P:(i + 1) * P], kT[:, 0:n],
                                          start=True, stop=False)
                                pe.matmul(ps[:, n - P:n], identb[:, :], mask_qk[:, :],
                                              start=False, stop=True).then_inc(s1["scores"].sem, 1)
                            next(q, None)
                        whole(q)
                        if h >= 1:
                            for i in range(NT):
                                m = 4 * (h - 1) + i
                                pe.wait_ge(s1["norm"].sem, s1["norm"].at(m + 1, g))
                                pe.wait_ge(s1["pT"].sem, s1["pT"].at(m - 1, g))
                                for j in range(i + 1):
                                    x = pe.transpose(PS[:, 4 + i % 2, j * P:(j + 1) * P],
                                                     PR[:, (h - 1) % 2, OFF[i] + j * P:OFF[i] + (j + 1) * P],
                                                     ident[:, :])
                                x.then_inc(s1["pT_psum"].sem, 1)
                            pe.wait_ge(s1["oT"].sem, s1["oT"].at(h - 1, g))
                            pe.wait_ge(s1["pT"].sem, s1["pT"].at(4 * h, g))
                            if h == 1:
                                pe.wait_ge(s1["proj_read"].sem, s1["proj_read"].at(2, g))
                                pe.wait_ge(s1["added"].sem, s1["added"].at(0, g))
                            for j in range(NT):
                                x = pe.matmul(PS[:, 6, j * P:T], V1[:, j, :],
                                              PRT[:, (h - 1) % 2, j, j * P:T],
                                              start=(j == 0), stop=(j == NT - 1))
                            x.then_inc(s1["pv"].sem, 1)
                    pe.wait_ge(s1["wo_loaded"].sem, s1["wo_loaded"].at(16, g))
                    pe.wait_ge(s1["oT"].sem, s1["oT"].at(GQ, g))
                    for t in range(NT):
                        pe.wait_ge(s1["added"].sem, s1["added"].at(t - 1, g))
                        for h in range(GQ):
                            x = pe.matmul(PS[:, 7 - t % 2, :], OT1[:, h, t * P:(t + 1) * P], Wo1[:, h, :],
                                          start=(h == 0), stop=(h == GQ - 1))
                        x.then_inc(s1["y"].sem, 1)
                self.tail.tensor(pe)

            def vector(self, dve, st):
                dve.wait_ge(s1["tab"].sem, s1["tab"].at(16))
                alone(dve)
                with dve.Fori(0, NG) as g:

                    def rope(n, slot, r, c):
                        dve.wait_ge(s1["proj"].sem, s1["proj"].at(n + 1, g))
                        dve.wait_ge(s1["rope"].sem, s1["rope"].at(max(r - 1, 0), g))
                        ps = PS[:, n % 2, :]
                        dve.tensor_tensor(RA[:, slot, :], ps, TAB[:, c, :], ALU.mult)
                        dve.tensor_tensor(RB[0:64, slot, :], ps[64:128], TAB[64:128, c + 1, :], ALU.mult)
                        dve.tensor_tensor(RB[64:128, slot, :], ps[0:64], TAB[0:64, c + 1, :], ALU.mult)\
                           .then_inc(s1["proj_read"].sem, 1)
                    rope(0, 0, 0, 2)
                    dve.wait_ge(s1["proj"].sem, s1["proj"].at(2, g))
                    dve.wait_ge(s1["pv"].sem, s1["pv"].at(0, g))
                    dve.tensor_copy(V1[:, :, :], PS[:, 1, :].rearrange("p (t n) -> p t n", t=NT))\
                       .then_inc(s1["proj_read"].sem, 1)
                    rope(2, 1, 1, 0)
                    for h in range(GQ + 1):
                        for i in range(NT):
                            if h < GQ:
                                m = 4 * h + i
                                dve.wait_ge(s1["scores"].sem, s1["scores"].at(m + 1, g))
                                dve.tensor_reduce(NX[:, h % 2, i:i + 1], PS[:, 2 + i % 2, 0:(i + 1) * P],
                                                  AX.X, ALU.max, negate=True).then_inc(s1["negmax"].sem, 1)
                                if i >= 1:
                                    self.recip(dve, g, m - 1)
                        if h < GQ:
                            self.recip(dve, g, 4 * h + 3)
                        if h < GQ - 1:
                            rope(h + 3, h % 2, h + 2, 0)
                        if h >= 1:
                            dve.wait_ge(s1["pv"].sem, s1["pv"].at(h, g))
                            dve.tensor_copy(OT1[:, h - 1, :], PS[:, 6, :]).then_inc(s1["oT"].sem, 1)
                    for t in range(NT):
                        dve.wait_ge(s1["y"].sem, s1["y"].at(t + 1, g))
                        dve.tensor_tensor(XB[:, t, :], PS[:, 7 - t % 2, :], XB[:, t, :], ALU.add)\
                           .then_inc(s1["added"].sem, 1)
                dve.wait_ge(s1["added"].sem, s1["added"].at(NT, NG - 1))
                self.tail.vector(dve, st)

            def recip(self, dve, g, m):
                dve.wait_ge(s1["exp"].sem, s1["exp"].at(m + 1, g))
                h, i = m // 4, m % 4
                dve.reciprocal(RCP[:, h % 2, i:i + 1], SM[:, h % 2, i:i + 1]).then_inc(s1["recip"].sem, 1)

            def scalar(self, act):
                with act.Fori(0, NG) as g:
                    for h in range(GQ + 1):
                        for i in range(NT):
                            if h < GQ:
                                m = 4 * h + i
                                act.wait_ge(s1["negmax"].sem, s1["negmax"].at(m + 1, g))
                                n = (i + 1) * P
                                if i == 0 and h >= 2:
                                    act.wait_ge(s1["pT_psum"].sem, s1["pT_psum"].at(4 * (h - 1), g))
                                act.activation(PR[:, h % 2, OFF[i]:OFF[i] + n], PS[:, 2 + i % 2, 0:n],
                                               ACT.Exp, bias=NX[:, h % 2, i:i + 1],
                                               accum_out=SM[:, h % 2, i:i + 1]).then_inc(s1["exp"].sem, 1)
                        if h >= 1:
                            for i in range(NT):
                                act.wait_ge(s1["pT_psum"].sem, s1["pT_psum"].at(4 * (h - 1) + i + 1, g))
                                act.copy(PRT[:, (h - 1) % 2, 0:i + 1, i * P:(i + 1) * P],
                                         PS[:, 4 + i % 2, 0:(i + 1) * P].rearrange("p (j q) -> p j q", q=P))\
                                   .then_inc(s1["pT"].sem, 1)
                self.tail.scalar(act)

            def gpsimd(self, pool, st):
                with pool.Fori(0, NG) as g:

                    def rope(n, slot, r, dst):
                        pool.wait_ge(s1["proj_read"].sem, s1["proj_read"].at(n + 1, g))
                        pool.tensor_tensor(dst, RA[:, slot, :], RB[:, slot, :], ALU.add)\
                            .then_inc(s1["rope"].sem, 1)
                    pool.wait_ge(s1["scores"].sem, s1["scores"].at(0, g))
                    rope(0, 0, 0, kT[:, :])
                    rope(2, 1, 1, qT[:, 0, :])
                    for h in range(GQ):
                        for i in range(NT):
                            m = 4 * h + i
                            pool.wait_ge(s1["recip"].sem, s1["recip"].at(m + 1, g))
                            pr = PR[:, h % 2, OFF[i]:OFF[i] + (i + 1) * P]
                            alone(pool)
                            pool.tensor_scalar(pr, pr, RCP[:, h % 2, i:i + 1], 1.0, ALU.mult, ALU.mult)\
                                .then_inc(s1["norm"].sem, 1)
                        if h < GQ - 1:
                            rope(h + 3, h % 2, h + 2, qT[:, (h + 1) % 2, :])
                self.tail.gpsimd(pool, st)

            def sync(self, sp):
                sp.dma_start(TAB[:, :, :], d["c_rope1"]).then_inc(s1["tab"].sem, 16)
                with sp.Fori(0, NG) as g:
                    sp.wait_ge(s1["proj"].sem, s1["proj"].at(0, g))
                    alone(sp)
                    sp.dma_start(WB[:, 0:3072], d["w1qkv"][g]).then_inc(s1["qkv_loaded"].sem, 16)
                    sp.wait_ge(s1["y"].sem, s1["y"].at(0, g))
                    alone(sp)
                    sp.dma_start(WB[:, 3072:5120], d["w1o"][g]).then_inc(s1["wo_loaded"].sem, 16)

        F1 = ExitStack()
        H1 = sb("H1", [P, 2, T], F32, F1)
        SG = sb("SG", [P, 2, T], F32, F1)
        AD = sb("AD", [P, D], F32, F1)
        AGU = sb("AGU", [P, 2, M1], F32, F1)
        F1.close()
        f1 = {k: sig("f1_" + k, 0, n) for k, n in dict(
            scales_loaded=32, w0=16 * 4, w1=16 * 4, w2=16 * 3, gu_psum=M1, silu=M1, h=M1, down=M1).items()}
        RING = 3
        f1w = [WC[:, s * 1536:(s + 1) * 1536] for s in range(RING)]

        def gated(pe, m, gate, up):
            for b, pairs in ((m % 2, gate), (2 + m % 2, up)):
                for i, (w, x) in enumerate(pairs):
                    ins = pe.matmul(PS[:, b, :], w, x, start=(i == 0), stop=(i == len(pairs) - 1))
            return ins

        class Ffn1(Stage):
            def __init__(self, loop):
                self.tail = Tail(loop, y_done=(f1["down"], M1), mul=AD[:, :])

            def tensor(self, pe):
                for m in range(M1 + 1):
                    if m < M1:
                        w = f1w[m % RING]
                        pe.wait_ge(f1[f"w{m % RING}"].sem, f1[f"w{m % RING}"].at(16 * (m // RING + 1)))
                        if m >= 2:
                            pe.wait_ge(f1["h"].sem, f1["h"].at(m - 1))
                        gated(pe, m, [(w[:, c * P:(c + 1) * P], XT[:, c, :]) for c in range(NC)],
                              [(w[:, 512 + c * P:512 + (c + 1) * P], XT[:, c, :]) for c in range(NC)])\
                            .then_inc(f1["gu_psum"].sem, 1)
                    if m >= 1:
                        k = m - 1
                        pe.wait_ge(f1["h"].sem, f1["h"].at(k + 1))
                        for t in range(NT):
                            x = pe.matmul(PS[:, 4 + t, :], H1[:, k % 2, t * P:(t + 1) * P],
                                          f1w[k % RING][:, 1024:1536], start=(k == 0), stop=(k == M1 - 1))
                        x.then_inc(f1["down"].sem, 1)
                self.tail.tensor(pe)

            def scalar(self, act):
                act.wait_ge(f1["scales_loaded"].sem, f1["scales_loaded"].at(32))
                for m in range(M1):
                    act.wait_ge(f1["gu_psum"].sem, f1["gu_psum"].at(m + 1))
                    if m >= 2:
                        act.wait_ge(f1["h"].sem, f1["h"].at(m - 1))
                    act.activation(SG[:, m % 2, :], PS[:, m % 2, :], ACT.Silu, scale=AGU[:, 0, m:m + 1])\
                       .then_inc(f1["silu"].sem, 1)
                self.tail.scalar(act)

            def vector(self, dve, st):
                dve.wait_ge(f1["scales_loaded"].sem, f1["scales_loaded"].at(32))
                for m in range(M1):
                    dve.wait_ge(f1["silu"].sem, f1["silu"].at(m + 1))
                    if m >= 2:
                        dve.wait_ge(f1["down"].sem, f1["down"].at(m - 1))
                    dve.scalar_tensor_tensor(H1[:, m % 2, :], PS[:, 2 + m % 2, :], AGU[:, 1, m:m + 1],
                                             SG[:, m % 2, :], ALU.mult, ALU.mult).then_inc(f1["h"].sem, 1)
                self.tail.vector(dve, st)

            def gpsimd(self, pool, st):
                self.tail.gpsimd(pool, st)

            def sync(self, sp):
                sp.dma_start(AGU[:, :, :], d["f1_agu"]).then_inc(f1["scales_loaded"].sem, 16)
                sp.dma_start(AD[:, :], d["f1_ad"].partition_broadcast(P)).then_inc(f1["scales_loaded"].sem, 16)
                for m in range(M1):
                    if m >= RING:
                        sp.wait_ge(f1["down"].sem, f1["down"].at(m - RING + 1))
                    sp.dma_start(f1w[m % RING], d["f1_w"][m]).then_inc(f1[f"w{m % RING}"].sem, 16)

        F2 = ExitStack()
        LO = sb("LO", [P, NT, P], F32, F2)
        LG = sb("LG", [P, NT, 8], F32, F2)
        M82 = sb("M82", [P, NT, 8], F32, F2)
        I8 = sb("I8", [P, NT, 8], U32, F2)
        IF = sb("IF", [P, NT, 2], F32, F2)
        WF = sb("WF", [P, 2, NT, 8], F32, F2)
        GW = sb("GW", [P, 4, NT], F32, F2)
        LT = sb("LT", [P, T], F32, F2)
        F2.close()
        f2 = {k: sig("f2_" + k, 0, n) for k, n in dict(
            low_psum=1, diff=1, exp=1, low_ready=1, lT_psum=1, lT_ready=1).items()}
        f2_base = WC[:, 0:2048].rearrange("p (c n) -> p c n", c=NC)
        f2_ga = WC[:, 2048:2592].rearrange("p (c n) -> p c n", c=NC)
        f2_B = WC[:, 2592:3104]
        f2_b = WC[:, 3104:3616]

        class Ffn2(Stage):
            def __init__(self, loop):
                self.tail = Tail(loop, self.y_tile, add=f2_b)

            def y_tile(self, pe, t, ps):
                for c in range(NC):
                    pe.matmul(ps, XT[:, c, t * P:(t + 1) * P], f2_base[:, c, :], start=(c == 0), stop=False)
                return pe.matmul(ps, LT[:, t * P:(t + 1) * P], f2_B, start=False, stop=True)

            def low(self, t):
                return PS[:, 4 + t // 2, 256 * (t % 2):256 * (t % 2) + 136]

            def tensor(self, pe):
                pe.wait_ge(S_wc.sem, S_wc.at(W_C[1]))
                for t in range(NT):
                    for c in range(NC):
                        x = pe.matmul(self.low(t), XT[:, c, t * P:(t + 1) * P], f2_ga[:, c, :],
                                      start=(c == 0), stop=(c == NC - 1))
                x.then_inc(f2["low_psum"].sem, 1)
                pe.wait_ge(f2["low_ready"].sem, f2["low_ready"].at(1))
                for t in range(NT):
                    x = pe.transpose(PS[:, 6, t * P:(t + 1) * P], LO[:, t, :], ident[:, :])
                x.then_inc(f2["lT_psum"].sem, 1)
                pe.wait_ge(f2["lT_ready"].sem, f2["lT_ready"].at(1))
                self.tail.tensor(pe)

            def scalar(self, act):
                act.wait_ge(f2["diff"].sem, f2["diff"].at(1))
                act.activation(GW[:, 1, :], GW[:, 0, :], ACT.Exp).then_inc(f2["exp"].sem, 1)
                act.wait_ge(f2["lT_psum"].sem, f2["lT_psum"].at(1))
                act.copy(LT[:, :], PS[:, 6, :]).then_inc(f2["lT_ready"].sem, 1)
                self.tail.scalar(act)

            def gpsimd(self, pool, st):
                self.tail.gpsimd(pool, st)

            def vector(self, dve, st):
                dve.wait_ge(S_wc.sem, S_wc.at(W_C[1]))
                dve.wait_ge(f2["low_psum"].sem, f2["low_psum"].at(1))
                for t in range(NT):
                    st.done(dve.tensor_copy(LG[:, t, :], self.low(t)[:, P:P + 8]))
                st.wait()
                alone(dve)
                alone(dve)
                for t in range(NT):
                    st.done(dve.max(M82[:, t, :], LG[:, t, :]))
                st.wait()
                alone(dve)
                for t in range(NT):
                    st.done(dve.max_index(I8[:, t, :], M82[:, t, :], LG[:, t, :]))
                dve.tensor_tensor(GW[:, 0, :], M82[:, :, 1], M82[:, :, 0], ALU.subtract)\
                   .then_inc(f2["diff"].sem, 1)
                st.wait()
                st.done(dve.tensor_copy(IF[:, :, :], I8[:, :, 0:2]))
                dve.wait_ge(f2["exp"].sem, f2["exp"].at(1))
                st.link(dve.tensor_scalar(GW[:, 2, :], GW[:, 1, :], 1.0, None, ALU.add))
                st.link(dve.reciprocal(GW[:, 2, :], GW[:, 2, :]))
                st.link(dve.tensor_scalar(GW[:, 2, :], GW[:, 2, :], 2.0, None, ALU.mult))
                st.link(dve.tensor_tensor(GW[:, 3, :], GW[:, 2, :], GW[:, 1, :], ALU.mult))
                bc = lambda a: a.unsqueeze(2).to_broadcast([P, NT, 8])
                for k in range(2):
                    st.link(dve.tensor_tensor(WF[:, k, :, :], iota8[:, :].unsqueeze(1).to_broadcast([P, NT, 8]),
                                              bc(IF[:, :, k]), ALU.is_equal))
                    st.link(dve.tensor_tensor(WF[:, k, :, :], WF[:, k, :, :], bc(GW[:, 2 + k, :]), ALU.mult))
                st.link(dve.tensor_tensor(WF[:, 0, :, :], WF[:, 0, :, :], WF[:, 1, :, :], ALU.add))
                for t in range(NT):
                    x = dve.tensor_tensor(LO[:, t, :].rearrange("p (e r) -> p e r", e=8),
                                          self.low(t)[:, 0:P].rearrange("p (e r) -> p e r", e=8),
                                          WF[:, 0, t, :].unsqueeze(2).to_broadcast([P, 8, 16]), ALU.mult)
                x.then_inc(f2["low_ready"].sem, 1)
                self.tail.vector(dve, st)

        F3 = ExitStack()
        XS = sb("XS", [P, T], F32, F3)
        Z = sb("Z", [4, T], F32, F3)
        Z2 = sb("Z2", [2, T], F32, F3)
        H3 = sb("H3", [P, M3, T], F32, F3)
        HS = sb("HS", [P, 3, T], F32, F3)
        SG3 = sb("SG3", [P, 2, T], F32, F3)
        B2 = sb("B2", [2, D], F32, F3)
        F3.close()
        f3 = {k: sig("f3_" + k, 0, n) for k, n in dict(
            b2_loaded=16, xs=1, z_psum=1, z=1, gu_psum=M3, silu=M3, h=M3, z2_psum=1, z2=1, hs=3).items()}
        w3 = WA[:, :]
        f3_w1, f3_w3 = w3[:, 0:1536], w3[:, 1536:3072]
        f3_w2 = w3[:, 3072:4608].rearrange("p (k n) -> p k n", k=3)
        f3_b1, f3_b3 = w3[0:4, 4608:6144], w3[0:4, 6144:7680]
        f3_a13 = w3[:, 7680:7696].rearrange("p (c n) -> p c n", c=NC)
        f3_a2 = w3[:, 7696:7720].rearrange("p (m n) -> p m n", m=M3)

        class Ffn3(Stage):
            def __init__(self, loop):
                self.tail = Tail(loop, self.y_tile, last=True)

            def y_tile(self, pe, t, ps):
                for k in range(3):
                    pe.matmul(ps, HS[:, k, t * P:(t + 1) * P], f3_w2[:, k, :], start=(k == 0), stop=False)
                return pe.matmul(ps, Z2[:, t * P:(t + 1) * P], B2[:, :], start=False, stop=True)

            def tensor(self, pe):
                pe.wait_ge(S_wa.sem, S_wa.at(W_A[1]))
                for c in range(NC):
                    x = pe.matmul(PS[0:4, 7, :], f3_a13[:, c, :], XT[:, c, :], start=(c == 0), stop=(c == NC - 1))
                x.then_inc(f3["z_psum"].sem, 1)
                pe.wait_ge(f3["xs"].sem, f3["xs"].at(1))
                pe.wait_ge(f3["z"].sem, f3["z"].at(1))
                for m in range(M3):
                    if m >= 2:
                        pe.wait_ge(f3["h"].sem, f3["h"].at(m - 1))
                    cols = slice(m * P, (m + 1) * P)
                    gated(pe, m, [(f3_w1[:, cols], XS[:, :]), (f3_b1[:, cols], Z[:, :])],
                          [(f3_w3[:, cols], XS[:, :]), (f3_b3[:, cols], Z[:, :])])\
                        .then_inc(f3["gu_psum"].sem, 1)
                for m in range(M3):
                    pe.wait_ge(f3["h"].sem, f3["h"].at(m + 1))
                    x = pe.matmul(PS[0:2, 6, :], f3_a2[:, m, :], H3[:, m, :], start=(m == 0), stop=(m == M3 - 1))
                x.then_inc(f3["z2_psum"].sem, 1)
                pe.wait_ge(f3["b2_loaded"].sem, f3["b2_loaded"].at(16))
                pe.wait_ge(f3["z2"].sem, f3["z2"].at(1))
                pe.wait_ge(f3["hs"].sem, f3["hs"].at(3))
                self.tail.tensor(pe)

            def scalar(self, act):
                for m in range(M3):
                    act.wait_ge(f3["gu_psum"].sem, f3["gu_psum"].at(m + 1))
                    if m >= 2:
                        act.wait_ge(f3["h"].sem, f3["h"].at(m - 1))
                    act.activation(SG3[:, m % 2, :], PS[:, m % 2, :], ACT.Silu).then_inc(f3["silu"].sem, 1)
                act.wait_ge(f3["z2_psum"].sem, f3["z2_psum"].at(1))
                act.mul(Z2[:, :], PS[0:2, 6, :], 0.5).then_inc(f3["z2"].sem, 1)

            def vector(self, dve, st):
                st.done(dve.tensor_tensor(XS[:, :], XT[:, 0, :], XT[:, 1, :], ALU.add))
                st.link(dve.tensor_tensor(SG3[:, 0, :], XT[:, 2, :], XT[:, 3, :], ALU.add))
                dve.tensor_tensor(XS[:, :], XS[:, :], SG3[:, 0, :], ALU.add).then_inc(f3["xs"].sem, 1)
                dve.wait_ge(f3["z_psum"].sem, f3["z_psum"].at(1))
                dve.tensor_scalar(Z[:, :], PS[0:4, 7, :], 0.5, None, ALU.mult).then_inc(f3["z"].sem, 1)
                for m in range(M3):
                    dve.wait_ge(f3["silu"].sem, f3["silu"].at(m + 1))
                    dve.tensor_tensor(H3[:, m, :], PS[:, 2 + m % 2, :], SG3[:, m % 2, :], ALU.mult)\
                       .then_inc(f3["h"].sem, 1)
                dve.wait_ge(f3["h"].sem, f3["h"].at(M3))
                for k in range(3):
                    st.link(dve.tensor_tensor(HS[:, k, :], H3[:, k, :], H3[:, 3 + k, :], ALU.add))
                    st.link(dve.tensor_tensor(HS[:, k, :], HS[:, k, :], H3[:, 6 + k, :], ALU.add))
                    dve.tensor_tensor(HS[:, k, :], HS[:, k, :], H3[:, 9 + k, :], ALU.add)\
                       .then_inc(f3["hs"].sem, 1)
                self.tail.vector(dve, st)

            def gpsimd(self, pool, st):
                self.tail.gpsimd(pool, st)

        s_lv = sig("logvar_arg_ready", 1, 0)
        s_lvd = sig("logvar_ready", 1, 0)

        class LogVar(Stage):
            def vector(self, dve, st):
                for t in range(NT):
                    st.link(dve.bn_stats(stat[:, t % 2, :], XB[:, t, :]))
                    alone(dve)
                    st.link(dve.bn_aggr(mv[:, t % 2, :], stat[:, t % 2, :]))
                    x = dve.tensor_copy(VV[:, t:t + 1], mv[:, t % 2, 1:2])
                    st.link(x) if t < NT - 1 else x.then_inc(s_lv.sem, 1)

            def scalar(self, act):
                act.wait_ge(s_lv.sem, s_lv.at(1))
                lv = LV[:, :].rearrange("p (b t) -> p b t", b=NB)[:, Signal.batch, :]
                act.activation(lv, VV[:, :], ACT.Ln, bias=1.0).then_inc(s_lvd.sem, 1)
                act.wait_ge(s_lvd.sem, s_lvd.at(1))

        s_in = sig("xin_T_psum", 0, NT)
        s_ind = sig("xin_T", 0, NT)

        class Enter(Stage):
            def __init__(self, loop):
                self.loop = loop

            def tensor(self, pe):
                pe.wait_ge(S_x.sem, S_x.at(16))
                for t in range(NT):
                    if t >= 2:
                        pe.wait_ge(s_ind.sem, s_ind.at(t - 1))
                    for c in range(NC):
                        x = pe.transpose(PS[:, t % 2, c * P:(c + 1) * P], XB[:, t, c * P:(c + 1) * P], ident[:, :])
                    x.then_inc(s_in.sem, 1)

            def scalar(self, act):
                for t in range(NT):
                    act.wait_ge(s_in.sem, s_in.at(t + 1))
                    act.copy(XT[:, :, t * P:(t + 1) * P], PS[:, t % 2, :].rearrange("p (c q) -> p c q", c=NC))\
                       .then_inc(s_ind.sem, 1)

        consts += [(iota8[:, :], d["c_iota8"]), (cos0[:, :, :], d["c_cos0"]), (sin0[:, :, :], d["c_sin0"])]
        W0 = WA[:, 0:3072].rearrange("p (c u n) -> p c u n", c=NC, u=UNITS)
        Wo0 = WA[:, 3072:5120].rearrange("p (c n) -> p c n", c=NC)
        b0 = WA[:, 5120:5888].rearrange("p (u n) -> p u n", u=UNITS)
        bo0 = WA[:, 5888:6400]
        W2 = WA[:, 0:6144].rearrange("p (c u n) -> p c u n", c=NC, u=UNITS)
        Wo2 = WA[:, 6144:8192].rearrange("p (c n) -> p c n", c=NC)
        b2 = WC[:, 3616:5152].rearrange("p (u n) -> p u n", u=UNITS)
        bo2 = WC[:, 5152:5664]
        W3 = WB[:, 0:3072].rearrange("p (c u n) -> p c u n", c=NC, u=UNITS)
        Wo3 = WB[:, 3072:5120].rearrange("p (c n) -> p c n", c=NC)
        W_A, W_B, W_C = [16, 32], [16], [16, 64]
        S_w0 = sig("w0_loaded")
        S_wa.per[1], S_wb.per[1], S_wc.per[1] = 32, 16, 64

        def load0(eng):
            eng.wait_ge(S_w0.sem, 16 * 4)

        def load2(eng):
            eng.wait_ge(S_wa.sem, S_wa.at(16))
            eng.wait_ge(S_wc.sem, S_wc.at(48))

        def load3(eng):
            eng.wait_ge(S_wb.sem, S_wb.at(16))

        S_x.per = [16 * 2, 16]
        S_store.per = [16, 16]
        passes = [
            [Attention16(0, W0, Wo0, 8, 1.0 / 16, load0, b0, (cos0, sin0), bo0, last=True), LogVar()],
            [Enter(1), Ffn0(1), Attention1(1), Ffn1(1),
             Attention16(1, W2, Wo2, 32, 0.25, load2, b2, None, bo2), Ffn2(1),
             Attention16(1, W3, Wo3, 8, 0.25, load3), Ffn3(1)]]
        S_bar.per = [4 * len(p) for p in passes]

        block = ctx.enter_context(nc.Block())
        steps = {"vector": [], "gpsimd": []}

        @block.tensor
        def _(pe):
            pe.wait_ge(start.sem, START)
            pe.wait_ge(S_const.sem, 16 * len(consts))
            for loop in range(2):
                Signal.loop = loop
                with pe.Fori(0, NB) as b:
                    Signal.batch = b
                    pe.wait_ge(S_x.sem, S_x.at(S_x.per[loop]))
                    for k, stage in enumerate(passes[loop]):
                        stage.tensor(pe)
                        alone(pe)
                        pe.drain().then_inc(S_bar.sem, 1)
                        pe.wait_ge(S_bar.sem, S_bar.at(4 * (k + 1)))
                        alone(pe)

        @block.scalar
        def _(act):
            act.wait_ge(start.sem, START)
            for loop in range(2):
                Signal.loop = loop
                with act.Fori(0, NB) as b:
                    Signal.batch = b
                    act.wait_ge(S_x.sem, S_x.at(S_x.per[loop]))
                    for k, stage in enumerate(passes[loop]):
                        stage.scalar(act)
                        alone(act)
                        act.drain().then_inc(S_bar.sem, 1)
                        act.wait_ge(S_bar.sem, S_bar.at(4 * (k + 1)))
                        alone(act)

        @block.vector
        def _(dve):
            dve.memset(ones[:, :], 1.0).then_inc(start.sem, 1)
            dve.memset(halfneg[:, :], -0.5).then_inc(start.sem, 1)
            dve.wait_ge(S_const.sem, 16 * len(consts))
            dve.tensor_copy(ident_masks_b[:], ident_masks[:]).then_inc(start.sem, 1)
            dve.wait_ge(start.sem, START)
            dve.wait_ge(S_w0.sem, 16 * 4)
            st = Steps(dve, S_step)
            for loop in range(2):
                Signal.loop = loop
                st.n = 0
                with dve.Fori(0, NB) as b:
                    Signal.batch = b
                    dve.wait_ge(S_x.sem, S_x.at(S_x.per[loop]))
                    for k, stage in enumerate(passes[loop]):
                        stage.vector(dve, st)
                        alone(dve)
                        dve.drain().then_inc(S_bar.sem, 1)
                        dve.wait_ge(S_bar.sem, S_bar.at(4 * (k + 1)))
                        alone(dve)
                steps["vector"].append(st.n)

        @block.gpsimd
        def _(pool):
            for s in sigs.values():
                if s.credit:
                    pool.sem_inc(s.sem, s.credit)
            pool.sem_inc(start.sem, 1)
            pool.wait_ge(start.sem, START)
            st = Steps(pool, S_pstep)
            for loop in range(2):
                Signal.loop = loop
                st.n = 0
                with pool.Fori(0, NB) as b:
                    Signal.batch = b
                    pool.wait_ge(S_x.sem, S_x.at(S_x.per[loop]))
                    for k, stage in enumerate(passes[loop]):
                        stage.gpsimd(pool, st)
                        alone(pool)
                        pool.drain().then_inc(S_bar.sem, 1)
                        pool.wait_ge(S_bar.sem, S_bar.at(4 * (k + 1)))
                        alone(pool)
                steps["gpsimd"].append(st.n)

        @block.sync
        def _(sp):
            for buf, src in consts:
                sp.dma_start(buf, src).then_inc(S_const.sem, 16)
            sp.dma_start(WA[:, 0:3072], d["w0qkv"]).then_inc(S_w0.sem, 16)
            sp.dma_start(WA[:, 3072:5120], d["w0o"]).then_inc(S_w0.sem, 16)
            sp.dma_start(WA[:, 5120:5888], d["b0qkv"].partition_broadcast(P)).then_inc(S_w0.sem, 16)
            sp.dma_start(WA[:, 5888:6400], d["b0o"].partition_broadcast(P)).then_inc(S_w0.sem, 16)
            sp.wait_ge(start.sem, START)
            Signal.loop = 0
            with sp.Fori(0, NB) as b:
                Signal.batch = b
                sp.dma_start(XB[:, :, :], d["x"][b]).then_inc(S_x.sem, 16)
                sp.dma_start(XT[:, :, :], d["xT"][b]).then_inc(S_x.sem, 16)
                sp.wait_ge(S_bar.sem, S_bar.at(S_bar.per[0]))
                sp.dma_start(xmid[b], XB[:, :, :]).then_inc(S_store.sem, 16)
                sp.wait_ge(S_store.sem, S_store.at(16))
                alone(sp)
            Signal.loop = 1
            with sp.Fori(0, NB) as b:
                Signal.batch = b
                sp.dma_start(XB[:, :, :], xmid[b]).then_inc(S_x.sem, 16)
                sp.dma_start(WC[:, 0:2293], d["f0_w"]).then_inc(S_wc.sem, 16)
                sp.dma_start(WA[:, :], d["w2"]).then_inc(S_wa.sem, 16)
                passes[1][2].sync(sp)
                sp.wait_ge(S_bar.sem, S_bar.at(4 * 3))
                sp.dma_start(WB[:, :], d["w3"]).then_inc(S_wb.sem, 16)
                passes[1][3].sync(sp)
                sp.wait_ge(S_bar.sem, S_bar.at(4 * 4))
                sp.dma_start(WC[:, 3616:5152], d["b2qkv"].partition_broadcast(P)).then_inc(S_wc.sem, 16)
                sp.dma_start(WC[:, 5152:5664], d["b2o"].partition_broadcast(P)).then_inc(S_wc.sem, 16)
                sp.wait_ge(S_wc.sem, S_wc.at(48))
                sp.dma_start(WC[:, 0:3616], d["f2_w"]).then_inc(S_wc.sem, 16)
                sp.wait_ge(S_bar.sem, S_bar.at(4 * 5))
                sp.dma_start(WA[:, 0:7720], d["f3_w"]).then_inc(S_wa.sem, 16)
                sp.wait_ge(S_bar.sem, S_bar.at(4 * 7))
                sp.dma_start(B2[:, :], d["f3_b2"]).then_inc(f3["b2_loaded"].sem, 16)
                sp.wait_ge(S_bar.sem, S_bar.at(4 * 8))
                sp.dma_start(out[b], XB[:, :, :]).then_inc(S_store.sem, 16)
                sp.wait_ge(S_store.sem, S_store.at(16))
                alone(sp)
            sp.wait_ge(S_store.sem, 16 * 2 * NB)

    assert all(tuple(steps[k]) == STEPS[k] for k in STEPS), steps
    return steps


def chunked(w):
    k = w.shape[0] // P
    return np.ascontiguousarray(w.reshape(k, P, -1).transpose(1, 0, 2))


def heads(w, n, width):
    return w.reshape(n, width, *w.shape[1:])


def tables():
    f = np.float32
    c = {}
    eye = np.eye(P, dtype=f)
    q, k = np.arange(P)[:, None], np.arange(P)[None, :]
    m = np.where(k > q, f(MASKED), f(0))
    c["c_ident_masks"] = np.stack([eye, m, m.T], 1)
    c["c_iota8"] = np.tile(np.arange(8, dtype=f), (P, 1))
    pos = np.arange(T, dtype=f)
    inv = (1.0 / 1000000.0 ** (np.arange(0, HD, 2, dtype=f) / f(HD))).astype(f)
    fr = np.outer(pos, inv).astype(f)
    cos, sin = np.cos(fr), np.sin(fr)
    tile = lambda a: np.ascontiguousarray(a.reshape(NT, P, HD).transpose(1, 0, 2)).astype(f)
    c["c_cos0"] = tile(np.concatenate([cos, cos], 1))
    c["c_sin0"] = tile(np.concatenate([-sin, sin], 1))
    inv = (1.0 / 500000.0 ** (np.arange(0, L1D, 2, dtype=f) / L1D)).astype(f)
    wl = 2.0 * np.pi / inv
    scaled = np.where(wl > 1024 / 1.0, inv / 8.0, inv)
    smooth = (1024 / wl - 1.0) / (4.0 - 1.0)
    smoothed = (1.0 - smooth) / 8.0 * inv + smooth * inv
    medium = (wl <= 1024 / 1.0) & (wl >= 1024 / 4.0)
    inv = np.where(medium, smoothed, scaled).astype(f)
    fr = (pos[:, None] * inv[None, :]).astype(f).T
    cos, sin = np.cos(fr).astype(np.float64), np.sin(fr).astype(np.float64)
    both = np.concatenate([cos, cos], 0)
    swap = np.concatenate([sin, -sin], 0)
    sc = 1.0 / np.sqrt(128.0)
    c["c_rope1"] = np.ascontiguousarray(np.stack([both * sc, swap * sc, both, swap], 1)).astype(f)
    return c


def layout(i):
    f = np.float32
    a = {}
    x = i["L0_attn_hidden_states"]
    a["x"] = np.ascontiguousarray(x.reshape(NB, NT, P, D).transpose(0, 2, 1, 3))
    a["xT"] = np.ascontiguousarray(x.transpose(0, 2, 1).reshape(NB, NC, P, T).transpose(0, 2, 1, 3))

    def units(q, k, v):
        h = lambda w, u: np.split(w, UNITS)[u]
        return np.concatenate([np.concatenate([h(q, u), h(k, u), h(v, u)]) for u in range(UNITS)])

    def split0(w):
        w = w.reshape(8, 6, HD, *w.shape[1:])
        r = w.shape[3:]
        return w[:, 0:4].reshape(512, *r), w[:, 4].reshape(128, *r), w[:, 5].reshape(128, *r)
    a["w0qkv"] = chunked(np.ascontiguousarray(units(*split0(i["L0_attn_w_qkv"])).T)).reshape(P, -1)
    a["b0qkv"] = units(*split0(i["L0_attn_b_qkv"]))
    a["w0o"] = chunked(i["L0_attn_w_dense"].T).reshape(P, -1)
    a["b0o"] = i["L0_attn_b_dense"]

    def col(n, w):
        r = np.zeros((P, w[0].size), f)
        r[:w.shape[0]] = w.reshape(w.shape[0], -1)
        assert r.shape[1] == n
        return r
    bc = lambda v: np.tile(v.reshape(1, -1), (P, 1))
    a["f0_w"] = np.concatenate([
        col(256, chunked(i["L0_ffn_Wq"].T)), col(512, chunked(i["L0_ffn_Wu1"].T)),
        col(128, chunked(i["L0_ffn_Wvd"].T)), col(512, chunked(i["L0_ffn_aux_values"].T)),
        col(64, i["L0_ffn_Wr"]), col(48, i["L0_ffn_Wr"].T), col(128, i["L0_ffn_aux_keys"].T),
        col(512, i["L0_ffn_Wvu"].T), bc(i["L0_ffn_log_rel"]),
        i["L0_ffn_bu1"].reshape(P, 1), i["L0_ffn_Wu2"].reshape(P, 1), bc(i["L0_ffn_bu2"]),
        bc(i["L0_ffn_gate_w1"]), bc(i["L0_ffn_gate_bias"])], 1).astype(f, copy=False)
    q = i["L1_attn_Wq"].reshape(L1KV, GQ * L1D, D)
    k = i["L1_attn_Wk"].reshape(L1KV, L1D, D)
    v = i["L1_attn_Wv"].reshape(L1KV, L1D, D)
    w = np.concatenate([q, k, v], 1).transpose(0, 2, 1)
    a["w1qkv"] = np.ascontiguousarray(w.reshape(L1KV, NC, P, 768).transpose(0, 2, 1, 3)).reshape(L1KV, P, -1)
    w = i["L1_attn_Wo"].T.reshape(L1KV, GQ, L1D, D)
    a["w1o"] = np.ascontiguousarray(w.transpose(0, 2, 1, 3)).reshape(L1KV, P, -1)
    pad = M1 * P - 1376

    def rows(w):
        return np.concatenate([w, np.zeros((pad,) + w.shape[1:], f)])
    gu = [rows(i[n]).reshape(M1, P, NC, P).transpose(0, 3, 2, 1).reshape(M1, P, 512)
          for n in ("L1_ffn_Wg", "L1_ffn_Wu")]
    dn = rows(np.ascontiguousarray(i["L1_ffn_Wd"].T)).reshape(M1, P, D)
    a["f1_w"] = np.ascontiguousarray(np.concatenate(gu + [dn], 2))
    a["f1_agu"] = np.ascontiguousarray(np.stack([rows(i["L1_ffn_ag"]).reshape(M1, P).T,
                                                 rows(i["L1_ffn_au"]).reshape(M1, P).T], 1))
    a["f1_ad"] = i["L1_ffn_ad"]
    w = units(i["L2_attn_Wq"], i["L2_attn_Wk"], i["L2_attn_Wv"]).T
    a["w2"] = np.concatenate([chunked(w).reshape(P, -1), chunked(i["L2_attn_Wo"].T).reshape(P, -1)], 1)
    a["b2qkv"] = units(i["L2_attn_bq"], i["L2_attn_bk"], i["L2_attn_bv"])
    a["b2o"] = i["L2_attn_bo"]
    ga = np.concatenate([i["L2_ffn_lora_A"].reshape(P, D), i["L2_ffn_gate_w"]]).T
    a["f2_w"] = np.concatenate([
        chunked(i["L2_ffn_base_w"].T).reshape(P, -1), chunked(ga).reshape(P, -1),
        i["L2_ffn_lora_B"].transpose(0, 2, 1).reshape(P, D), bc(i["L2_ffn_base_b"])], 1)
    w = units(i["L3_attn_wq"].T, i["L3_attn_wk"].T, i["L3_attn_wv"].T).T
    a["w3"] = np.concatenate([chunked(w).reshape(P, -1), chunked(i["L3_attn_wo"]).reshape(P, -1)], 1)

    def inter(w, axis=0):
        w = np.moveaxis(w, axis, 0)
        n = w.shape[0] // 344
        w = w.reshape(n, 344, *w.shape[1:])
        w = np.concatenate([w, np.zeros((n, 40) + w.shape[2:], f)], 1)
        return np.moveaxis(w.reshape(n * 384, *w.shape[2:]), 0, axis)
    z = np.zeros((2, 1376), f)
    a["f3_w"] = np.concatenate([
        np.ascontiguousarray(inter(i["L3_ffn_w1q"]).T), np.ascontiguousarray(inter(i["L3_ffn_w3q"]).T),
        chunked(inter(i["L3_ffn_w2q"].T)).reshape(P, -1),
        col(1536, inter(np.concatenate([i["L3_ffn_b1"].T, z]), 1)),
        col(1536, inter(np.concatenate([z, i["L3_ffn_b3"].T]), 1)),
        chunked(np.concatenate([i["L3_ffn_a1"], i["L3_ffn_a3"]]).T).reshape(P, -1),
        chunked(inter(i["L3_ffn_a2"].T)).reshape(P, -1)], 1)
    a["f3_b2"] = np.ascontiguousarray(i["L3_ffn_b2"].T)
    return {k: np.ascontiguousarray(v) for k, v in a.items()}


def kernel(**inputs):
    import concourse.bacc as bacc
    from concourse.bass_utils import run_bass_kernel_spmd
    arrays = {**layout({k: np.asarray(v) for k, v in inputs.items()}), **tables()}
    nc = bacc.Bacc("TRN2", target_bir_lowering=False, num_devices=1)
    d = {k: nc.dram_tensor(k, v.shape, mybir.dt.from_np(v.dtype), kind="ExternalInput").ap()
         for k, v in arrays.items()}
    out = nc.dram_tensor("out", (NB, P, NT, D), F32, kind="ExternalOutput").ap()
    build(nc, d, out)
    r = run_bass_kernel_spmd(nc, [arrays], core_ids=[0])
    y = r.results[0]["out"]
    return np.ascontiguousarray(y.transpose(0, 2, 1, 3)).reshape(NB, T, D)
```

```python
from contextlib import ExitStack

import numpy as np
import concourse.bass as bass
from concourse import mybir

F32 = mybir.dt.float32
BF16 = mybir.dt.bfloat16
F32R = mybir.dt.float32r
U32 = mybir.dt.uint32
ALU = mybir.AluOpType
ACT = mybir.ActivationFunctionType
AX = mybir.AxisListType

P = 128
NB = 2
T = 512
NT = T // P
D = 512
NC = D // P
EPS = 1e-5
MASKED = -1e30
TAKEN = -3e38

NH, HD = 32, 16
UNITS, UH = 2, 16
SLOTS = 6
SR = SLOTS * HD
MR = 3
REGION = {0: 0, 1: 512, 3: 896, 2: 1024}
SCOLS = 1280
EARLY = 2
PBS = 6

L1H, L1KV, L1D, GQ = 32, 8, 128, 4
M1 = 11
M3 = 12


class Signal:

    loop, batch = 0, 0

    def __init__(self, sem, name, first=0, second=0):
        self.sem, self.name, self.per = sem, name, [first, second]

    def at(self, n):
        before = NB * self.per[0] if Signal.loop else 0
        return Signal.batch * self.per[Signal.loop] + (before + n)

    def claim(self, loop, n):
        share = Share(self, self.per[loop])
        self.per[loop] += n
        return share


class GroupSignal(Signal):

    def __init__(self, sem, name, groups, each):
        super().__init__(sem, name, 0, groups * each)
        self.each = each

    def at(self, n, g):
        return super().at(n) + g * self.each


class Share:
    def __init__(self, whole, before):
        self.whole, self.sem, self.before = whole, whole.sem, before

    def at(self, n):
        return self.whole.at(self.before + n)


class Steps:

    def __init__(self, eng, sig):
        self.eng, self.sig, self.n = eng, sig, 0

    def done(self, ins):
        self.n += 1
        self.sig.n = self.n
        ins.then_inc(self.sig.sem, 1)
        return self.n

    def wait(self, n=None):
        self.eng.wait_ge(self.sig.sem, self.sig.at(self.n if n is None else n))

    def link(self, ins):
        self.done(ins)
        self.wait()


STEPS = {'vector': (83, 197)}


def build(nc, d, out):
    ctx = ExitStack()
    sigs = {}

    def sig(name, first=0, second=0):
        sigs[name] = Signal(ctx.enter_context(nc.semaphore(name)), name, first, second)
        return sigs[name]

    def sb(name, shape, dt=F32, where=None):
        return (where or ctx).enter_context(nc.sbuf_tensor(name, shape, dt))

    with ctx:
        PS = ctx.enter_context(nc.psum_tensor("PS", [P, 8, 512], F32))
        XB = sb("XB", [P, NT, D])
        XT = sb("XT", [P, NC, T])
        ident_masks = sb("ident_masks", [P, 3, P])
        ident_masks_b = sb("ident_masks_b", [P, 3, P], BF16)
        ident = ident_masks[:, 0]
        identb = ident_masks_b[:, 0]
        mask_qk = ident_masks_b[:, 1]
        mask_kq = ident_masks_b[:, 2]
        ones = sb("ones", [P, P])
        halfneg = sb("halfneg", [P, 1])
        S = sb("S", [P, 2, D])
        stat = sb("stat", [P, 2, 6])
        mv = sb("mv", [P, 2, 2])
        ve = sb("ve", [P, 2, 1])
        rstd = sb("rstd", [P, 2, 1])
        LV = sb("LV", [P, 2 * NB * NT])
        VV = sb("VV", [P, NT], F32)
        iota8 = sb("iota8", [P, 8])
        cos0 = sb("cos0", [P, NT, HD])
        sin0 = sb("sin0", [P, NT, HD])
        xmid = nc.dram_tensor("xmid", (P, NT, D), F32, kind="Internal").ap()

        WB = sb("WB", [P, 5120])
        WC = sb("WC", [P, 5664])

        S_const = sig("const_loaded")
        S_wa, S_wb, S_wc = sig("wa_loaded", 0, 32), sig("wb_loaded", 0, 32), sig("wc_loaded", 0, 32)
        S_x = sig("x_loaded", 16, 0)
        S_xT = sig("xT_loaded", 16, 0)
        S_bar = sig("stage_done")
        S_store = sig("x_stored", 16, 16)
        S_step = sig("vector_step", STEPS["vector"][0], STEPS["vector"][1])

        consts = []

        def const(name, shape, dt=F32, src=None):
            buf = sb(name, shape, dt)
            consts.append((buf[:], d[name] if src is None else src))
            return buf

        consts += [(ident_masks[:], d["c_ident_masks"])]

        start = sig("constants_ready")
        START = 3

        waited = sig("waited")

        def alone(eng):
            eng.sem_inc(waited.sem, 1)

        class Stage:

            def tensor(self, pe):
                pass

            def scalar(self, act):
                pass

            def vector(self, dve, st):
                pass

            def gpsimd(self, pool):
                pass

        TAIL = "y_ready var_ready rstd_ready x_ready xt_psum_ready xt_ready".split()
        s_tail = {k: sig("tail_" + k) for k in TAIL}

        class Tail(Stage):

            def __init__(self, loop, y_tile=None, y_done=None, mul=None, add=None, times=1.0,
                         last=False):
                self.times = times
                self.y, self.y_done, self.mul, self.add_t, self.last = y_tile, y_done, mul, add, last
                n = dict.fromkeys(TAIL, NT)
                if not y_tile:
                    n["y_ready"] = 0
                if last:
                    n["xt_psum_ready"] = n["xt_ready"] = 0
                self.s_y, self.s_v, self.s_r, self.s_x, self.s_tp, self.s_t = [
                    s_tail[k].claim(loop, n[k]) for k in TAIL]

            def tensor(self, pe):
                for t in range(NT + 2):
                    if t < NT and self.y:
                        if t >= 2:
                            pe.wait_ge(self.s_v.sem, self.s_v.at(t - 1))
                        self.y(pe, t, PS[:, t % 2, :]).then_inc(self.s_y.sem, 1)
                    if t >= 2 and not self.last:
                        u = t - 2
                        pe.wait_ge(self.s_x.sem, self.s_x.at(u + 1))
                        if u >= 2:
                            pe.wait_ge(self.s_t.sem, self.s_t.at(u - 1))
                        for c in range(NC):
                            x = pe.transpose(PS[:, 2 + u % 2, c * P:(c + 1) * P],
                                             XB[:, u, c * P:(c + 1) * P], ident[:, :])
                        x.then_inc(self.s_tp.sem, 1)

            def vector(self, dve, st):
                for t in range(NT + 1):
                    if t < NT:
                        src = S[:, t % 2, :]
                        if t >= 2:
                            dve.wait_ge(self.s_x.sem, self.s_x.at(t - 1))
                        if self.y or self.y_done:
                            if self.y:
                                dve.wait_ge(self.s_y.sem, self.s_y.at(t + 1))
                                y = PS[:, t % 2, :]
                            else:
                                dve.wait_ge(self.y_done[0].sem, self.y_done[0].at(self.y_done[1]))
                                y = PS[:, 4 + t, :]
                            if self.mul is not None:
                                st.link(dve.tensor_tensor(src, y, self.mul, ALU.mult))
                                y = src
                            st.link(dve.scalar_tensor_tensor(src, XB[:, t, :], self.times, y,
                                                             ALU.mult, ALU.add))
                            if self.add_t is not None:
                                st.link(dve.tensor_tensor(src, src, self.add_t, ALU.add))
                        else:
                            src = XB[:, t, :]
                        st.link(dve.bn_stats(stat[:, t % 2, :], src))
                        alone(dve)
                        st.link(dve.bn_aggr(mv[:, t % 2, :], stat[:, t % 2, :]))
                        dve.tensor_scalar(ve[:, t % 2, :], mv[:, t % 2, 1:2], EPS, None, ALU.add)\
                           .then_inc(self.s_v.sem, 1)
                    if t >= 1:
                        u = t - 1
                        dve.wait_ge(self.s_r.sem, self.s_r.at(u + 1))
                        src = S[:, u % 2, :] if self.y or self.y_done else XB[:, u, :]
                        dve.tensor_scalar(XB[:, u, :], src, mv[:, u % 2, 0:1], rstd[:, u % 2, :],
                                          ALU.subtract, ALU.mult).then_inc(self.s_x.sem, 1)
                dve.wait_ge(self.s_x.sem, self.s_x.at(NT))

            def gpsimd(self, pool):
                for t in range(NT):
                    pool.wait_ge(self.s_v.sem, self.s_v.at(t + 1))
                    if t >= 2:
                        pool.wait_ge(self.s_x.sem, self.s_x.at(t - 1))
                    pool.tensor_tensor(rstd[:, t % 2, :], ve[:, t % 2, :], halfneg[:, :], ALU.pow)\
                        .then_inc(self.s_r.sem, 1)

            def scalar(self, act):
                if self.last:
                    return
                for t in range(NT):
                    act.wait_ge(self.s_tp.sem, self.s_tp.at(t + 1))
                    act.copy(XT[:, :, t * P:(t + 1) * P],
                             PS[:, 2 + t % 2, :].rearrange("p (c q) -> p c q", c=NC))\
                       .then_inc(self.s_t.sem, 1)

        L1 = ExitStack()
        kT = sb("kT", [P, T], F32, L1)
        V1 = sb("V1", [P, NT, P], F32, L1)
        qT = sb("qT", [P, 2, T], F32, L1)
        RA = sb("RA", [P, 2, T], F32, L1)
        RB = sb("RB", [P, 2, T], F32, L1)
        PR = sb("PR", [P, 2, SCOLS], F32, L1)
        PRT = sb("PRT", [P, 2, NT, T], F32, L1)
        OTH = sb("OTH", [P, GQ, T], F32R, L1)
        OTL = sb("OTL", [P, GQ, T], F32R, L1)
        XH1 = sb("XH1", [P, NC, T], F32R, L1)
        XL1 = sb("XL1", [P, NC, T], F32R, L1)
        NX = sb("NX", [P, 2, NT], F32, L1)
        SM = sb("SM", [P, 2, NT], F32, L1)
        RCP = sb("RCP", [P, 2, NT], F32, L1)
        TAB = sb("TAB", [P, 4, T], F32, L1)
        A1H = sb("A1H", [P, NC, 256], F32R, L1)
        A1L = sb("A1L", [P, NC, 256], F32R, L1)
        B1H = sb("B1H", [P, NC, 384], F32R, L1)
        B1L = sb("B1L", [P, NC, 384], F32R, L1)
        Wo1H = sb("Wo1H", [P, GQ, D], F32R, L1)
        Wo1L = sb("Wo1L", [P, GQ, D], F32R, L1)
        L1.close()
        WA = sb("WA", [P, 8192])

        A16 = ExitStack()
        QT = sb("QT", [P, UH, T], BF16, A16)
        KT = sb("KT", [P, UH, T], BF16, A16)
        VA = sb("VA", [P, NT, UH, 32], F32, A16)
        PB = sb("PB", [P, PBS, SCOLS], F32, A16)
        CTX = sb("CTX", [P, NT, D], F32, A16)
        CT = PB[:, 0, 0:2 * D].rearrange("p (s n) -> p s n", s=2)
        QK = sb("QK", [P, 512], F32, A16)
        SPL = sb("SPL", [P, 3, 2 * UH, SR], BF16, A16)
        R1 = sb("R1", [P, 512], F32, A16)
        NM = sb("NM", [P, 2, UH], F32, A16)
        NMR = sb("NMR", [P, UH], F32, A16)
        NM3 = sb("NM3", [P, 2, MR * UH], BF16, A16)
        NMT = sb("NMT", [MR * UH, T], BF16, A16)
        OT = sb("OT", [P, 512], F32, A16)
        RT = OT[:, 0:320]
        RC = sb("RC", [P, NT, 4], F32, A16)
        A16.close()
        s16 = {k: sig("a16_" + k) for k in (
            "pads_ready qk_psum v_psum qk_ready h_ready m_ready parts_ready h_copied m_copied v_ready qkT_psum_ready qkT_ready qkT_ready_v scores_ready max_ready "
            "max_step max_parts_ready maxT_psum_ready maxT_ready max_rows_loaded scoresT_ready "
            "probs_ready pv_ready outT_ready out_psum_ready ctx_ready ctxT_psum_ready ctxT_ready").split()}

        class Attention16(Stage):
            def __init__(self, loop, W, Wo, nkv, scale, loaded, bias=None, rope=None, bo=None,
                         last=False, bias_loaded=None):
                self.W, self.Wo, self.scale, self.bias, self.rope = W, Wo, scale, bias, rope
                self.nk = nkv // UNITS
                self.rep = UH // self.nk
                self.nqk = UH * HD + self.nk * HD
                self.nv = self.nk * HD
                self.loop, self.loaded, self.bias_loaded = loop, loaded, bias_loaded
                self.tail = Tail(loop, self.y_tile, add=bo, last=last)
                hs = UH + self.nk
                self.lots = [(a, min(8, hs - a)) for a in range(0, hs, 8)]
                L, N = len(self.lots), UNITS * NT
                events = dict(pads_ready=3, qk_psum=N, v_psum=N, v_ready=N, parts_ready=N, qk_ready=N,
                              h_ready=N, m_ready=N, h_copied=N, m_copied=3 * N,
                              qkT_psum_ready=N * L, qkT_ready=self.copied(N * L)[0], qkT_ready_v=self.copied(N * L)[1], scores_ready=4 * N,
                              max_ready=4 * N, max_step=3 * N, max_parts_ready=N, maxT_psum_ready=N, maxT_ready=N,
                              max_rows_loaded=16 * UNITS, scoresT_ready=UNITS * UH,
                              probs_ready=UNITS * UH, pv_ready=4 * UNITS, outT_ready=4 * UNITS,
                              out_psum_ready=4 * UNITS, ctx_ready=4 * UNITS,
                              ctxT_psum_ready=NT, ctxT_ready=NT)
                self.on = {k: s16[k].claim(loop, n) for k, n in events.items()}

            def by_vector(self, m):
                return m // len(self.lots) % NT >= 2 and m % 2 == 1

            def copied(self, m):
                v = sum(self.by_vector(k) for k in range(m))
                return m - v, v

            def take_qkT(self, eng, copy, m):
                n, i = divmod(m, len(self.lots))
                a, k = self.lots[i]
                eng.wait_ge(self.on["qkT_psum_ready"].sem, self.on["qkT_psum_ready"].at(m + 1))
                tp = PS[:, 4 + m % 2, :].bitcast(BF16)[0:SR, 0:k * P]
                at = slice(n % NT * P, (n % NT + 1) * P)
                dst = QT[0:SR, a:a + k, at] if a < UH else KT[0:SR, a - UH:a - UH + k, at]
                return copy(dst, tp.rearrange("p (h q) -> p h q", q=P))

            def wait_qkT(self, pe, m, bank=None):
                act, dve = self.copied(m + 1)
                if bank is None or not self.by_vector(m):
                    pe.wait_ge(self.on["qkT_ready"].sem, self.on["qkT_ready"].at(act))
                if dve and (bank is None or self.by_vector(m)):
                    pe.wait_ge(self.on["qkT_ready_v"].sem, self.on["qkT_ready_v"].at(dve))

            def y_tile(self, pe, t, ps):
                if t + 1 < NT:
                    self.ctx_T(pe, t + 1)
                pe.wait_ge(self.on["ctxT_ready"].sem, self.on["ctxT_ready"].at(t + 1))
                for c in range(NC):
                    x = pe.matmul(ps, CT[:, t % 2, c * P:(c + 1) * P], self.Wo[:, c, :],
                                  start=(c == 0), stop=(c == NC - 1))
                return x

            def tensor(self, pe):
                L = len(self.lots)
                self.loaded(pe)
                for u in range(UNITS):
                    def transposes(t):
                        n = u * NT + t
                        pe.wait_ge(self.on["parts_ready"].sem, self.on["parts_ready"].at(n + 1))
                        pe.wait_ge(self.on["h_copied"].sem, self.on["h_copied"].at(n + 1))
                        pe.wait_ge(self.on["m_copied"].sem, self.on["m_copied"].at(3 * (n + 1)))
                        for i, (a, k) in enumerate(self.lots):
                            m = n * L + i
                            if m - u * NT * L >= 2:
                                self.wait_qkT(pe, m - 2, 4 + m % 2)
                            tp = PS[:, 4 + m % 2, :].bitcast(BF16)
                            for h in range(k):
                                x = pe.transpose(tp[0:SR, h * P:(h + 1) * P],
                                                 SPL[:, n % 3, a + h, :], identb[:, :])
                            x.then_inc(s16["qkT_psum_ready"].sem, 1)
                    if u:
                        pe.wait_ge(self.on["ctx_ready"].sem, self.on["ctx_ready"].at(u * 4))
                    early = EARLY if u else 0
                    for s in range(NT + 2 - early):
                        t = s + early
                        if t < NT:
                            self.project_qk(pe, u, t, t % 2)
                        if early and s < NT:
                            self.project_v(pe, u, s)
                        elif t < NT:
                            self.project_v(pe, u, t)
                        if t >= 2:
                            transposes(t - 2)
                    self.wait_qkT(pe, (u + 1) * NT * L - 1)
                    pe.wait_ge(self.on["v_ready"].sem, self.on["v_ready"].at((u + 1) * NT))
                    for k in range(NT):
                        i = NT - 1 - k
                        n = (i + 1) * P
                        for g in range(4):
                            m = (u * NT + k) * 4 + g
                            if m - u * 16 >= 2:
                                pe.wait_ge(self.on["max_ready"].sem, self.on["max_ready"].at(m - 1))
                            if k >= 1 and g == 2:
                                self.max_T(pe, u, k - 1)
                            for h in (1, 2, 3, 0):
                                if k >= 1 and g == 2 and h == 0:
                                    pe.wait_ge(self.on["maxT_ready"].sem, self.on["maxT_ready"].at(u * NT + k))
                                head = 4 * g + h
                                ps = PS[:, 4 * (m % 2) + h, 0:n]
                                pe.matmul(ps, QT[0:SR, head, i * P:(i + 1) * P],
                                          KT[0:SR, head // self.rep, 0:n], start=True, stop=False)
                                x = pe.matmul(ps[:, n - P:n], identb[:, :], mask_qk[:, :],
                                              start=False, stop=True)
                            x.then_inc(s16["scores_ready"].sem, 1)
                    if u < UNITS - 1:
                        pe.wait_ge(self.on["max_ready"].sem, self.on["max_ready"].at((u + 1) * NT * 4))
                        self.project_qk(pe, u + 1, 0, 6)
                    self.max_T(pe, u, NT - 1)
                    if u < UNITS - 1:
                        self.project_qk(pe, u + 1, 1, 7)
                    pe.wait_ge(self.on["pads_ready"].sem, self.on["pads_ready"].at(3))
                    pe.wait_ge(self.on["max_rows_loaded"].sem, self.on["max_rows_loaded"].at(16 * (u + 1)))
                    for g in range(5):
                        for h in range(4):
                            if g < 4:
                                n = u * UH + 4 * g + h
                                if 4 * g + h >= 2:
                                    pe.wait_ge(self.on["probs_ready"].sem, self.on["probs_ready"].at(n - 1))
                                head = 4 * g + h
                                s = 3 * (n % 2)
                                flat = PS[:, s:s + 3, :].rearrange("p a b -> p (a b)")
                                for j in range(NT):
                                    w = T - j * P
                                    pe.matmul(flat[:, REGION[j]:REGION[j] + w],
                                              KT[0:SR + MR, head // self.rep, j * P:(j + 1) * P],
                                              QT[0:SR + MR, head, j * P:T], start=True, stop=False)
                                    x = pe.matmul(flat[:, REGION[j]:REGION[j] + P], identb[:, :],
                                                  mask_kq[:, :], start=False, stop=True)
                                x.then_inc(s16["scoresT_ready"].sem, 1)
                            if g >= 1 and h == 1:
                                self.pv(pe, u, g - 1)
                            if g >= 1 and h == 2:
                                self.back(pe, u, g - 1)
                if not self.loop:
                    pe.wait_ge(S_w0o.sem, 16 * 3)
                pe.wait_ge(self.on["ctx_ready"].sem, self.on["ctx_ready"].at(UNITS * 4))
                self.ctx_T(pe, 0)
                self.tail.tensor(pe)

            def project_qk(self, pe, u, t, bank):
                if t >= 2 and not u:
                    pe.wait_ge(self.on["qk_ready"].sem, self.on["qk_ready"].at(t - 1))
                for c in range(NC):
                    x = pe.matmul(PS[:, bank, 0:self.nqk], XT[:, c, t * P:(t + 1) * P],
                                  self.W[:, c, u, 0:self.nqk], start=(c == 0), stop=(c == NC - 1))
                x.then_inc(s16["qk_psum"].sem, 1)

            def project_v(self, pe, u, t):
                if t >= 2:
                    pe.wait_ge(self.on["v_ready"].sem, self.on["v_ready"].at(u * NT + t - 1))
                for c in range(NC):
                    x = pe.matmul(PS[:, 2 + t % 2, 0:self.nv], XT[:, c, t * P:(t + 1) * P],
                                  self.W[:, c, u, self.nqk:self.nqk + self.nv],
                                  start=(c == 0), stop=(c == NC - 1))
                x.then_inc(s16["v_psum"].sem, 1)

            def maxT_psum(self):
                return PS[0:MR * UH, 0, 0:P // 2].bitcast(BF16)

            def max_T(self, pe, u, k):
                pe.wait_ge(self.on["max_parts_ready"].sem, self.on["max_parts_ready"].at(u * NT + k + 1))
                alone(pe)
                pe.transpose(self.maxT_psum(), NM3[:, k % 2, :], identb[:, :])\
                  .then_inc(s16["maxT_psum_ready"].sem, 1)

            def ctx_T(self, pe, t):
                if t >= 2:
                    pe.wait_ge(self.on["ctxT_ready"].sem, self.on["ctxT_ready"].at(t - 1))
                for c in range(NC):
                    x = pe.transpose(PS[:, 4 + t % 2, c * P:(c + 1) * P],
                                     CTX[:, t, c * P:(c + 1) * P], ident[:, :])
                x.then_inc(s16["ctxT_psum_ready"].sem, 1)

            def pv(self, pe, u, g):
                n = u * 4 + g
                pe.wait_ge(self.on["probs_ready"].sem, self.on["probs_ready"].at(u * UH + 4 * g + 4))
                if g >= 1:
                    pe.wait_ge(self.on["outT_ready"].sem, self.on["outT_ready"].at(n))
                for j in range(NT):
                    w = T - j * P
                    for h in range(4):
                        head = 4 * g + h
                        x = pe.matmul(PS[32 * h:32 * h + 32, 6, j * P:T],
                                      VA[:, j, head // self.rep, :],
                                      PB[:, (u * UH + head) % PBS, REGION[j]:REGION[j] + w],
                                      start=(j == 0), stop=(j == NT - 1), tile_position=(0, 32 * h))
                x.then_inc(s16["pv_ready"].sem, 1)

            def back(self, pe, u, g):
                n = u * 4 + g
                pe.wait_ge(self.on["outT_ready"].sem, self.on["outT_ready"].at(n + 1))
                if g >= 1:
                    pe.wait_ge(self.on["ctx_ready"].sem, self.on["ctx_ready"].at(n))
                for t in range(NT):
                    x = pe.transpose(PS[:, 7, t * P:(t + 1) * P], OT[:, t * P:(t + 1) * P], ident[:, :])
                x.then_inc(s16["out_psum_ready"].sem, 1)

            def take_qk(self, dve, st, u, t):
                n = u * NT + t
                NQK = self.nqk
                H = NQK // HD
                dve.wait_ge(self.on["qk_psum"].sem, self.on["qk_psum"].at(n + 1))
                if n >= 3:
                    dve.wait_ge(self.on["qkT_psum_ready"].sem, self.on["qkT_psum_ready"].at((n - 2) * len(self.lots)))
                src = PS[:, 6 + t if u and t < EARLY else t % 2, 0:NQK]
                if self.bias is not None:
                    dve.tensor_tensor(QK[:, 0:NQK], src, self.bias[:, u, 0:NQK], ALU.add)\
                       .then_inc(s16["qk_ready"].sem, 1)
                else:
                    dve.tensor_copy(QK[:, 0:NQK], src).then_inc(s16["qk_ready"].sem, 1)
                dve.wait_ge(self.on["qk_ready"].sem, self.on["qk_ready"].at(n + 1))
                qk = QK[:, 0:NQK].rearrange("p (h e) -> p h e", e=HD)
                if self.rope is not None:
                    cos, sin = self.rope
                    r1 = R1[:, 0:NQK].rearrange("p (h e) -> p h e", e=HD)
                    rt = RT[:, 0:NQK].rearrange("p (h e) -> p h e", e=HD)
                    hh = HD // 2
                    bc = lambda a, w: a.unsqueeze(1).to_broadcast([P, H, w])
                    st.done(dve.tensor_tensor(r1, qk, bc(cos[:, t, :], HD), ALU.mult))
                    st.done(dve.tensor_tensor(rt[:, :, 0:hh], qk[:, :, hh:HD],
                                              bc(sin[:, t, 0:hh], hh), ALU.mult))
                    st.link(dve.tensor_tensor(rt[:, :, hh:HD], qk[:, :, 0:hh],
                                              bc(sin[:, t, hh:HD], hh), ALU.mult))
                    st.link(dve.tensor_tensor(qk, r1, rt, ALU.add))
                sp = SPL[:, n % 3, 0:H, :].rearrange("p h (s e) -> p h s e", e=HD)
                r1 = R1[:, 0:NQK].rearrange("p (h e) -> p h e", e=HD)
                dve.tensor_copy(sp[:, :, 2, :], qk).then_inc(s16["h_ready"].sem, 1)
                dve.wait_ge(self.on["h_ready"].sem, self.on["h_ready"].at(n + 1))
                st.link(dve.tensor_tensor(r1, qk, sp[:, :, 2, :], ALU.subtract))
                dve.tensor_copy(sp[:, :, 5, :], r1).then_inc(s16["m_ready"].sem, 1)
                dve.wait_ge(self.on["m_ready"].sem, self.on["m_ready"].at(n + 1))
                st.done(dve.tensor_tensor(sp[:, 0:UH, 3, :], r1[:, 0:UH, :],
                                          sp[:, 0:UH, 5, :], ALU.subtract))
                dve.tensor_tensor(sp[:, UH:H, 0, :], r1[:, UH:H, :],
                                  sp[:, UH:H, 5, :], ALU.subtract)\
                   .then_inc(s16["parts_ready"].sem, 1)
                dve.wait_ge(self.on["parts_ready"].sem, self.on["parts_ready"].at(n + 1))
                st.wait()

            def take_v(self, dve, u, t):
                n = u * NT + t
                dve.wait_ge(self.on["v_psum"].sem, self.on["v_psum"].at(n + 1))
                if u and t == 0:
                    dve.wait_ge(self.on["pv_ready"].sem, self.on["pv_ready"].at(4 * u))
                v = PS[:, 2 + t % 2, 0:self.nv].rearrange("p (h e) -> p h e", e=HD)
                va = VA[:, t, 0:self.nk, 0:HD]
                if self.bias is not None:
                    dve.tensor_tensor(va, v, self.bias[:, u, self.nqk:self.nqk + self.nv]
                                      .rearrange("p (h e) -> p h e", e=HD), ALU.add)\
                       .then_inc(s16["v_ready"].sem, 1)
                else:
                    dve.tensor_copy(va, v).then_inc(s16["v_ready"].sem, 1)

            def vector(self, dve, st):
                if self.bias_loaded:
                    self.bias_loaded(dve)
                for u in range(UNITS):
                    early = EARLY if u else 0
                    for s in range(NT):
                        if s + early < NT:
                            self.take_qk(dve, st, u, s + early)
                        self.take_v(dve, u, s)
                        if u and s == 2:
                            dve.wait_ge(self.on["scoresT_ready"].sem, self.on["scoresT_ready"].at(u * UH))
                        for t in [s] if early else [2, 3] if s == NT - 1 else []:
                            for m in range((u * NT + t) * len(self.lots), (u * NT + t + 1) * len(self.lots)):
                                if self.by_vector(m):
                                    self.take_qkT(dve, dve.tensor_copy, m)\
                                        .then_inc(s16["qkT_ready_v"].sem, 1)
                    for k in range(NT):
                        n = (NT - k) * P
                        if k >= 2:
                            dve.wait_ge(self.on["max_parts_ready"].sem, self.on["max_parts_ready"].at(u * NT + k - 1))
                        elif u:
                            dve.wait_ge(self.on["max_parts_ready"].sem, self.on["max_parts_ready"].at(u * NT))
                        for g in range(4):
                            m = (u * NT + k) * 4 + g
                            dve.wait_ge(self.on["scores_ready"].sem, self.on["scores_ready"].at(m + 1))
                            dve.tensor_reduce(NM[:, k % 2, 4 * g:4 * g + 4],
                                              PS[:, 4 * (m % 2):4 * (m % 2) + 4, 0:n], AX.X, ALU.max,
                                              negate=True).then_inc(s16["max_ready"].sem, 1)
                    for t in range(EARLY if u < UNITS - 1 else 0):
                        self.take_qk(dve, st, u + 1, t)
                    for g in range(4):
                        n = u * 4 + g
                        dve.wait_ge(self.on["pv_ready"].sem, self.on["pv_ready"].at(n + 1))
                        if n >= 1:
                            dve.wait_ge(self.on["out_psum_ready"].sem, self.on["out_psum_ready"].at(n))
                        dve.tensor_copy(OT[:, :], PS[:, 6, :]).then_inc(s16["outT_ready"].sem, 1)
                        dve.wait_ge(self.on["out_psum_ready"].sem, self.on["out_psum_ready"].at(n + 1))
                        o = PS[:, 7, :].rearrange("p (t h e) -> p t h e", t=NT, h=4)
                        st.link(dve.reciprocal(RC[:, :, :], o[:, :, :, HD]))
                        c = CTX[:, :, u * 256 + g * 64:u * 256 + g * 64 + 64]
                        dve.tensor_tensor(c.rearrange("p t (h e) -> p t h e", e=HD), o[:, :, :, 0:HD],
                                          RC[:, :, :].unsqueeze(3).to_broadcast([P, NT, 4, HD]), ALU.mult)\
                           .then_inc(s16["ctx_ready"].sem, 1)
                if not self.loop:
                    dve.wait_ge(S_x.sem, S_x.at(16))
                self.tail.vector(dve, st)

            def copy_m(self, pool, n):
                pool.wait_ge(self.on["h_ready"].sem, self.on["h_ready"].at(n + 1))
                H = self.nqk // HD
                sp = SPL[:, n % 3, 0:H, :].rearrange("p h (s e) -> p h s e", e=HD)
                alone(pool)
                pool.tensor_copy(sp[:, 0:UH, 0:2, :], sp[:, 0:UH, 2:3, :].to_broadcast([P, UH, 2, HD]))\
                    .then_inc(s16["m_copied"].sem, 1)
                pool.wait_ge(self.on["m_ready"].sem, self.on["m_ready"].at(n + 1))
                alone(pool)
                pool.tensor_copy(sp[:, 0:UH, 4, :], sp[:, 0:UH, 5, :]).then_inc(s16["m_copied"].sem, 1)
                pool.tensor_copy(sp[:, UH:H, 1, :], sp[:, UH:H, 5, :]).then_inc(s16["m_copied"].sem, 1)

            def split_max(self, pool, n):
                pool.wait_ge(self.on["max_ready"].sem, self.on["max_ready"].at(4 * (n + 1)))
                if n >= 2:
                    pool.wait_ge(self.on["maxT_psum_ready"].sem, self.on["maxT_psum_ready"].at(n - 1))
                nm, n3 = NM[:, n % 2, :], NM3[:, n % 2, :].rearrange("p (s h) -> p s h", s=MR)
                alone(pool)
                pool.tensor_copy(n3[:, 0, :], nm).then_inc(s16["max_step"].sem, 1)
                pool.wait_ge(self.on["max_step"].sem, self.on["max_step"].at(3 * n + 1))
                pool.tensor_tensor(NMR[:, :], nm, n3[:, 0, :], ALU.subtract).then_inc(s16["max_step"].sem, 1)
                pool.wait_ge(self.on["max_step"].sem, self.on["max_step"].at(3 * n + 2))
                alone(pool)
                pool.tensor_copy(n3[:, 1, :], NMR[:, :]).then_inc(s16["max_step"].sem, 1)
                pool.wait_ge(self.on["max_step"].sem, self.on["max_step"].at(3 * n + 3))
                pool.tensor_tensor(n3[:, 2, :], NMR[:, :], n3[:, 1, :], ALU.subtract)\
                    .then_inc(s16["max_parts_ready"].sem, 1)
                pool.wait_ge(self.on["max_parts_ready"].sem, self.on["max_parts_ready"].at(n + 1))

            def gpsimd(self, pool):
                alone(pool)
                pool.memset(VA[:, :, :, HD + 1:32], 0.0).then_inc(s16["pads_ready"].sem, 1)
                pool.memset(VA[:, :, :, HD:HD + 1], 1.0).then_inc(s16["pads_ready"].sem, 1)
                pool.wait_ge(self.on["pads_ready"].sem, self.on["pads_ready"].at(2))
                alone(pool)
                pool.memset(KT[SR:SR + MR, 0:self.nk, :], 1.0).then_inc(s16["pads_ready"].sem, 1)
                pool.wait_ge(self.on["pads_ready"].sem, self.on["pads_ready"].at(3))
                for u in range(UNITS):
                    for t in range(EARLY if u else 0, NT):
                        self.copy_m(pool, u * NT + t)
                    for k in range(NT):
                        self.split_max(pool, u * NT + k)
                    for t in range(EARLY if u < UNITS - 1 else 0):
                        self.copy_m(pool, (u + 1) * NT + t)
                self.tail.gpsimd(pool)

            def copy_h(self, act, n):
                act.wait_ge(self.on["h_ready"].sem, self.on["h_ready"].at(n + 1))
                H = self.nqk // HD
                sp = SPL[:, n % 3, 0:H, :].rearrange("p h (s e) -> p h s e", e=HD)
                act.copy(sp[:, UH:H, 3:5, :], sp[:, UH:H, 2:3, :].to_broadcast([P, H - UH, 2, HD]))\
                   .then_inc(s16["h_copied"].sem, 1)

            def scalar(self, act):
                L = len(self.lots)
                for u in range(UNITS):
                    for t in range(EARLY if u else 0, NT + 2):
                        if t < NT:
                            self.copy_h(act, u * NT + t)
                        if t == 2 and u:
                            act.wait_ge(self.on["scoresT_ready"].sem, self.on["scoresT_ready"].at(u * UH))
                        for i in range(L if t >= 2 else 0):
                            m = (u * NT + t - 2) * L + i
                            if not self.by_vector(m):
                                self.take_qkT(act, act.copy, m).then_inc(s16["qkT_ready"].sem, 1)
                    for k in range(NT):
                        i = NT - 1 - k
                        act.wait_ge(self.on["maxT_psum_ready"].sem, self.on["maxT_psum_ready"].at(u * NT + k + 1))
                        act.copy(NMT[:, i * P:(i + 1) * P], self.maxT_psum())\
                           .then_inc(s16["maxT_ready"].sem, 1)
                    act.wait_ge(self.on["maxT_ready"].sem, self.on["maxT_ready"].at((u + 1) * NT))
                    act.dma_start(QT[SR:SR + MR, :, :], NMT[:, :])\
                       .then_inc(s16["max_rows_loaded"].sem, 16)
                    for t in range(EARLY if u < UNITS - 1 else 0):
                        self.copy_h(act, (u + 1) * NT + t)
                    for n in range(UH):
                        m = u * UH + n
                        act.wait_ge(self.on["scoresT_ready"].sem, self.on["scoresT_ready"].at(m + 1))
                        if n >= PBS:
                            act.wait_ge(self.on["pv_ready"].sem, self.on["pv_ready"].at(u * 4 + (n - PBS) // 4 + 1))
                        s = 3 * (m % 2)
                        act.activation(PB[:, m % PBS, :],
                                       PS[:, s:s + 3, :].rearrange("p a b -> p (a b)")[:, 0:SCOLS],
                                       ACT.Exp, scale=self.scale).then_inc(s16["probs_ready"].sem, 1)
                for t in range(NT):
                    act.wait_ge(self.on["ctxT_psum_ready"].sem, self.on["ctxT_psum_ready"].at(t + 1))
                    if t >= 2:
                        act.wait_ge(self.tail.s_y.sem, self.tail.s_y.at(t - 1))
                    act.copy(CT[:, t % 2, :], PS[:, 4 + t % 2, :]).then_inc(s16["ctxT_ready"].sem, 1)
                self.tail.scalar(act)

        F0 = ExitStack()
        QF = sb("QF", [64, T], F32, F0)
        GEL = sb("GEL", [P, T], F32, F0)
        RKT = sb("RKT", [48, P], F32, F0)
        G = sb("G", [64, 2 * P], F32, F0)
        AVT = sb("AVT", [32, P], F32, F0)
        PT0 = sb("PT0", [P, D], F32, F0)
        RS = sb("RS", [P, NT, 2 * P], F32, F0)
        MRP = sb("MRP", [P, NT, P], F32, F0)
        M8 = sb("M8", [P, NT, 8], F32, F0)
        EX = sb("EX", [P, NT, P], F32, F0)
        W0T = sb("W0T", [P, T], F32, F0)
        GA = sb("GA", [P, 12, NT], F32, F0)
        F0.close()
        f0 = {k: sig("f0_" + k, 0, n) for k, n in dict(
            q_psum=1, q_ready=1, u_psum=1, gelu_ready=1, rk_psum=1, rk_ready=1, g_psum=1, g_ready=1,
            av_psum=1, av_ready=1, p_psum=1, p_ready=1, r_psum=1, learned_psum=1, logvar_psum=1,
            masked_ready=1, exp_ready=1, learned=1, gate_arg=1, gate=1, weights_ready=1,
            wT_psum=1, wT_ready=1).items()}
        c0 = WC[:, :]
        f0_Wq = c0[:, 0:256].rearrange("p (c n) -> p c n", c=NC)
        f0_Wu1 = c0[:, 256:768].rearrange("p (c n) -> p c n", c=NC)
        f0_Wvd = c0[:, 768:896].rearrange("p (c n) -> p c n", c=NC)
        f0_avT = c0[:, 896:1408].rearrange("p (c n) -> p c n", c=NC)
        f0_Wr = c0[0:48, 1408:1472]
        f0_WrT = c0[0:64, 1472:1520]
        f0_keysT = c0[0:64, 1520:1648]
        f0_WvuT = c0[0:32, 1648:2160]
        f0_lr = c0[:, 2160:2288]
        f0_bu1, f0_Wu2, f0_bu2, f0_gw, f0_gb = [c0[:, 2288 + i:2289 + i] for i in range(5)]

        class Ffn0(Stage):
            def __init__(self, loop):
                self.tail = Tail(loop, self.y_tile, times=2.0)

            def y_tile(self, pe, t, ps):
                return pe.matmul(ps, W0T[:, t * P:(t + 1) * P], PT0[:, :], start=True, stop=True)

            def tensor(self, pe):
                pe.wait_ge(S_wc.sem, S_wc.at(W_C[0]))
                def mms(ps, pairs, s):
                    for i, (a, b) in enumerate(pairs):
                        x = pe.matmul(ps, a, b, start=(i == 0), stop=(i == len(pairs) - 1))
                    x.then_inc(f0[s].sem, 1)
                mms(PS[0:64, 0, :], [(f0_Wq[:, c, :], XT[:, c, :]) for c in range(NC)], "q_psum")
                mms(PS[:, 1, :], [(f0_Wu1[:, c, :], XT[:, c, :]) for c in range(NC)], "u_psum")
                mms(PS[0:48, 2, 0:P], [(f0_WrT, f0_keysT)], "rk_psum")
                mms(PS[0:32, 3, 0:P], [(f0_Wvd[:, c, :], f0_avT[:, c, :]) for c in range(NC)], "av_psum")
                pe.wait_ge(f0["rk_ready"].sem, f0["rk_ready"].at(1))
                alone(pe)
                mms(PS[0:64, 2, 0:P], [(f0_Wr, RKT[:, :])], "g_psum")
                pe.wait_ge(f0["av_ready"].sem, f0["av_ready"].at(1))
                mms(PS[:, 3, :], [(AVT[:, :], f0_WvuT)], "p_psum")
                mms(PS[:, 7, 0:NB * NT], [(ones[:, :], LV[:, 0:NB * NT])], "logvar_psum")
                pe.wait_ge(f0["g_ready"].sem, f0["g_ready"].at(1))
                pe.wait_ge(f0["q_ready"].sem, f0["q_ready"].at(1))
                for t in range(NT):
                    x = pe.matmul(PS[:, 4 + t // 2, 256 * (t % 2):256 * (t % 2) + 256],
                                  QF[:, t * P:(t + 1) * P], G[:, :], start=True, stop=True)
                x.then_inc(f0["r_psum"].sem, 1)
                pe.wait_ge(f0["gelu_ready"].sem, f0["gelu_ready"].at(1))
                for t in range(NT):
                    x = pe.matmul(PS[:, 6, t:t + 1], GEL[:, t * P:(t + 1) * P], f0_Wu2,
                                  start=True, stop=True)
                x.then_inc(f0["learned_psum"].sem, 1)
                pe.wait_ge(f0["weights_ready"].sem, f0["weights_ready"].at(1))
                for t in range(NT):
                    x = pe.transpose(PS[:, 4, t * P:(t + 1) * P], EX[:, t, :], ident[:, :])
                x.then_inc(f0["wT_psum"].sem, 1)
                pe.wait_ge(f0["wT_ready"].sem, f0["wT_ready"].at(1))
                pe.wait_ge(f0["p_ready"].sem, f0["p_ready"].at(1))
                self.tail.tensor(pe)

            def scalar(self, act):
                act.wait_ge(f0["u_psum"].sem, f0["u_psum"].at(1))
                act.activation(GEL[:, :], PS[:, 1, :], ACT.Gelu_apprx_tanh, bias=f0_bu1)\
                   .then_inc(f0["gelu_ready"].sem, 1)
                act.wait_ge(f0["masked_ready"].sem, f0["masked_ready"].at(1))
                act.activation(EX[:, :, :], MRP[:, :, :], ACT.Exp).then_inc(f0["exp_ready"].sem, 1)
                act.wait_ge(f0["learned_psum"].sem, f0["learned_psum"].at(1))
                act.activation(GA[:, 3, :], PS[:, 6, 0:NT], ACT.Sigmoid, bias=f0_bu2)\
                   .then_inc(f0["learned"].sem, 1)
                act.wait_ge(f0["gate_arg"].sem, f0["gate_arg"].at(1))
                act.activation(GA[:, 7, :], GA[:, 5, :], ACT.Sigmoid).then_inc(f0["gate"].sem, 1)
                act.wait_ge(f0["wT_psum"].sem, f0["wT_psum"].at(1))
                act.copy(W0T[:, :], PS[:, 4, :]).then_inc(f0["wT_ready"].sem, 1)
                self.tail.scalar(act)

            def gpsimd(self, pool):
                self.tail.gpsimd(pool)

            def vector(self, dve, st):
                dve.wait_ge(S_wc.sem, S_wc.at(W_C[0]))
                dve.wait_ge(f0["rk_psum"].sem, f0["rk_psum"].at(1))
                dve.tensor_copy(RKT[:, :], PS[0:48, 2, 0:P]).then_inc(f0["rk_ready"].sem, 1)
                dve.wait_ge(f0["av_psum"].sem, f0["av_psum"].at(1))
                dve.tensor_copy(AVT[:, :], PS[0:32, 3, 0:P]).then_inc(f0["av_ready"].sem, 1)
                dve.wait_ge(f0["q_psum"].sem, f0["q_psum"].at(1))
                dve.tensor_copy(QF[:, :], PS[0:64, 0, :]).then_inc(f0["q_ready"].sem, 1)
                dve.wait_ge(f0["g_psum"].sem, f0["g_psum"].at(1))
                st.done(dve.tensor_scalar(G[:, 0:P], PS[0:64, 2, 0:P], 1.0 / np.sqrt(48.0), None, ALU.mult))
                dve.tensor_scalar(G[:, P:2 * P], f0_keysT, 0.125, None, ALU.mult)\
                   .then_inc(f0["g_ready"].sem, 1)
                dve.wait_ge(f0["p_psum"].sem, f0["p_psum"].at(1))
                dve.tensor_copy(PT0[:, :], PS[:, 3, :]).then_inc(f0["p_ready"].sem, 1)
                dve.wait_ge(f0["logvar_psum"].sem, f0["logvar_psum"].at(1))
                st.link(dve.tensor_reduce(GA[:, 8, 0:1], PS[:, 7, 0:NB * NT], AX.X, ALU.add))
                st.link(dve.tensor_scalar(GA[:, 8, 1:2], GA[:, 8, 0:1], 1.0 / (NB * T), 1e-6,
                                          ALU.mult, ALU.add))
                st.link(dve.reciprocal(GA[:, 8, 2:3], GA[:, 8, 1:2]))
                st.link(dve.tensor_scalar(GA[:, 9, :], LV[:, :].rearrange("p (b t) -> p b t", t=NT)
                                          [:, Signal.batch + NB - 1, :], GA[:, 8, 2:3], 0.5, ALU.mult, ALU.mult))
                dve.wait_ge(f0["r_psum"].sem, f0["r_psum"].at(1))
                rps = PS[:, 4:6, :].rearrange("p a (s h n) -> p (a s) h n", s=2, h=2)
                rs = RS[:, :, :].rearrange("p t (h n) -> p t h n", h=2)
                for h in range(2):
                    st.done(dve.tensor_tensor(rs[:, :, h, :], rps[:, :, h, :],
                                              f0_lr.unsqueeze(1).to_broadcast([P, NT, P]), ALU.add))
                st.wait()
                alone(dve)
                for t in range(NT):
                    st.done(dve.max(M8[:, t, :], RS[:, t, 0:P]))
                st.wait()
                alone(dve)
                for t in range(NT):
                    st.done(dve.match_replace(MRP[:, t, :], M8[:, t, :], RS[:, t, 0:P], TAKEN))
                st.wait()
                st.link(dve.tensor_scalar(MRP[:, :, :], MRP[:, :, :], TAKEN, 1.0, ALU.is_equal, ALU.subtract))
                st.link(dve.scalar_tensor_tensor(MRP[:, :, :], MRP[:, :, :], -MASKED, RS[:, :, P:2 * P],
                                                 ALU.mult, ALU.add))
                st.link(dve.tensor_reduce(GA[:, 10, :], MRP[:, :, :], AX.X, ALU.max))
                dve.tensor_tensor(MRP[:, :, :], MRP[:, :, :],
                                  GA[:, 10, :].unsqueeze(2).to_broadcast([P, NT, P]), ALU.subtract)\
                   .then_inc(f0["masked_ready"].sem, 1)
                dve.wait_ge(f0["learned"].sem, f0["learned"].at(1))
                st.link(dve.scalar_tensor_tensor(GA[:, 4, :], GA[:, 3, :], 2.5, GA[:, 9, :], ALU.mult, ALU.add))
                st.link(dve.tensor_scalar(GA[:, 4, :], GA[:, 4, :], 0.0, 5.0, ALU.max, ALU.min))
                st.link(dve.tensor_scalar(GA[:, 4, :], GA[:, 4, :], 0.5, 1.0 / 1.5, ALU.subtract, ALU.mult))
                st.link(dve.tensor_scalar(GA[:, 4, :], GA[:, 4, :], 0.0, 1.0, ALU.max, ALU.min))
                dve.tensor_scalar(GA[:, 5, :], GA[:, 4, :], f0_gw, f0_gb, ALU.mult, ALU.add)\
                   .then_inc(f0["gate_arg"].sem, 1)
                dve.wait_ge(f0["gate"].sem, f0["gate"].at(1))
                st.link(dve.tensor_scalar(GA[:, 11, :], GA[:, 7, :], 0.05, None, ALU.is_ge))
                st.link(dve.tensor_tensor(GA[:, 7, :], GA[:, 7, :], GA[:, 11, :], ALU.mult))
                dve.wait_ge(f0["exp_ready"].sem, f0["exp_ready"].at(1))
                st.link(dve.tensor_reduce(GA[:, 2, :], EX[:, :, :], AX.X, ALU.add))
                st.link(dve.reciprocal(GA[:, 2, :], GA[:, 2, :]))
                st.link(dve.tensor_tensor(GA[:, 2, :], GA[:, 2, :], GA[:, 7, :], ALU.mult))
                dve.tensor_tensor(EX[:, :, :], EX[:, :, :],
                                  GA[:, 2, :].unsqueeze(2).to_broadcast([P, NT, P]), ALU.mult)\
                   .then_inc(f0["weights_ready"].sem, 1)
                self.tail.vector(dve, st)

        NG = 8
        ev1 = dict(a_loaded=16, b_loaded=16, wo_loaded=16, a_hi=1, a_lo=1, b_hi=1, b_lo=1, wo_hi=1, wo_lo=1,
                   oT_hi=4, k_psum=1, v_psum=1, q_psum=4, k_read=1, q_read=4,
                   v_ready=1, k_rope=1, q_rope=4, scores=16, negmax=16, exp=16, recip=16, norm=16,
                   pT_psum=16, pT=16, pv=4, oT=4, y=4, added=4)
        s1 = {k: sigs.setdefault("l1_" + k, GroupSignal(ctx.enter_context(nc.semaphore("l1_" + k)), k, NG, n))
              for k, n in ev1.items()}
        s1_tab = sig("l1_tab_loaded", 0, 16)
        s1_xh, s1_xl = sig("l1_x_hi", 0, NC), sig("l1_x_lo", 0, NC)
        A1 = WB[:, 0:1536].rearrange("p (c n) -> p c n", c=NC)
        B1 = WB[:, 1536:3072].rearrange("p (c n) -> p c n", c=NC)
        Wo1 = WB[:, 3072:5120].rearrange("p (h n) -> p h n", h=GQ)
        OFF = [0, 128, 384, 768]

        class Attention1(Stage):

            def __init__(self, loop):
                self.tail = Tail(loop)

            def project(self, pe, bank, high, low, s):
                for c in range(NC):
                    pairs = ((high, XH1), (low, XH1), (high, XL1))
                    for i, (w, x) in enumerate(pairs):
                        x = pe.matmul(PS[:, bank, :], w[:, c, :], x[:, c, :],
                                      start=(c == 0 and i == 0), stop=(c == NC - 1 and i == 2))
                    if c == NC - 1:
                        x.then_inc(s1[s].sem, 1)
                    yield

            def project_k(self, pe, g, first):
                pe.wait_ge(s1["a_hi"].sem, s1["a_hi"].at(1, g))
                pe.wait_ge(s1["a_lo"].sem, s1["a_lo"].at(1, g))
                if not first:
                    pe.wait_ge(s1["q_read"].sem, s1["q_read"].at(0, g))
                return self.project(pe, 0, A1H[:, :, P:2 * P], A1L[:, :, P:2 * P], "k_psum")

            def project_q(self, pe, g, h, first):
                if h == 0 and not first:
                    pe.wait_ge(s1["q_read"].sem, s1["q_read"].at(-1, g))
                if h == 1:
                    pe.wait_ge(s1["b_hi"].sem, s1["b_hi"].at(1, g))
                    pe.wait_ge(s1["b_lo"].sem, s1["b_lo"].at(1, g))
                    pe.wait_ge(s1["k_read"].sem, s1["k_read"].at(1, g))
                if h >= 2:
                    pe.wait_ge(s1["q_read"].sem, s1["q_read"].at(h - 1, g))
                if h == 0:
                    high, low = A1H[:, :, 0:P], A1L[:, :, 0:P]
                else:
                    high, low = B1H[:, :, (h - 1) * P:h * P], B1L[:, :, (h - 1) * P:h * P]
                return self.project(pe, 1 - h % 2, high, low, "q_psum")

            def project_v(self, pe, g, first):
                if not first:
                    pe.wait_ge(s1["added"].sem, s1["added"].at(-4, g))
                for t in range(NT):
                    for c in range(NC):
                        x = pe.matmul(PS[:, 7, t * P:(t + 1) * P], XT[:, c, t * P:(t + 1) * P],
                                      A1[:, c, 256:384], start=(c == 0), stop=(c == NC - 1))
                x.then_inc(s1["v_psum"].sem, 1)

            def transpose_probs(self, pe, g, h, i, first):
                m = 4 * h + i
                pe.wait_ge(s1["norm"].sem, s1["norm"].at(m + 1, g))
                if m >= 2 or not first:
                    pe.wait_ge(s1["pT"].sem, s1["pT"].at(m - 1, g))
                t = NT - 1 - i
                for j in range(t + 1):
                    x = pe.transpose(PS[:, 4 + i % 2, j * P:(j + 1) * P],
                                     PR[:, h % 2, OFF[t] + j * P:OFF[t] + (j + 1) * P], ident[:, :])
                x.then_inc(s1["pT_psum"].sem, 1)

            def weighted(self, pe, g, h, first):
                if h == 0:
                    pe.wait_ge(s1["v_ready"].sem, s1["v_ready"].at(1, g))
                    if not first:
                        pe.wait_ge(s1["added"].sem, s1["added"].at(-1, g))
                else:
                    pe.wait_ge(s1["oT"].sem, s1["oT"].at(h, g))
                pe.wait_ge(s1["pT"].sem, s1["pT"].at(4 * h + 4, g))
                for j in range(NT):
                    x = pe.matmul(PS[:, 6, j * P:T], V1[:, j, :], PRT[:, h % 2, j, j * P:T],
                                  start=(j == 0), stop=(j == NT - 1))
                x.then_inc(s1["pv"].sem, 1)

            def output(self, pe, g, last):
                pe.wait_ge(s1["wo_hi"].sem, s1["wo_hi"].at(1, g))
                pe.wait_ge(s1["wo_lo"].sem, s1["wo_lo"].at(1, g))
                pe.wait_ge(s1["oT"].sem, s1["oT"].at(GQ, g))
                if not last:
                    pe.wait_ge(s1["v_ready"].sem, s1["v_ready"].at(1, g + 1))
                for t in range(NT):
                    if t >= 2:
                        pe.wait_ge(s1["added"].sem, s1["added"].at(t - 1, g))
                    for h in range(GQ):
                        for i, (o, w) in enumerate(((OTH, Wo1H), (OTL, Wo1H), (OTH, Wo1L))):
                            x = pe.matmul(PS[:, 6 + t % 2, :], o[:, h, t * P:(t + 1) * P], w[:, h, :],
                                          start=(h == 0 and i == 0), stop=(h == GQ - 1 and i == 2))
                    x.then_inc(s1["y"].sem, 1)

            def tensor_group(self, pe, g, first, last):
                for h in range(GQ):
                    q = self.project_q(pe, g, h + 1, first) if h < GQ - 1 else \
                        iter(()) if last else self.project_k(pe, g + 1, False)
                    if h == 0:
                        pe.wait_ge(s1["k_rope"].sem, s1["k_rope"].at(1, g))
                    pe.wait_ge(s1["q_rope"].sem, s1["q_rope"].at(h + 1, g))
                    for i in range(NT):
                        m = 4 * h + i
                        if m >= 2 or not first:
                            pe.wait_ge(s1["exp"].sem, s1["exp"].at(m - 1, g))
                        n = (NT - i) * P
                        ps = PS[:, 2 + i % 2, 0:n]
                        pe.matmul(ps, qT[:, h % 2, n - P:n], kT[:, 0:n], start=True, stop=False)
                        pe.matmul(ps[:, n - P:n], identb[:, :], mask_qk[:, :], start=False, stop=True)\
                          .then_inc(s1["scores"].sem, 1)
                        if h >= 1:
                            self.transpose_probs(pe, g, h - 1, i, first)
                        elif not first:
                            self.transpose_probs(pe, g - 1, GQ - 1, i, False)
                        next(q, None)
                    if h == 1 and not first:
                        self.output(pe, g - 1, False)
                    if h >= 1:
                        self.weighted(pe, g, h - 1, first)
                    elif not first:
                        self.weighted(pe, g - 1, GQ - 1, False)
                    if h == GQ - 1 and not last:
                        for _ in self.project_q(pe, g + 1, 0, False):
                            pass
                        self.project_v(pe, g + 1, first)

            def tensor(self, pe):
                pe.wait_ge(s1_xh.sem, s1_xh.at(NC))
                pe.wait_ge(s1_xl.sem, s1_xl.at(NC))
                for _ in self.project_k(pe, 0, True):
                    pass
                for _ in self.project_q(pe, 0, 0, True):
                    pass
                self.project_v(pe, 0, True)
                self.tensor_group(pe, 0, True, False)
                with pe.Fori(1, NG - 1) as g:
                    self.tensor_group(pe, g, False, False)
                self.tensor_group(pe, NG - 1, False, True)
                for i in range(NT):
                    self.transpose_probs(pe, NG - 1, GQ - 1, i, False)
                self.weighted(pe, NG - 1, GQ - 1, False)
                self.output(pe, NG - 1, True)
                self.tail.tensor(pe)

            def rope_products(self, dve, bank, slot, c, s):
                ps = PS[:, bank, :]
                dve.tensor_tensor(RA[:, slot, :], ps, TAB[:, c, :], ALU.mult)
                dve.tensor_tensor(RB[0:64, slot, :], ps[64:128], TAB[64:128, c + 1, :], ALU.mult)
                dve.tensor_tensor(RB[64:128, slot, :], ps[0:64], TAB[0:64, c + 1, :], ALU.mult)\
                   .then_inc(s1[s].sem, 1)

            def rope_k(self, dve, g, first):
                dve.wait_ge(s1["k_psum"].sem, s1["k_psum"].at(1, g))
                if not first:
                    dve.wait_ge(s1["q_rope"].sem, s1["q_rope"].at(0, g))
                self.rope_products(dve, 0, 0, 2, "k_read")

            def rope_q(self, dve, g, h, first):
                dve.wait_ge(s1["q_psum"].sem, s1["q_psum"].at(h + 1, g))
                if h == 1:
                    dve.wait_ge(s1["k_rope"].sem, s1["k_rope"].at(1, g))
                elif h or not first:
                    dve.wait_ge(s1["q_rope"].sem, s1["q_rope"].at(h - 1, g))
                self.rope_products(dve, 1 - h % 2, 1 - h % 2, 0, "q_read")

            def take_v(self, dve, g, first):
                dve.wait_ge(s1["v_psum"].sem, s1["v_psum"].at(1, g))
                if not first:
                    dve.wait_ge(s1["pv"].sem, s1["pv"].at(0, g))
                dve.tensor_copy(V1[:, :, :], PS[:, 7, :].rearrange("p (t n) -> p t n", t=NT))\
                   .then_inc(s1["v_ready"].sem, 1)

            def take_o(self, dve, g, h):
                dve.wait_ge(s1["pv"].sem, s1["pv"].at(h + 1, g))
                dve.tensor_copy(OTH[:, h, :], PS[:, 6, :]).then_inc(s1["oT_hi"].sem, 1)
                dve.wait_ge(s1["oT_hi"].sem, s1["oT_hi"].at(h + 1, g))
                dve.tensor_tensor(OTL[:, h, :], PS[:, 6, :], OTH[:, h, :].bitcast(F32), ALU.subtract)\
                   .then_inc(s1["oT"].sem, 1)

            def add(self, dve, g):
                for t in range(NT):
                    dve.wait_ge(s1["y"].sem, s1["y"].at(t + 1, g))
                    dve.tensor_tensor(XB[:, t, :], PS[:, 6 + t % 2, :], XB[:, t, :], ALU.add)\
                       .then_inc(s1["added"].sem, 1)

            def recip(self, dve, g, m):
                dve.wait_ge(s1["exp"].sem, s1["exp"].at(m + 1, g))
                h, i = m // 4, m % 4
                dve.reciprocal(RCP[:, h % 2, i:i + 1], SM[:, h % 2, i:i + 1]).then_inc(s1["recip"].sem, 1)

            def vector_group(self, dve, g, first, last):
                for h in range(GQ):
                    for i in range(NT):
                        m = 4 * h + i
                        dve.wait_ge(s1["scores"].sem, s1["scores"].at(m + 1, g))
                        dve.tensor_reduce(NX[:, h % 2, i:i + 1], PS[:, 2 + i % 2, 0:(NT - i) * P],
                                          AX.X, ALU.max, negate=True).then_inc(s1["negmax"].sem, 1)
                        if i >= 1:
                            self.recip(dve, g, m - 1)
                    self.recip(dve, g, 4 * h + 3)
                    if h < GQ - 1:
                        self.rope_q(dve, g, h + 1, first)
                    elif not last:
                        self.rope_k(dve, g + 1, False)
                    if h == 1 and not first:
                        self.add(dve, g - 1)
                    if h >= 1:
                        self.take_o(dve, g, h - 1)
                    elif not first:
                        self.take_o(dve, g - 1, GQ - 1)
                        self.take_v(dve, g, False)
                    if h == GQ - 1 and not last:
                        self.rope_q(dve, g + 1, 0, False)

            def vector(self, dve, st):
                for c in range(NC):
                    dve.tensor_copy(XH1[:, c, :], XT[:, c, :]).then_inc(s1_xh.sem, 1)
                for c in range(NC):
                    dve.wait_ge(s1_xh.sem, s1_xh.at(c + 1))
                    dve.tensor_tensor(XL1[:, c, :], XT[:, c, :], XH1[:, c, :].bitcast(F32), ALU.subtract)\
                       .then_inc(s1_xl.sem, 1)
                dve.wait_ge(s1_tab.sem, s1_tab.at(16))
                self.rope_k(dve, 0, True)
                self.rope_q(dve, 0, 0, True)
                self.take_v(dve, 0, True)
                self.vector_group(dve, 0, True, False)
                with dve.Fori(1, NG - 1) as g:
                    self.vector_group(dve, g, False, False)
                self.vector_group(dve, NG - 1, False, True)
                self.take_o(dve, NG - 1, GQ - 1)
                self.add(dve, NG - 1)
                dve.wait_ge(s1["added"].sem, s1["added"].at(NT, NG - 1))
                self.tail.vector(dve, st)

            def copy_pT(self, act, g, h, i):
                act.wait_ge(s1["pT_psum"].sem, s1["pT_psum"].at(4 * h + i + 1, g))
                n = (NT - i) * P
                act.copy(PRT[:, h % 2, 0:NT - i, n - P:n],
                         PS[:, 4 + i % 2, 0:n].rearrange("p (j q) -> p j q", q=P))\
                   .then_inc(s1["pT"].sem, 1)

            def high(self, act, g, which, first=False):
                if which == "a":
                    act.wait_ge(s1["a_loaded"].sem, s1["a_loaded"].at(16, g))
                    if not first:
                        act.wait_ge(s1["q_psum"].sem, s1["q_psum"].at(-3, g))
                    act.copy(A1H[:, :, :], A1[:, :, 0:256]).then_inc(s1["a_hi"].sem, 1)
                elif which == "b":
                    act.wait_ge(s1["b_loaded"].sem, s1["b_loaded"].at(16, g))
                    if not first:
                        act.wait_ge(s1["q_psum"].sem, s1["q_psum"].at(0, g))
                    act.copy(B1H[:, :, :], B1).then_inc(s1["b_hi"].sem, 1)
                else:
                    act.wait_ge(s1["wo_loaded"].sem, s1["wo_loaded"].at(16, g))
                    if not first:
                        act.wait_ge(s1["y"].sem, s1["y"].at(0, g))
                    act.copy(Wo1H[:, :, :], Wo1).then_inc(s1["wo_hi"].sem, 1)

            def scalar_group(self, act, g, first, last):
                for h in range(GQ):
                    for i in range(NT):
                        n, at = (NT - i) * P, OFF[NT - 1 - i]
                        if i == 0 and (h >= 2 or not first):
                            act.wait_ge(s1["pT_psum"].sem, s1["pT_psum"].at(4 * (h - 1), g))
                        act.wait_ge(s1["negmax"].sem, s1["negmax"].at(4 * h + i + 1, g))
                        act.activation(PR[:, h % 2, at:at + n], PS[:, 2 + i % 2, 0:n],
                                       ACT.Exp, bias=NX[:, h % 2, i:i + 1],
                                       accum_out=SM[:, h % 2, i:i + 1]).then_inc(s1["exp"].sem, 1)
                        if h >= 1:
                            self.copy_pT(act, g, h - 1, i)
                        elif not first:
                            self.copy_pT(act, g - 1, GQ - 1, i)
                    if h == 1 and not last:
                        self.high(act, g + 1, "a")
                    if h == 2:
                        self.high(act, g, "wo", first)
                    if h == 3 and not last:
                        self.high(act, g + 1, "b")

            def scalar(self, act):
                self.high(act, 0, "a", True)
                self.high(act, 0, "b", True)
                self.scalar_group(act, 0, True, False)
                with act.Fori(1, NG - 1) as g:
                    self.scalar_group(act, g, False, False)
                self.scalar_group(act, NG - 1, False, True)
                for i in range(NT):
                    self.copy_pT(act, NG - 1, GQ - 1, i)
                self.tail.scalar(act)

            def sum_k(self, pool, g, first):
                pool.wait_ge(s1["k_read"].sem, s1["k_read"].at(1, g))
                if not first:
                    pool.wait_ge(s1["scores"].sem, s1["scores"].at(0, g))
                pool.tensor_tensor(kT[:, :], RA[:, 0, :], RB[:, 0, :], ALU.add).then_inc(s1["k_rope"].sem, 1)

            def sum_q(self, pool, g, h, first):
                pool.wait_ge(s1["q_read"].sem, s1["q_read"].at(h + 1, g))
                if h >= 2 or not first:
                    pool.wait_ge(s1["scores"].sem, s1["scores"].at(4 * (h - 1), g))
                s = 1 - h % 2
                pool.tensor_tensor(qT[:, h % 2, :], RA[:, s, :], RB[:, s, :], ALU.add)\
                    .then_inc(s1["q_rope"].sem, 1)

            def low(self, pool, g, which):
                if which == "a":
                    pool.wait_ge(s1["a_hi"].sem, s1["a_hi"].at(1, g))
                    pool.tensor_tensor(A1L[:, :, :], A1[:, :, 0:256], A1H[:, :, :].bitcast(F32), ALU.subtract)\
                        .then_inc(s1["a_lo"].sem, 1)
                elif which == "b":
                    pool.wait_ge(s1["b_hi"].sem, s1["b_hi"].at(1, g))
                    pool.tensor_tensor(B1L[:, :, :], B1, B1H[:, :, :].bitcast(F32), ALU.subtract).then_inc(s1["b_lo"].sem, 1)
                else:
                    pool.wait_ge(s1["wo_hi"].sem, s1["wo_hi"].at(1, g))
                    pool.tensor_tensor(Wo1L[:, :, :], Wo1, Wo1H[:, :, :].bitcast(F32), ALU.subtract)\
                        .then_inc(s1["wo_lo"].sem, 1)

            def gpsimd_group(self, pool, g, first, last):
                for h in range(GQ):
                    for i in range(NT):
                        pool.wait_ge(s1["recip"].sem, s1["recip"].at(4 * h + i + 1, g))
                        pr = PR[:, h % 2, OFF[NT - 1 - i]:OFF[NT - 1 - i] + (NT - i) * P]
                        alone(pool)
                        pool.tensor_scalar(pr, pr, RCP[:, h % 2, i:i + 1], 1.0, ALU.mult, ALU.mult)\
                            .then_inc(s1["norm"].sem, 1)
                    if h < GQ - 1:
                        self.sum_q(pool, g, h + 1, first)
                    elif not last:
                        self.low(pool, g + 1, "b")
                        self.sum_k(pool, g + 1, False)
                        self.sum_q(pool, g + 1, 0, False)
                    if h == 1 and not last:
                        self.low(pool, g + 1, "a")
                    if h == 2:
                        self.low(pool, g, "wo")

            def gpsimd(self, pool):
                self.low(pool, 0, "a")
                self.sum_k(pool, 0, True)
                self.sum_q(pool, 0, 0, True)
                self.low(pool, 0, "b")
                self.gpsimd_group(pool, 0, True, False)
                with pool.Fori(1, NG - 1) as g:
                    self.gpsimd_group(pool, g, False, False)
                self.gpsimd_group(pool, NG - 1, False, True)
                self.tail.gpsimd(pool)

            def sync(self, sp):
                sp.dma_start(TAB[:, :, :], d["c_rope1"]).then_inc(s1_tab.sem, 16)
                sp.dma_start(WB[:, 0:1536], d["w1a"][0]).then_inc(s1["a_loaded"].sem, 16)
                sp.dma_start(WB[:, 1536:3072], d["w1b"][0]).then_inc(s1["b_loaded"].sem, 16)
                sp.dma_start(WB[:, 3072:5120], d["w1o"][0]).then_inc(s1["wo_loaded"].sem, 16)
                self.load_a(sp, 1)
                self.load_b(sp, 1)
                with sp.Fori(1, NG - 1) as g:
                    self.load_o(sp, g)
                    self.load_a(sp, g + 1)
                    self.load_b(sp, g + 1)
                self.load_o(sp, NG - 1)

            def load_a(self, sp, g):
                sp.wait_ge(s1["v_psum"].sem, s1["v_psum"].at(0, g))
                alone(sp)
                sp.dma_start(WB[:, 0:1536], d["w1a"][g]).then_inc(s1["a_loaded"].sem, 16)

            def load_b(self, sp, g):
                sp.wait_ge(s1["b_lo"].sem, s1["b_lo"].at(0, g))
                alone(sp)
                sp.dma_start(WB[:, 1536:3072], d["w1b"][g]).then_inc(s1["b_loaded"].sem, 16)

            def load_o(self, sp, g):
                sp.wait_ge(s1["wo_lo"].sem, s1["wo_lo"].at(0, g))
                alone(sp)
                sp.dma_start(WB[:, 3072:5120], d["w1o"][g]).then_inc(s1["wo_loaded"].sem, 16)

        F1 = ExitStack()
        RING = 4
        H1 = sb("H1", [P, 2, T], F32, F1)
        HH = sb("HH", [P, 2, T], F32R, F1)
        HL = sb("HL", [P, 2, T], F32R, F1)
        SG = sb("SG", [P, 2, T], F32, F1)
        AD = sb("AD", [P, D], F32, F1)
        AGU = sb("AGU", [P, 2, M1], F32, F1)
        XH2 = sb("XH2", [P, NC, T], F32R, F1)
        XL2 = sb("XL2", [P, NC, T], F32R, F1)
        WH = sb("WH", [P, RING, 1536], F32R, F1)
        WL = sb("WL", [P, RING, 1536], F32R, F1)
        F1.close()
        f1 = {k: sig("f1_" + k, 0, n) for k, n in dict(
            scales_loaded=32, w0=16 * 3, w1=16 * 3, w2=16 * 3, w3=16 * 2, x_hi=NC, x_lo=NC, w_hi=M1,
            w_lo=M1, gu_psum=M1, silu=M1, h=M1, h_hi=M1, h_lo=M1, down=M1).items()}
        f1w = [WC[:, s * 1536:(s + 1) * 1536] for s in range(RING - 1)] + [WB[:, 0:1536]]

        def gated(pe, m, gate, up):
            for b, pairs in ((m % 2, gate), (2 + m % 2, up)):
                for i, (w, x) in enumerate(pairs):
                    ins = pe.matmul(PS[:, b, :], w, x, start=(i == 0), stop=(i == len(pairs) - 1))
            return ins

        class Ffn1(Stage):
            def __init__(self, loop):
                self.tail = Tail(loop, y_done=(f1["down"], M1), mul=AD[:, :])

            def tensor(self, pe):
                for m in range(M1 + 1):
                    if m < M1:
                        high, low = WH[:, m % RING, :], WL[:, m % RING, :]
                        if m >= 2:
                            pe.wait_ge(f1["h"].sem, f1["h"].at(m - 1))
                        pe.wait_ge(f1["w_hi"].sem, f1["w_hi"].at(m + 1))
                        for kind, (w, x) in enumerate(((high, XH2), (high, XL2), (low, XH2))):
                            if kind == 2:
                                pe.wait_ge(f1["w_lo"].sem, f1["w_lo"].at(m + 1))
                            for b, a in ((m % 2, 0), (2 + m % 2, 512)):
                                for c in range(NC):
                                    if not m and kind == 0 and not a:
                                        pe.wait_ge(f1["x_hi"].sem, f1["x_hi"].at(c + 1))
                                    if not m and kind == 1 and not a:
                                        pe.wait_ge(f1["x_lo"].sem, f1["x_lo"].at(c + 1))
                                    ins = pe.matmul(PS[:, b, :], w[:, a + c * P:a + (c + 1) * P], x[:, c, :],
                                                    start=(kind == 0 and c == 0),
                                                    stop=(kind == 2 and c == NC - 1))
                        ins.then_inc(f1["gu_psum"].sem, 1)
                    if m >= 1:
                        k = m - 1
                        high, low = WH[:, k % RING, 1024:1536], WL[:, k % RING, 1024:1536]
                        pe.wait_ge(f1["h_lo"].sem, f1["h_lo"].at(k + 1))
                        for t in range(NT):
                            rows = slice(t * P, (t + 1) * P)
                            for i, (h, w) in enumerate(((HH, high), (HL, high), (HH, low))):
                                x = pe.matmul(PS[:, 4 + t, :], h[:, k % 2, rows], w,
                                              start=(k == 0 and i == 0), stop=(k == M1 - 1 and i == 2))
                        x.then_inc(f1["down"].sem, 1)
                self.tail.tensor(pe)

            def high(self, act, m):
                act.wait_ge(f1[f"w{m % RING}"].sem, f1[f"w{m % RING}"].at(16 * (m // RING + 1)))
                if m >= RING:
                    act.wait_ge(f1["down"].sem, f1["down"].at(m - RING + 1))
                act.copy(WH[:, m % RING, :], f1w[m % RING]).then_inc(f1["w_hi"].sem, 1)

            def scalar(self, act):
                self.high(act, 0)
                self.high(act, 1)
                act.wait_ge(f1["scales_loaded"].sem, f1["scales_loaded"].at(32))
                for m in range(M1):
                    act.wait_ge(f1["gu_psum"].sem, f1["gu_psum"].at(m + 1))
                    if m >= 2:
                        act.wait_ge(f1["h"].sem, f1["h"].at(m - 1))
                    act.activation(SG[:, m % 2, :], PS[:, m % 2, :], ACT.Silu, scale=AGU[:, 0, m:m + 1])\
                       .then_inc(f1["silu"].sem, 1)
                    act.wait_ge(f1["h"].sem, f1["h"].at(m + 1))
                    if m >= 2:
                        act.wait_ge(f1["down"].sem, f1["down"].at(m - 1))
                    act.copy(HH[:, m % 2, :], H1[:, m % 2, :]).then_inc(f1["h_hi"].sem, 1)
                    if m + 2 < M1:
                        self.high(act, m + 2)
                self.tail.scalar(act)

            def vector(self, dve, st):
                for c in range(NC):
                    dve.tensor_copy(XH2[:, c, :], XT[:, c, :]).then_inc(f1["x_hi"].sem, 1)
                for c in range(NC):
                    dve.wait_ge(f1["x_hi"].sem, f1["x_hi"].at(c + 1))
                    dve.tensor_tensor(XL2[:, c, :], XT[:, c, :], XH2[:, c, :].bitcast(F32), ALU.subtract)\
                       .then_inc(f1["x_lo"].sem, 1)
                dve.wait_ge(f1["scales_loaded"].sem, f1["scales_loaded"].at(32))
                for m in range(M1):
                    dve.wait_ge(f1["silu"].sem, f1["silu"].at(m + 1))
                    dve.scalar_tensor_tensor(H1[:, m % 2, :], PS[:, 2 + m % 2, :], AGU[:, 1, m:m + 1],
                                             SG[:, m % 2, :], ALU.mult, ALU.mult).then_inc(f1["h"].sem, 1)
                    dve.wait_ge(f1["h_hi"].sem, f1["h_hi"].at(m + 1))
                    dve.tensor_tensor(HL[:, m % 2, :], H1[:, m % 2, :], HH[:, m % 2, :].bitcast(F32),
                                      ALU.subtract).then_inc(f1["h_lo"].sem, 1)
                self.tail.vector(dve, st)

            def gpsimd(self, pool):
                for m in range(M1):
                    pool.wait_ge(f1["w_hi"].sem, f1["w_hi"].at(m + 1))
                    w = f1w[m % RING]
                    pool.tensor_tensor(WL[:, m % RING, :], w, WH[:, m % RING, :].bitcast(F32), ALU.subtract)\
                        .then_inc(f1["w_lo"].sem, 1)
                self.tail.gpsimd(pool)

            def load(self, sp, m):
                sp.dma_start(f1w[m % RING], d["f1_w"][m]).then_inc(f1[f"w{m % RING}"].sem, 16)

            def sync(self, sp):
                sp.dma_start(AGU[:, :, :], d["f1_agu"]).then_inc(f1["scales_loaded"].sem, 16)
                sp.dma_start(AD[:, :], d["f1_ad"].partition_broadcast(P)).then_inc(f1["scales_loaded"].sem, 16)
                for m in range(RING - 1, M1):
                    if m >= RING:
                        sp.wait_ge(f1["w_lo"].sem, f1["w_lo"].at(m - RING + 1))
                    self.load(sp, m)
                    if m in (4, 5, 6, 7):
                        at = slice((m - 4) * 2048, (m - 3) * 2048)
                        sp.dma_start(WA[:, at], d["w2"][:, at]).then_inc(S_wa.sem, 16)

        F2 = ExitStack()
        LO = sb("LO", [P, NT, P], F32, F2)
        LG = sb("LG", [P, NT, 8], F32, F2)
        M82 = sb("M82", [P, NT, 8], F32, F2)
        I8 = sb("I8", [P, NT, 8], U32, F2)
        IF = sb("IF", [P, NT, 2], F32, F2)
        WF = sb("WF", [P, 2, NT, 8], F32, F2)
        GW = sb("GW", [P, 4, NT], F32, F2)
        LT = sb("LT", [P, T], F32, F2)
        F2.close()
        f2 = {k: sig("f2_" + k, 0, n) for k, n in dict(
            low_psum=1, diff=1, exp=1, low_ready=1, lT_psum=1, lT_ready=1).items()}
        f2_base = WC[:, 0:2048].rearrange("p (c n) -> p c n", c=NC)
        f2_ga = WC[:, 2048:2592].rearrange("p (c n) -> p c n", c=NC)
        f2_B = WC[:, 2592:3104]
        f2_b = WC[:, 3104:3616]

        class Ffn2(Stage):
            def __init__(self, loop):
                self.tail = Tail(loop, self.y_tile, add=f2_b)

            def y_tile(self, pe, t, ps):
                for c in range(NC):
                    pe.matmul(ps, XT[:, c, t * P:(t + 1) * P], f2_base[:, c, :], start=(c == 0), stop=False)
                return pe.matmul(ps, LT[:, t * P:(t + 1) * P], f2_B, start=False, stop=True)

            def low(self, t):
                return PS[:, 4 + t // 2, 256 * (t % 2):256 * (t % 2) + 136]

            def tensor(self, pe):
                pe.wait_ge(S_wc.sem, S_wc.at(W_C[1]))
                for t in range(NT):
                    for c in range(NC):
                        x = pe.matmul(self.low(t), XT[:, c, t * P:(t + 1) * P], f2_ga[:, c, :],
                                      start=(c == 0), stop=(c == NC - 1))
                x.then_inc(f2["low_psum"].sem, 1)
                pe.wait_ge(f2["low_ready"].sem, f2["low_ready"].at(1))
                for t in range(NT):
                    x = pe.transpose(PS[:, 6, t * P:(t + 1) * P], LO[:, t, :], ident[:, :])
                x.then_inc(f2["lT_psum"].sem, 1)
                pe.wait_ge(f2["lT_ready"].sem, f2["lT_ready"].at(1))
                self.tail.tensor(pe)

            def scalar(self, act):
                act.wait_ge(f2["diff"].sem, f2["diff"].at(1))
                act.activation(GW[:, 1, :], GW[:, 0, :], ACT.Exp).then_inc(f2["exp"].sem, 1)
                act.wait_ge(f2["lT_psum"].sem, f2["lT_psum"].at(1))
                act.copy(LT[:, :], PS[:, 6, :]).then_inc(f2["lT_ready"].sem, 1)
                self.tail.scalar(act)

            def gpsimd(self, pool):
                self.tail.gpsimd(pool)

            def vector(self, dve, st):
                dve.wait_ge(S_wc.sem, S_wc.at(W_C[1]))
                dve.wait_ge(f2["low_psum"].sem, f2["low_psum"].at(1))
                for t in range(NT):
                    st.done(dve.tensor_copy(LG[:, t, :], self.low(t)[:, P:P + 8]))
                st.wait()
                alone(dve)
                alone(dve)
                for t in range(NT):
                    st.done(dve.max(M82[:, t, :], LG[:, t, :]))
                st.wait()
                alone(dve)
                for t in range(NT):
                    st.done(dve.max_index(I8[:, t, :], M82[:, t, :], LG[:, t, :]))
                dve.tensor_tensor(GW[:, 0, :], M82[:, :, 1], M82[:, :, 0], ALU.subtract)\
                   .then_inc(f2["diff"].sem, 1)
                st.wait()
                st.done(dve.tensor_copy(IF[:, :, :], I8[:, :, 0:2]))
                dve.wait_ge(f2["exp"].sem, f2["exp"].at(1))
                st.link(dve.tensor_scalar(GW[:, 2, :], GW[:, 1, :], 1.0, None, ALU.add))
                st.link(dve.reciprocal(GW[:, 2, :], GW[:, 2, :]))
                st.link(dve.tensor_scalar(GW[:, 2, :], GW[:, 2, :], 2.0, None, ALU.mult))
                st.link(dve.tensor_tensor(GW[:, 3, :], GW[:, 2, :], GW[:, 1, :], ALU.mult))
                bc = lambda a: a.unsqueeze(2).to_broadcast([P, NT, 8])
                for k in range(2):
                    st.link(dve.tensor_tensor(WF[:, k, :, :], iota8[:, :].unsqueeze(1).to_broadcast([P, NT, 8]),
                                              bc(IF[:, :, k]), ALU.is_equal))
                    st.link(dve.tensor_tensor(WF[:, k, :, :], WF[:, k, :, :], bc(GW[:, 2 + k, :]), ALU.mult))
                st.link(dve.tensor_tensor(WF[:, 0, :, :], WF[:, 0, :, :], WF[:, 1, :, :], ALU.add))
                for t in range(NT):
                    x = dve.tensor_tensor(LO[:, t, :].rearrange("p (e r) -> p e r", e=8),
                                          self.low(t)[:, 0:P].rearrange("p (e r) -> p e r", e=8),
                                          WF[:, 0, t, :].unsqueeze(2).to_broadcast([P, 8, 16]), ALU.mult)
                x.then_inc(f2["low_ready"].sem, 1)
                self.tail.vector(dve, st)

        F3 = ExitStack()
        XS = sb("XS", [P, T], F32, F3)
        LR = 96
        Z = sb("Z", [LR, T], F32R, F3)
        BP = sb("BP", [LR, 2 * M3 * P], F32R, F3)
        Z2 = sb("Z2", [2, T], F32, F3)
        H3 = sb("H3", [P, M3, T], F32, F3)
        HS = sb("HS", [P, 3, T], F32, F3)
        SG3 = sb("SG3", [P, 2, T], F32, F3)
        B2 = sb("B2", [2, D], F32, F3)
        F3.close()
        f3 = {k: sig("f3_" + k, 0, n) for k, n in dict(
            b2_loaded=16, xs=1, z_psum=1, z_hi=1, z=1, b_hi=2, b1_lo=1, b3_lo=1, gu_psum=M3, silu=M3, h=M3, z2_psum=1, z2=1, hs=3).items()}
        w3 = WA[:, :]
        f3_w1, f3_w3 = w3[:, 0:1536], w3[:, 1536:3072]
        f3_w2 = w3[:, 3072:4608].rearrange("p (k n) -> p k n", k=3)
        f3_b = w3[0:LR, 4608:7680]
        f3_a13 = w3[:, 7680:8064].rearrange("p (c n) -> p c n", c=NC)
        f3_a2 = w3[:, 8064:8088].rearrange("p (m n) -> p m n", m=M3)

        class Ffn3(Stage):
            def __init__(self, loop):
                self.tail = Tail(loop, self.y_tile, last=True)

            def y_tile(self, pe, t, ps):
                for k in range(3):
                    pe.matmul(ps, HS[:, k, t * P:(t + 1) * P], f3_w2[:, k, :], start=(k == 0), stop=False)
                return pe.matmul(ps, Z2[:, t * P:(t + 1) * P], B2[:, :], start=False, stop=True)

            def tensor(self, pe):
                pe.wait_ge(S_wa.sem, S_wa.at(W_A[1]))
                for c in range(NC):
                    x = pe.matmul(PS[0:LR, 7, :], f3_a13[:, c, :], XT[:, c, :], start=(c == 0), stop=(c == NC - 1))
                x.then_inc(f3["z_psum"].sem, 1)
                pe.wait_ge(f3["xs"].sem, f3["xs"].at(1))
                pe.wait_ge(f3["z"].sem, f3["z"].at(1))
                pe.wait_ge(f3["b1_lo"].sem, f3["b1_lo"].at(1))
                pe.wait_ge(f3["b3_lo"].sem, f3["b3_lo"].at(1))
                for m in range(M3):
                    if m >= 2:
                        pe.wait_ge(f3["h"].sem, f3["h"].at(m - 1))
                    cols = slice(m * P, (m + 1) * P)
                    gated(pe, m, [(f3_w1[:, cols], XS[:, :]), (BP[:, cols], Z[:, :])],
                          [(f3_w3[:, cols], XS[:, :]),
                           (BP[:, M3 * P + m * P:M3 * P + (m + 1) * P], Z[:, :])])\
                        .then_inc(f3["gu_psum"].sem, 1)
                for m in range(M3):
                    pe.wait_ge(f3["h"].sem, f3["h"].at(m + 1))
                    x = pe.matmul(PS[0:2, 6, :], f3_a2[:, m, :], H3[:, m, :], start=(m == 0), stop=(m == M3 - 1))
                x.then_inc(f3["z2_psum"].sem, 1)
                pe.wait_ge(f3["b2_loaded"].sem, f3["b2_loaded"].at(16))
                pe.wait_ge(f3["z2"].sem, f3["z2"].at(1))
                pe.wait_ge(f3["hs"].sem, f3["hs"].at(3))
                self.tail.tensor(pe)

            def scalar(self, act):
                act.wait_ge(S_wa.sem, S_wa.at(W_A[1]))
                for k in range(2):
                    act.copy(BP[:, k * M3 * P:(k + 1) * M3 * P], f3_b[:, k * M3 * P:(k + 1) * M3 * P])\
                       .then_inc(f3["b_hi"].sem, 1)
                for m in range(M3):
                    act.wait_ge(f3["gu_psum"].sem, f3["gu_psum"].at(m + 1))
                    if m >= 2:
                        act.wait_ge(f3["h"].sem, f3["h"].at(m - 1))
                    act.activation(SG3[:, m % 2, :], PS[:, m % 2, :], ACT.Silu).then_inc(f3["silu"].sem, 1)
                act.wait_ge(f3["z2_psum"].sem, f3["z2_psum"].at(1))
                act.mul(Z2[:, :], PS[0:2, 6, :], 0.5).then_inc(f3["z2"].sem, 1)

            def vector(self, dve, st):
                low = slice(64, 96)
                dve.wait_ge(f3["b_hi"].sem, f3["b_hi"].at(1))
                dve.tensor_tensor(BP[low, 0:M3 * P], f3_b[low, 0:M3 * P],
                                  BP[low, 0:M3 * P].bitcast(F32), ALU.subtract).then_inc(f3["b1_lo"].sem, 1)
                st.done(dve.tensor_tensor(XS[:, :], XT[:, 0, :], XT[:, 1, :], ALU.add))
                st.link(dve.tensor_tensor(SG3[:, 0, :], XT[:, 2, :], XT[:, 3, :], ALU.add))
                dve.tensor_tensor(XS[:, :], XS[:, :], SG3[:, 0, :], ALU.add).then_inc(f3["xs"].sem, 1)
                dve.wait_ge(f3["z_psum"].sem, f3["z_psum"].at(1))
                dve.tensor_scalar(Z[:, :], PS[0:LR, 7, :], 0.5, None, ALU.mult).then_inc(f3["z_hi"].sem, 1)
                dve.wait_ge(f3["z_hi"].sem, f3["z_hi"].at(1))
                low = slice(32, 64)
                dve.scalar_tensor_tensor(Z[low, :], PS[low, 7, :], 0.5, Z[low, :].bitcast(F32),
                                         ALU.mult, ALU.subtract).then_inc(f3["z"].sem, 1)
                for m in range(M3):
                    dve.wait_ge(f3["silu"].sem, f3["silu"].at(m + 1))
                    dve.tensor_tensor(H3[:, m, :], PS[:, 2 + m % 2, :], SG3[:, m % 2, :], ALU.mult)\
                       .then_inc(f3["h"].sem, 1)
                dve.wait_ge(f3["h"].sem, f3["h"].at(M3))
                for k in range(3):
                    st.link(dve.tensor_tensor(HS[:, k, :], H3[:, k, :], H3[:, 3 + k, :], ALU.add))
                    st.link(dve.tensor_tensor(HS[:, k, :], HS[:, k, :], H3[:, 6 + k, :], ALU.add))
                    dve.tensor_tensor(HS[:, k, :], HS[:, k, :], H3[:, 9 + k, :], ALU.add)\
                       .then_inc(f3["hs"].sem, 1)
                self.tail.vector(dve, st)

            def gpsimd(self, pool):
                low, up = slice(64, 96), slice(M3 * P, 2 * M3 * P)
                pool.wait_ge(f3["b_hi"].sem, f3["b_hi"].at(2))
                pool.tensor_tensor(BP[low, up], f3_b[low, up], BP[low, up].bitcast(F32), ALU.subtract)\
                    .then_inc(f3["b3_lo"].sem, 1)
                self.tail.gpsimd(pool)

        s_lv = sig("logvar_arg_ready", 1, 0)
        s_lvd = sig("logvar_ready", 2, 0)

        class LogVar(Stage):
            def vector(self, dve, st):
                for t in range(NT):
                    st.link(dve.bn_stats(stat[:, t % 2, :], XB[:, t, :]))
                    alone(dve)
                    st.link(dve.bn_aggr(mv[:, t % 2, :], stat[:, t % 2, :]))
                    x = dve.tensor_copy(VV[:, t:t + 1], mv[:, t % 2, 1:2])
                    st.link(x) if t < NT - 1 else x.then_inc(s_lv.sem, 1)

            def scalar(self, act):
                act.wait_ge(s_lv.sem, s_lv.at(1))
                lv = LV[:, :].rearrange("p (k b t) -> p k b t", k=2, b=NB)
                for k in range(2):
                    act.activation(lv[:, k, Signal.batch, :], VV[:, :], ACT.Ln, bias=1.0)\
                       .then_inc(s_lvd.sem, 1)
                act.wait_ge(s_lvd.sem, s_lvd.at(2))

        s_in = sig("xin_T_psum", 0, NT)
        s_ind = sig("xin_T", 0, NT)

        class Enter(Stage):
            def __init__(self, loop):
                self.loop = loop

            def tensor(self, pe):
                pe.wait_ge(S_x.sem, S_x.at(16))
                for t in range(NT):
                    if t >= 2:
                        pe.wait_ge(s_ind.sem, s_ind.at(t - 1))
                    for c in range(NC):
                        x = pe.transpose(PS[:, t % 2, c * P:(c + 1) * P], XB[:, t, c * P:(c + 1) * P], ident[:, :])
                    x.then_inc(s_in.sem, 1)

            def scalar(self, act):
                for t in range(NT):
                    act.wait_ge(s_in.sem, s_in.at(t + 1))
                    act.copy(XT[:, :, t * P:(t + 1) * P], PS[:, t % 2, :].rearrange("p (c q) -> p c q", c=NC))\
                       .then_inc(s_ind.sem, 1)

        consts += [(iota8[:, :], d["c_iota8"]), (cos0[:, :, :], d["c_cos0"]), (sin0[:, :, :], d["c_sin0"])]
        W0 = WA[:, 0:3072].rearrange("p (c u n) -> p c u n", c=NC, u=UNITS)
        Wo0 = WA[:, 3072:5120].rearrange("p (c n) -> p c n", c=NC)
        b0 = WA[:, 5120:5888].rearrange("p (u n) -> p u n", u=UNITS)
        bo0 = WA[:, 5888:6400]
        W2 = WA[:, 0:6144].rearrange("p (c u n) -> p c u n", c=NC, u=UNITS)
        Wo2 = WA[:, 6144:8192].rearrange("p (c n) -> p c n", c=NC)
        b2 = WC[:, 3616:5152].rearrange("p (u n) -> p u n", u=UNITS)
        bo2 = WC[:, 5152:5664]
        W3 = WB[:, 0:3072].rearrange("p (c u n) -> p c u n", c=NC, u=UNITS)
        Wo3 = WB[:, 3072:5120].rearrange("p (c n) -> p c n", c=NC)
        W_A, W_B, W_C = [64, 80], [16], [16, 64]
        S_w0, S_w0o = sig("w0_loaded"), sig("w0o_loaded")
        S_wa.per[1], S_wb.per[1], S_wc.per[1] = 80, 16, 64

        def load0(eng):
            eng.wait_ge(S_w0.sem, 16)
            eng.wait_ge(S_xT.sem, S_xT.at(16))

        def bias0(eng):
            eng.wait_ge(S_w0o.sem, 16 * 3)

        def load2(eng):
            eng.wait_ge(S_wa.sem, S_wa.at(W_A[0]))

        def bias2(eng):
            eng.wait_ge(S_wc.sem, S_wc.at(48))

        def load3(eng):
            eng.wait_ge(S_wb.sem, S_wb.at(16))

        S_x.per = [16, 16]
        S_store.per = [16, 16]
        passes = [
            [Attention16(0, W0, Wo0, 8, 1.0 / 16, load0, b0, (cos0, sin0), bo0, last=True,
                         bias_loaded=bias0), LogVar()],
            [Enter(1), Ffn0(1), Attention1(1), Ffn1(1),
             Attention16(1, W2, Wo2, 32, 0.25, load2, b2, None, bo2, bias_loaded=bias2), Ffn2(1),
             Attention16(1, W3, Wo3, 8, 0.25, load3), Ffn3(1)]]
        S_bar.per = [4 * len(p) for p in passes]

        block = ctx.enter_context(nc.Block())
        steps = {"vector": []}

        @block.tensor
        def _(pe):
            pe.wait_ge(start.sem, START)
            pe.wait_ge(S_const.sem, 16 * len(consts))
            for loop in range(2):
                Signal.loop = loop
                with pe.Fori(0, NB) as b:
                    Signal.batch = b
                    for k, stage in enumerate(passes[loop]):
                        stage.tensor(pe)
                        alone(pe)
                        pe.drain().then_inc(S_bar.sem, 1)
                        pe.wait_ge(S_bar.sem, S_bar.at(4 * (k + 1)))
                        alone(pe)

        @block.scalar
        def _(act):
            act.wait_ge(start.sem, START)
            for loop in range(2):
                Signal.loop = loop
                with act.Fori(0, NB) as b:
                    Signal.batch = b
                    for k, stage in enumerate(passes[loop]):
                        stage.scalar(act)
                        alone(act)
                        act.drain().then_inc(S_bar.sem, 1)
                        act.wait_ge(S_bar.sem, S_bar.at(4 * (k + 1)))
                        alone(act)

        @block.vector
        def _(dve):
            dve.memset(ones[:, :], 1.0).then_inc(start.sem, 1)
            dve.memset(halfneg[:, :], -0.5).then_inc(start.sem, 1)
            dve.wait_ge(S_const.sem, 16 * len(consts))
            dve.tensor_copy(ident_masks_b[:], ident_masks[:]).then_inc(start.sem, 1)
            dve.wait_ge(start.sem, START)
            st = Steps(dve, S_step)
            for loop in range(2):
                Signal.loop = loop
                st.n = 0
                with dve.Fori(0, NB) as b:
                    Signal.batch = b
                    for k, stage in enumerate(passes[loop]):
                        stage.vector(dve, st)
                        alone(dve)
                        dve.drain().then_inc(S_bar.sem, 1)
                        dve.wait_ge(S_bar.sem, S_bar.at(4 * (k + 1)))
                        alone(dve)
                steps["vector"].append(st.n)

        @block.gpsimd
        def _(pool):
            pool.wait_ge(start.sem, START)
            for loop in range(2):
                Signal.loop = loop
                with pool.Fori(0, NB) as b:
                    Signal.batch = b
                    for k, stage in enumerate(passes[loop]):
                        stage.gpsimd(pool)
                        alone(pool)
                        pool.drain().then_inc(S_bar.sem, 1)
                        pool.wait_ge(S_bar.sem, S_bar.at(4 * (k + 1)))
                        alone(pool)

        @block.sync
        def _(sp):
            sp.dma_start(XT[:, :, :], d["xT"][0]).then_inc(S_xT.sem, 16)
            sp.dma_start(WA[:, 0:3072], d["w0qkv"]).then_inc(S_w0.sem, 16)
            for buf, src in consts:
                sp.dma_start(buf, src).then_inc(S_const.sem, 16)
            sp.dma_start(WA[:, 5120:5888], d["b0qkv"].partition_broadcast(P)).then_inc(S_w0o.sem, 16)
            sp.dma_start(WA[:, 5888:6400], d["b0o"].partition_broadcast(P)).then_inc(S_w0o.sem, 16)
            sp.dma_start(WA[:, 3072:5120], d["w0o"]).then_inc(S_w0o.sem, 16)
            Signal.loop = 0
            made = passes[0][0].on["v_psum"]
            for n in range(NB):
                Signal.batch = n
                sp.dma_start(XB[:, :, :], d["x"][n]).then_inc(S_x.sem, 16)
                if n + 1 < NB:
                    sp.wait_ge(made.sem, made.at(UNITS * NT))
                    sp.dma_start(XT[:, :, :], d["xT"][n + 1]).then_inc(S_xT.sem, 16)
                sp.wait_ge(S_bar.sem, S_bar.at(S_bar.per[0]))
                if n + 1 < NB:
                    sp.dma_start(xmid, XB[:, :, :]).then_inc(S_store.sem, 16)
                    sp.wait_ge(S_store.sem, 16)
            Signal.loop = 1
            sp.sem_inc(S_x.sem, 16)
            for n in range(NB):
                Signal.batch = n
                if n:
                    sp.dma_start(XB[:, :, :], xmid).then_inc(S_x.sem, 16)
                sp.dma_start(WC[:, 0:2293], d["f0_w"]).then_inc(S_wc.sem, 16)
                passes[1][2].sync(sp)
                for m in range(RING - 1):
                    passes[1][3].load(sp, m)
                sp.wait_ge(S_bar.sem, S_bar.at(4 * 3))
                passes[1][3].sync(sp)
                sp.wait_ge(S_bar.sem, S_bar.at(4 * 4))
                sp.dma_start(WC[:, 3616:5152], d["b2qkv"].partition_broadcast(P)).then_inc(S_wc.sem, 16)
                sp.dma_start(WC[:, 5152:5664], d["b2o"].partition_broadcast(P)).then_inc(S_wc.sem, 16)
                sp.wait_ge(S_wc.sem, S_wc.at(48))
                sp.dma_start(WC[:, 0:3616], d["f2_w"]).then_inc(S_wc.sem, 16)
                sp.dma_start(WB[:, :], d["w3"]).then_inc(S_wb.sem, 16)
                sp.wait_ge(S_bar.sem, S_bar.at(4 * 5))
                sp.dma_start(WA[:, 0:8088], d["f3_w"]).then_inc(S_wa.sem, 16)
                sp.wait_ge(S_bar.sem, S_bar.at(4 * 7))
                sp.dma_start(B2[:, :], d["f3_b2"]).then_inc(f3["b2_loaded"].sem, 16)
                sp.wait_ge(S_bar.sem, S_bar.at(4 * 8))
                sp.dma_start(out[NB - 1 - n], XB[:, :, :]).then_inc(S_store.sem, 16)
                sp.wait_ge(S_store.sem, 16 * (n + 2))

    assert all(tuple(steps[k]) == STEPS[k] for k in STEPS), steps
    return steps


def chunked(w):
    k = w.shape[0] // P
    return np.ascontiguousarray(w.reshape(k, P, -1).transpose(1, 0, 2))


def heads(w, n, width):
    return w.reshape(n, width, *w.shape[1:])


def tables():
    f = np.float32
    c = {}
    eye = np.eye(P, dtype=f)
    q, k = np.arange(P)[:, None], np.arange(P)[None, :]
    m = np.where(k > q, f(MASKED), f(0))
    c["c_ident_masks"] = np.stack([eye, m, m.T], 1)
    c["c_iota8"] = np.tile(np.arange(8, dtype=f), (P, 1))
    pos = np.arange(T, dtype=f)
    inv = (1.0 / 1000000.0 ** (np.arange(0, HD, 2, dtype=f) / f(HD))).astype(f)
    fr = np.outer(pos, inv).astype(f)
    cos, sin = np.cos(fr), np.sin(fr)
    tile = lambda a: np.ascontiguousarray(a.reshape(NT, P, HD).transpose(1, 0, 2)).astype(f)
    c["c_cos0"] = tile(np.concatenate([cos, cos], 1))
    c["c_sin0"] = tile(np.concatenate([-sin, sin], 1))
    inv = (1.0 / 500000.0 ** (np.arange(0, L1D, 2, dtype=f) / L1D)).astype(f)
    wl = 2.0 * np.pi / inv
    scaled = np.where(wl > 1024 / 1.0, inv / 8.0, inv)
    smooth = (1024 / wl - 1.0) / (4.0 - 1.0)
    smoothed = (1.0 - smooth) / 8.0 * inv + smooth * inv
    medium = (wl <= 1024 / 1.0) & (wl >= 1024 / 4.0)
    inv = np.where(medium, smoothed, scaled).astype(f)
    fr = (pos[:, None] * inv[None, :]).astype(f).T
    cos, sin = np.cos(fr).astype(np.float64), np.sin(fr).astype(np.float64)
    both = np.concatenate([cos, cos], 0)
    swap = np.concatenate([sin, -sin], 0)
    sc = 1.0 / np.sqrt(128.0)
    c["c_rope1"] = np.ascontiguousarray(np.stack([both * sc, swap * sc, both, swap], 1)).astype(f)
    return c


def layout(i):
    f = np.float32
    a = {}
    x = i["L0_attn_hidden_states"]
    a["x"] = np.ascontiguousarray(x.reshape(NB, NT, P, D).transpose(0, 2, 1, 3))
    a["xT"] = np.ascontiguousarray(x.transpose(0, 2, 1).reshape(NB, NC, P, T).transpose(0, 2, 1, 3))

    def units(q, k, v):
        h = lambda w, u: np.split(w, UNITS)[u]
        return np.concatenate([np.concatenate([h(q, u), h(k, u), h(v, u)]) for u in range(UNITS)])

    def split0(w):
        w = w.reshape(8, 6, HD, *w.shape[1:])
        r = w.shape[3:]
        return w[:, 0:4].reshape(512, *r), w[:, 4].reshape(128, *r), w[:, 5].reshape(128, *r)
    a["w0qkv"] = chunked(np.ascontiguousarray(units(*split0(i["L0_attn_w_qkv"])).T)).reshape(P, -1)
    a["b0qkv"] = units(*split0(i["L0_attn_b_qkv"]))
    a["w0o"] = chunked(i["L0_attn_w_dense"].T).reshape(P, -1)
    a["b0o"] = i["L0_attn_b_dense"]

    def col(n, w):
        r = np.zeros((P, w[0].size), f)
        r[:w.shape[0]] = w.reshape(w.shape[0], -1)
        assert r.shape[1] == n
        return r
    bc = lambda v: np.tile(v.reshape(1, -1), (P, 1))
    a["f0_w"] = np.concatenate([
        col(256, chunked(i["L0_ffn_Wq"].T)), col(512, chunked(i["L0_ffn_Wu1"].T)),
        col(128, chunked(i["L0_ffn_Wvd"].T)), col(512, chunked(i["L0_ffn_aux_values"].T)),
        col(64, i["L0_ffn_Wr"]), col(48, i["L0_ffn_Wr"].T), col(128, i["L0_ffn_aux_keys"].T),
        col(512, i["L0_ffn_Wvu"].T), bc(i["L0_ffn_log_rel"]),
        i["L0_ffn_bu1"].reshape(P, 1), i["L0_ffn_Wu2"].reshape(P, 1), bc(i["L0_ffn_bu2"]),
        bc(i["L0_ffn_gate_w1"]), bc(i["L0_ffn_gate_bias"])], 1).astype(f, copy=False)
    q = i["L1_attn_Wq"].reshape(L1KV, GQ * L1D, D)
    k = i["L1_attn_Wk"].reshape(L1KV, L1D, D)
    v = i["L1_attn_Wv"].reshape(L1KV, L1D, D)
    for name, w in (("w1a", np.concatenate([q[:, 0:L1D], k, v], 1)), ("w1b", q[:, L1D:])):
        w = w.transpose(0, 2, 1).reshape(L1KV, NC, P, 3 * L1D)
        a[name] = np.ascontiguousarray(w.transpose(0, 2, 1, 3)).reshape(L1KV, P, -1)
    w = i["L1_attn_Wo"].T.reshape(L1KV, GQ, L1D, D)
    a["w1o"] = np.ascontiguousarray(w.transpose(0, 2, 1, 3)).reshape(L1KV, P, -1)
    pad = M1 * P - 1376

    def rows(w):
        return np.concatenate([w, np.zeros((pad,) + w.shape[1:], f)])
    gu = [rows(i[n]).reshape(M1, P, NC, P).transpose(0, 3, 2, 1).reshape(M1, P, 512)
          for n in ("L1_ffn_Wg", "L1_ffn_Wu")]
    dn = rows(np.ascontiguousarray(i["L1_ffn_Wd"].T)).reshape(M1, P, D)
    a["f1_w"] = np.ascontiguousarray(np.concatenate(gu + [dn], 2))
    a["f1_agu"] = np.ascontiguousarray(np.stack([rows(i["L1_ffn_ag"]).reshape(M1, P).T,
                                                 rows(i["L1_ffn_au"]).reshape(M1, P).T], 1))
    a["f1_ad"] = i["L1_ffn_ad"]
    w = units(i["L2_attn_Wq"], i["L2_attn_Wk"], i["L2_attn_Wv"]).T
    a["w2"] = np.concatenate([chunked(w).reshape(P, -1), chunked(i["L2_attn_Wo"].T).reshape(P, -1)], 1)
    a["b2qkv"] = units(i["L2_attn_bq"], i["L2_attn_bk"], i["L2_attn_bv"])
    a["b2o"] = i["L2_attn_bo"]
    ga = np.concatenate([i["L2_ffn_lora_A"].reshape(P, D), i["L2_ffn_gate_w"]]).T
    a["f2_w"] = np.concatenate([
        chunked(i["L2_ffn_base_w"].T).reshape(P, -1), chunked(ga).reshape(P, -1),
        i["L2_ffn_lora_B"].transpose(0, 2, 1).reshape(P, D), bc(i["L2_ffn_base_b"])], 1)
    w = units(i["L3_attn_wq"].T, i["L3_attn_wk"].T, i["L3_attn_wv"].T).T
    a["w3"] = np.concatenate([chunked(w).reshape(P, -1), chunked(i["L3_attn_wo"]).reshape(P, -1)], 1)

    def inter(w, axis=0):
        w = np.moveaxis(w, axis, 0)
        n = w.shape[0] // 344
        w = w.reshape(n, 344, *w.shape[1:])
        w = np.concatenate([w, np.zeros((n, 40) + w.shape[2:], f)], 1)
        return np.moveaxis(w.reshape(n * 384, *w.shape[2:]), 0, axis)
    z = np.zeros((2, 1376), f)

    def thrice(w):
        r = np.zeros((3, 32) + w.shape[1:], f)
        r[:, 0:4] = w
        return r.reshape(96, *w.shape[1:])
    a13 = thrice(np.concatenate([i["L3_ffn_a1"], i["L3_ffn_a3"]]))
    a["f3_w"] = np.concatenate([
        np.ascontiguousarray(inter(i["L3_ffn_w1q"]).T), np.ascontiguousarray(inter(i["L3_ffn_w3q"]).T),
        chunked(inter(i["L3_ffn_w2q"].T)).reshape(P, -1),
        col(1536, thrice(inter(np.concatenate([i["L3_ffn_b1"].T, z]), 1))),
        col(1536, thrice(inter(np.concatenate([z, i["L3_ffn_b3"].T]), 1))),
        chunked(a13.T).reshape(P, -1), chunked(inter(i["L3_ffn_a2"].T)).reshape(P, -1)], 1)
    a["f3_b2"] = np.ascontiguousarray(i["L3_ffn_b2"].T)
    return {k: np.ascontiguousarray(v) for k, v in a.items()}


def kernel(**inputs):
    import concourse.bacc as bacc
    from concourse.bass_utils import run_bass_kernel_spmd
    arrays = {**layout({k: np.asarray(v) for k, v in inputs.items()}), **tables()}
    nc = bacc.Bacc("TRN2", target_bir_lowering=False, num_devices=1)
    d = {k: nc.dram_tensor(k, v.shape, mybir.dt.from_np(v.dtype), kind="ExternalInput").ap()
         for k, v in arrays.items()}
    out = nc.dram_tensor("out", (NB, P, NT, D), F32, kind="ExternalOutput").ap()
    build(nc, d, out)
    r = run_bass_kernel_spmd(nc, [arrays], core_ids=[0])
    y = r.results[0]["out"]
    return np.ascontiguousarray(y.transpose(0, 2, 1, 3)).reshape(NB, T, D)
```
